# Optimizing a Trainium2 kernel written in Bass

```python
import numpy as np
import jax
import jax.numpy as jnp

def _softmax(x, axis=-1):
    return jax.nn.softmax(x, axis=axis)

def _gelu(x):
    return jax.nn.gelu(x, approximate=True)

def _silu(x):
    return jax.nn.silu(x)

def _sigmoid(x):
    return jax.nn.sigmoid(x)

def _layernorm(x, axis=-1, eps=1e-05):
    m = jnp.mean(x, axis=axis, keepdims=True)
    v = jnp.var(x, axis=axis, keepdims=True)
    return (x - m) / jnp.sqrt(v + eps)

def _scatter_add(tgt, idx, src, axis=0):
    return tgt.at[idx].add(src)

def _segment_sum(src, seg, n):
    return jax.ops.segment_sum(src, seg, n)
kernel_name = 'mk_flamingo_gated_d4_seqx_r8_3b8399'

def setup_inputs(seed: int=0):
    np.random.seed(seed)
    _w = jnp.asarray

    def _rec_inputs():
        import jax
        import jax.numpy as jnp
        _rk = jax.random.key(seed)
        x = -0.0002928 + 1 * jax.random.normal(jax.random.fold_in(_rk, 1), (32, 128, 128), jnp.float32)
        _lenS = 128 - jax.random.randint(jax.random.fold_in(_rk, 7), (32,), 0, max(1, 128 // 4) + 1, jnp.int32)
        _lenS2 = 77 - jax.random.randint(jax.random.fold_in(_rk, 8), (32,), 0, max(1, 77 // 4) + 1, jnp.int32)
        _ctx_1024P = jax.random.normal(jax.random.fold_in(_rk, 11), (32, 16, 128), jnp.float32)
        _ctx_1024c = jax.random.dirichlet(jax.random.fold_in(_rk, 511), 0.3 * jnp.ones((16,), jnp.float32), (32, 77))
        _ctx_1024t = jnp.einsum('bsk,bkd->bsd', _ctx_1024c, _ctx_1024P)
        _ctx_1024t = _ctx_1024t * jax.lax.rsqrt(jnp.mean(jnp.square(_ctx_1024t)) + 1e-12) * 0.953939
        ctx_1024 = -1.39393e-06 + 0.999914 * (_ctx_1024t + 0.3 * jax.random.normal(jax.random.fold_in(_rk, 611), (32, 77, 128), jnp.float32))
        _validS = jnp.arange(128)[None, :] < _lenS[:, None]
        _validS2 = jnp.arange(77)[None, :] < _lenS2[:, None]
        _causal = jnp.tril(jnp.ones((128, 128), dtype=bool))
        mask_BxS2_bk0 = jnp.logical_not(jnp.broadcast_to(_validS2[:, :], (32, 77)))
        _g = jax.random.normal(jax.random.fold_in(_rk, 9001), (2, 4), jnp.float32)
        _g = jnp.sign(_g) * jnp.maximum(jnp.abs(_g), 1.0) + (_g == 0) * 1.0
        g_xattn = _g[0]
        g_ffn = _g[1]
        return (x, ctx_1024, mask_BxS2_bk0, g_xattn, g_ffn)
    x, ctx_1024, mask_BxS2_bk0, g_xattn, g_ffn = _rec_inputs()

    def _L0_xattn_setup():
        import jax, jax.numpy as jnp
        import numpy as np
        EPS = 1e-06

        def _rmsnorm(x, scale):
            var = jnp.mean(jnp.square(x), axis=-1, keepdims=True)
            return x * jax.lax.rsqrt(var + EPS) * scale
        key = jax.random.key(seed)
        ks = jax.random.split(key, 6)
        B, S, D, H, Hd = (2, 256, 128, 16, 64)
        sc = 1.0 / np.sqrt(D)
        return {'inputs_q': jax.random.normal(ks[0], (B, S, D), jnp.float32), 'inputs_kv': jax.random.normal(ks[1], (B, S, D), jnp.float32), 'Wq': jax.random.normal(ks[2], (D, H, Hd), jnp.float32) * sc, 'Wk': jax.random.normal(ks[3], (D, H, Hd), jnp.float32) * sc, 'Wv': jax.random.normal(ks[4], (D, H, Hd), jnp.float32) * sc, 'Wo': jax.random.normal(ks[5], (H, Hd, D), jnp.float32) * (1.0 / np.sqrt(D)), 'bo': jnp.zeros((D,), jnp.float32), 'gq': jnp.ones((Hd,), jnp.float32), 'gk': jnp.ones((Hd,), jnp.float32)}
    _L0_xattn_all = _L0_xattn_setup()
    _L0_xattn_in = {k: v for k, v in _L0_xattn_all.items() if k in ('Wq', 'Wk', 'Wv', 'Wo', 'bo', 'gq', 'gk')}
    del _L0_xattn_all

    def _L0_ffn_setup():
        import jax, jax.numpy as jnp
        import numpy as np
        B, N, D = (4, 512, 128)
        E, S, F = (16, 64, 256)
        DO = 128
        EPS = 1e-05

        def _layernorm(x, g, b):
            mu = jnp.mean(x, axis=-1, keepdims=True)
            var = jnp.mean(jnp.square(x - mu), axis=-1, keepdims=True)
            return (x - mu) * jax.lax.rsqrt(var + EPS) * g + b
        key = jax.random.key(seed)
        ks = jax.random.split(key, 8)
        d = {'x': jax.random.normal(ks[0], (B, N, D), dtype=jnp.float32), 'norm_g': jnp.ones((D,), jnp.float32), 'norm_b': jnp.zeros((D,), jnp.float32), 'slot_g': jnp.ones((D,), jnp.float32), 'slot_b': jnp.zeros((D,), jnp.float32), 'scale': jnp.ones((1,), jnp.float32), 'slot_embeds': jax.random.normal(ks[1], (E, S, D), jnp.float32) / np.sqrt(D), 'Wg': jax.random.normal(ks[2], (E, D, F), jnp.float32) * np.sqrt(2.0 / (D + F)), 'bg': jnp.zeros((E, F), jnp.float32), 'Wu': jax.random.normal(ks[3], (E, D, F), jnp.float32) * np.sqrt(2.0 / (D + F)), 'bu': jnp.zeros((E, F), jnp.float32), 'Wd': jax.random.normal(ks[4], (E, F, DO), jnp.float32) * np.sqrt(2.0 / (F + DO)), 'bd': jnp.zeros((E, DO), jnp.float32)}
        return d
    _L0_ffn_all = _L0_ffn_setup()
    _L0_ffn_in = {k: v for k, v in _L0_ffn_all.items() if k in ('norm_g', 'norm_b', 'slot_g', 'slot_b', 'scale', 'slot_embeds', 'Wg', 'bg', 'Wu', 'bu', 'Wd', 'bd')}
    del _L0_ffn_all

    def _L1_xattn_setup():
        import jax, jax.numpy as jnp
        import numpy as np
        B, S, D_IN, D_MODEL = (4, 256, 128, 128)
        key = jax.random.key(seed)
        ks = jax.random.split(key, 9)
        return {'q': jax.random.normal(ks[0], (B, S, D_IN), jnp.float32), 'k': jax.random.normal(ks[1], (B, S, D_IN), jnp.float32), 'v': jax.random.normal(ks[2], (B, S, D_IN), jnp.float32), 'Wq': jax.random.normal(ks[3], (D_IN, D_MODEL), jnp.float32) * 0.02, 'bq': jax.random.normal(ks[4], (D_MODEL,), jnp.float32) * 0.02, 'Wk': jax.random.normal(ks[5], (D_IN, D_MODEL), jnp.float32) * 0.02, 'bk': jax.random.normal(ks[6], (D_MODEL,), jnp.float32) * 0.02, 'Wv': jax.random.normal(ks[7], (D_IN, D_MODEL), jnp.float32) * 0.02, 'bv': jax.random.normal(ks[8], (D_MODEL,), jnp.float32) * 0.02}
    _L1_xattn_all = _L1_xattn_setup()
    _L1_xattn_in = {k: v for k, v in _L1_xattn_all.items() if k in ('Wq', 'bq', 'Wk', 'bk', 'Wv', 'bv')}
    del _L1_xattn_all

    def _L1_ffn_setup():
        import jax, jax.numpy as jnp
        import numpy as np
        B, S, D, F, E, K = (2, 256, 128, 256, 8, 2)
        key = jax.random.key(seed)
        ks = jax.random.split(key, 5)
        scale = 0.02
        return {'x': jax.random.normal(ks[0], (B, S, D), dtype=jnp.float32), 'Wg': jax.random.normal(ks[1], (E, D), dtype=jnp.float32) * scale, 'W1': jax.random.normal(ks[2], (E, F, D), dtype=jnp.float32) * scale, 'W2': jax.random.normal(ks[3], (E, F, D), dtype=jnp.float32) * scale, 'W3': jax.random.normal(ks[4], (E, D, F), dtype=jnp.float32) * scale}
    _L1_ffn_all = _L1_ffn_setup()
    _L1_ffn_in = {k: v for k, v in _L1_ffn_all.items() if k in ('Wg', 'W1', 'W2', 'W3')}
    del _L1_ffn_all

    def _L2_xattn_setup():
        import jax, jax.numpy as jnp
        import numpy as np
        HEADS = 16
        key = jax.random.key(seed)
        ks = jax.random.split(key, 6)
        b, n, m, dim = (2, 256, 64, 128)
        s = dim ** (-0.5)
        return {'x': jax.random.normal(ks[0], (b, n, dim), jnp.float32), 'mem': jax.random.normal(ks[1], (b, m, dim), jnp.float32), 'Wq': jax.random.normal(ks[2], (dim, dim), jnp.float32) * s, 'Wkv': jax.random.normal(ks[3], (dim, 2 * dim), jnp.float32) * s, 'Wout': jax.random.normal(ks[4], (dim, dim), jnp.float32) * s, 'bout': jnp.zeros((dim,), jnp.float32)}
    _L2_xattn_all = _L2_xattn_setup()
    _L2_xattn_in = {k: v for k, v in _L2_xattn_all.items() if k in ('Wq', 'Wkv', 'Wout', 'bout')}
    del _L2_xattn_all

    def _L2_ffn_setup():
        import jax, jax.numpy as jnp
        import numpy as np
        HIDDEN = 128
        INNER = 512

        def _weight_quant(w):
            scale = 1.0 / jnp.clip(jnp.mean(jnp.abs(w)), 1e-05)
            wq = jnp.clip(jnp.round(w * scale), -1.0, 1.0) / scale
            return w + jax.lax.stop_gradient(wq - w)

        def _act_quant(x):
            scale = 127.0 / jnp.clip(jnp.max(jnp.abs(x), axis=-1, keepdims=True), 1e-05)
            xq = jnp.clip(jnp.round(x * scale), -128.0, 127.0) / scale
            return x + jax.lax.stop_gradient(xq - x)

        def _bitlinear(x, w):
            return jnp.einsum('bsi,oi->bso', _act_quant(x), _weight_quant(w))
        key = jax.random.key(seed)
        k0, k1, k2, k3 = jax.random.split(key, 4)
        x = jax.random.normal(k0, (4, 256, HIDDEN), dtype=jnp.float32)
        w_gate = jax.random.normal(k1, (INNER, HIDDEN), dtype=jnp.float32) / np.sqrt(HIDDEN)
        w_up = jax.random.normal(k2, (INNER, HIDDEN), dtype=jnp.float32) / np.sqrt(HIDDEN)
        w_down = jax.random.normal(k3, (HIDDEN, INNER), dtype=jnp.float32) / np.sqrt(INNER)
        return {'x': x, 'w_gate': w_gate, 'w_up': w_up, 'w_down': w_down}
    _L2_ffn_all = _L2_ffn_setup()
    _L2_ffn_in = {k: v for k, v in _L2_ffn_all.items() if k in ('w_gate', 'w_up', 'w_down')}
    del _L2_ffn_all

    def _L3_xattn_setup():
        import jax, jax.numpy as jnp
        import numpy as np
        import math
        B, SQ, SKV = (2, 256, 256)
        DQ, DKV, H, NH = (128, 128, 128, 16)
        HD = H // NH
        key = jax.random.key(seed)
        ks = jax.random.split(key, 12)
        s = 0.02
        return {'query_input': jax.random.normal(ks[0], (B, SQ, DQ), jnp.float32), 'key_value_input': jax.random.normal(ks[1], (B, SKV, DKV), jnp.float32), 'key_padding_mask': jax.random.randint(ks[2], (B, SKV), 0, 2) > 0, 'Wq': jax.random.normal(ks[3], (DQ, H), jnp.float32) * s, 'bq': jnp.zeros((H,), jnp.float32), 'Wk': jax.random.normal(ks[4], (DKV, H), jnp.float32) * s, 'bk': jnp.zeros((H,), jnp.float32), 'Wv': jax.random.normal(ks[5], (DKV, H), jnp.float32) * s, 'bv': jnp.zeros((H,), jnp.float32), 'Wo': jax.random.normal(ks[6], (H, DQ), jnp.float32) * s, 'bo': jnp.zeros((DQ,), jnp.float32)}
    _L3_xattn_all = _L3_xattn_setup()
    _L3_xattn_in = {k: v for k, v in _L3_xattn_all.items() if k in ('Wq', 'bq', 'Wk', 'bk', 'Wv', 'bv', 'Wo', 'bo')}
    del _L3_xattn_all

    def _L3_ffn_setup():
        import jax, jax.numpy as jnp
        import numpy as np
        MIN_EXPERT_CAPACITY = 4
        CAPACITY_FACTOR = 1.0

        def _moe_forward(x, router_w, w1, b1, w2, b2):
            B, S, D = x.shape
            E = router_w.shape[1]
            G = 1
            T = B * S
            C = max(int(round(CAPACITY_FACTOR * T / E)), MIN_EXPERT_CAPACITY)
            xt = x.reshape(G, T, D)
            logits = jnp.einsum('gtd,de->gte', xt, router_w)
            probs = jax.nn.softmax(logits, axis=-1)
            gate = jnp.max(probs, axis=-1)
            idx = jnp.argmax(probs, axis=-1)
            emask = jax.nn.one_hot(idx, E, dtype=x.dtype)
            pos = jnp.cumsum(emask, axis=1) * emask - 1.0
            pos = pos.astype(jnp.int32)
            slot = jax.nn.one_hot(pos, C, dtype=x.dtype)
            dispatch = emask[..., None] * slot
            combine = dispatch * gate[..., None, None]
            expert_inputs = jnp.einsum('gtd,gtec->gecd', xt, dispatch)
            h = jax.nn.relu(jnp.einsum('gecd,edf->gecf', expert_inputs, w1) + b1[None, :, None, :])
            expert_outputs = jnp.einsum('gecf,efd->gecd', h, w2) + b2[None, :, None, :]
            out = jnp.einsum('gecd,gtec->gtd', expert_outputs, combine)
            return out.reshape(B, S, D)
        key = jax.random.key(seed)
        k0, k1, k2, k3 = jax.random.split(key, 4)
        B, S, D, E, F = (4, 256, 128, 8, 512)
        x = jax.random.normal(k0, (B, S, D), dtype=jnp.float32)
        router_w = jax.random.normal(k1, (D, E), dtype=jnp.float32) * D ** (-0.5)
        w1 = jax.random.normal(k2, (E, D, F), dtype=jnp.float32) * D ** (-0.5)
        b1 = jnp.zeros((E, F), dtype=jnp.float32)
        w2 = jax.random.normal(k3, (E, F, D), dtype=jnp.float32) * F ** (-0.5)
        b2 = jnp.zeros((E, D), dtype=jnp.float32)
        return {'x': x, 'router_w': router_w, 'w1': w1, 'b1': b1, 'w2': w2, 'b2': b2}
    _L3_ffn_all = _L3_ffn_setup()
    _L3_ffn_in = {k: v for k, v in _L3_ffn_all.items() if k in ('router_w', 'w1', 'b1', 'w2', 'b2')}
    del _L3_ffn_all
    return {'x': x, 'ctx_1024': ctx_1024, 'mask_BxS2_bk0': mask_BxS2_bk0, 'g_xattn': g_xattn, 'g_ffn': g_ffn, 'L0_xattn_Wq': _L0_xattn_in['Wq'], 'L0_xattn_Wk': _L0_xattn_in['Wk'], 'L0_xattn_Wv': _L0_xattn_in['Wv'], 'L0_xattn_Wo': _L0_xattn_in['Wo'], 'L0_xattn_bo': _L0_xattn_in['bo'], 'L0_xattn_gq': _L0_xattn_in['gq'], 'L0_xattn_gk': _L0_xattn_in['gk'], 'L0_ffn_norm_g': _L0_ffn_in['norm_g'], 'L0_ffn_norm_b': _L0_ffn_in['norm_b'], 'L0_ffn_slot_g': _L0_ffn_in['slot_g'], 'L0_ffn_slot_b': _L0_ffn_in['slot_b'], 'L0_ffn_scale': _L0_ffn_in['scale'], 'L0_ffn_slot_embeds': _L0_ffn_in['slot_embeds'], 'L0_ffn_Wg': _L0_ffn_in['Wg'], 'L0_ffn_bg': _L0_ffn_in['bg'], 'L0_ffn_Wu': _L0_ffn_in['Wu'], 'L0_ffn_bu': _L0_ffn_in['bu'], 'L0_ffn_Wd': _L0_ffn_in['Wd'], 'L0_ffn_bd': _L0_ffn_in['bd'], 'L1_xattn_Wq': _L1_xattn_in['Wq'], 'L1_xattn_bq': _L1_xattn_in['bq'], 'L1_xattn_Wk': _L1_xattn_in['Wk'], 'L1_xattn_bk': _L1_xattn_in['bk'], 'L1_xattn_Wv': _L1_xattn_in['Wv'], 'L1_xattn_bv': _L1_xattn_in['bv'], 'L1_ffn_Wg': _L1_ffn_in['Wg'], 'L1_ffn_W1': _L1_ffn_in['W1'], 'L1_ffn_W2': _L1_ffn_in['W2'], 'L1_ffn_W3': _L1_ffn_in['W3'], 'L2_xattn_Wq': _L2_xattn_in['Wq'], 'L2_xattn_Wkv': _L2_xattn_in['Wkv'], 'L2_xattn_Wout': _L2_xattn_in['Wout'], 'L2_xattn_bout': _L2_xattn_in['bout'], 'L2_ffn_w_gate': _L2_ffn_in['w_gate'], 'L2_ffn_w_up': _L2_ffn_in['w_up'], 'L2_ffn_w_down': _L2_ffn_in['w_down'], 'L3_xattn_Wq': _L3_xattn_in['Wq'], 'L3_xattn_bq': _L3_xattn_in['bq'], 'L3_xattn_Wk': _L3_xattn_in['Wk'], 'L3_xattn_bk': _L3_xattn_in['bk'], 'L3_xattn_Wv': _L3_xattn_in['Wv'], 'L3_xattn_bv': _L3_xattn_in['bv'], 'L3_xattn_Wo': _L3_xattn_in['Wo'], 'L3_xattn_bo': _L3_xattn_in['bo'], 'L3_ffn_router_w': _L3_ffn_in['router_w'], 'L3_ffn_w1': _L3_ffn_in['w1'], 'L3_ffn_b1': _L3_ffn_in['b1'], 'L3_ffn_w2': _L3_ffn_in['w2'], 'L3_ffn_b2': _L3_ffn_in['b2']}

def reference(x, ctx_1024, mask_BxS2_bk0, g_xattn, g_ffn, L0_xattn_Wq, L0_xattn_Wk, L0_xattn_Wv, L0_xattn_Wo, L0_xattn_bo, L0_xattn_gq, L0_xattn_gk, L0_ffn_norm_g, L0_ffn_norm_b, L0_ffn_slot_g, L0_ffn_slot_b, L0_ffn_scale, L0_ffn_slot_embeds, L0_ffn_Wg, L0_ffn_bg, L0_ffn_Wu, L0_ffn_bu, L0_ffn_Wd, L0_ffn_bd, L1_xattn_Wq, L1_xattn_bq, L1_xattn_Wk, L1_xattn_bk, L1_xattn_Wv, L1_xattn_bv, L1_ffn_Wg, L1_ffn_W1, L1_ffn_W2, L1_ffn_W3, L2_xattn_Wq, L2_xattn_Wkv, L2_xattn_Wout, L2_xattn_bout, L2_ffn_w_gate, L2_ffn_w_up, L2_ffn_w_down, L3_xattn_Wq, L3_xattn_bq, L3_xattn_Wk, L3_xattn_bk, L3_xattn_Wv, L3_xattn_bv, L3_xattn_Wo, L3_xattn_bo, L3_ffn_router_w, L3_ffn_w1, L3_ffn_b1, L3_ffn_w2, L3_ffn_b2):
    import jax
    import jax.numpy as jnp

    def _L0_xattn_ref(inputs_q, inputs_kv, Wq, Wk, Wv, Wo, bo, gq, gk):
        import jax, jax.numpy as jnp
        import numpy as np
        EPS = 1e-06

        def _rmsnorm(x, scale):
            var = jnp.mean(jnp.square(x), axis=-1, keepdims=True)
            return x * jax.lax.rsqrt(var + EPS) * scale
        q = jnp.einsum('bsd,dhe->bshe', inputs_q, Wq)
        k = jnp.einsum('bsd,dhe->bshe', inputs_kv, Wk)
        v = jnp.einsum('bsd,dhe->bshe', inputs_kv, Wv)
        q = _rmsnorm(q, gq)
        k = _rmsnorm(k, gk)
        head_dim = q.shape[-1]
        scores = jnp.einsum('bqhe,bkhe->bhqk', q, k) / jnp.sqrt(jnp.asarray(head_dim, q.dtype))
        attn = jax.nn.softmax(scores, axis=-1)
        x = jnp.einsum('bhqk,bkhe->bqhe', attn, v)
        out = jnp.einsum('bqhe,hed->bqd', x, Wo) + bo
        return out

    def _L0_ffn_ref(x, norm_g, norm_b, slot_g, slot_b, scale, slot_embeds, Wg, bg, Wu, bu, Wd, bd):
        import jax, jax.numpy as jnp
        import numpy as np
        B, N, D = (4, 512, 128)
        E, S, F = (16, 64, 256)
        DO = 128
        EPS = 1e-05

        def _layernorm(x, g, b):
            mu = jnp.mean(x, axis=-1, keepdims=True)
            var = jnp.mean(jnp.square(x - mu), axis=-1, keepdims=True)
            return (x - mu) * jax.lax.rsqrt(var + EPS) * g + b
        x = _layernorm(x, norm_g, norm_b)
        se = _layernorm(slot_embeds, slot_g, slot_b) * scale
        logits = jnp.einsum('bnd,esd->bnes', x, se)
        dispatch = jax.nn.softmax(logits, axis=1)
        combine = jax.nn.softmax(logits.reshape(x.shape[0], x.shape[1], -1), axis=-1)
        slots = jnp.einsum('bnd,bnes->besd', x, dispatch)
        gate = jax.nn.gelu(jnp.einsum('besd,edf->besf', slots, Wg) + bg[None, :, None, :], approximate=False)
        up = jnp.einsum('besd,edf->besf', slots, Wu) + bu[None, :, None, :]
        eout = jnp.einsum('besf,efo->beso', gate * up, Wd) + bd[None, :, None, :]
        eout = eout.reshape(eout.shape[0], -1, eout.shape[-1])
        return jnp.einsum('bns,bso->bno', combine, eout)

    def _L1_xattn_ref(q, k, v, Wq, bq, Wk, bk, Wv, bv):
        import jax, jax.numpy as jnp
        import numpy as np
        B, S, D_IN, D_MODEL = (4, 256, 128, 128)
        qp = jnp.einsum('bsd,de->bse', q, Wq) + bq
        kp = jnp.einsum('bsd,de->bse', k, Wk) + bk
        vp = jnp.einsum('bsd,de->bse', v, Wv) + bv
        scale = 1.0 / jnp.sqrt(jnp.asarray(kp.shape[-1], jnp.float32))
        logits = jnp.einsum('bqe,bke->bqk', qp, kp) * scale
        attn = jax.nn.softmax(logits, axis=-1)
        return jnp.einsum('bqk,bke->bqe', attn, vp)

    def _L1_ffn_ref(x, Wg, W1, W2, W3):
        import jax, jax.numpy as jnp
        import numpy as np
        B, S, D, F, E, K = (2, 256, 128, 256, 8, 2)
        k = K
        scores = jnp.einsum('bsd,ed->bse', x, Wg)
        topk_scores, topk_idx = jax.lax.top_k(scores, k)
        topk_probs = jax.nn.softmax(topk_scores, axis=-1)
        h1 = jnp.einsum('bsd,efd->bsef', x, W1)
        h2 = jnp.einsum('bsd,efd->bsef', x, W2)
        hidden = jax.nn.silu(h1) * h2
        expert_out = jnp.einsum('bsef,edf->bsed', hidden, W3)
        onehot = jax.nn.one_hot(topk_idx, scores.shape[-1], dtype=x.dtype)
        gating = jnp.einsum('bsk,bske->bse', topk_probs, onehot)
        return jnp.einsum('bse,bsed->bsd', gating, expert_out)

    def _L2_xattn_ref(x, mem, Wq, Wkv, Wout, bout):
        import jax, jax.numpy as jnp
        import numpy as np
        HEADS = 16
        b, n, dim = x.shape
        h = HEADS
        d = dim // h
        scale = d ** (-0.5)
        mem_len = mem.shape[1]
        q = x @ Wq
        xc = jnp.concatenate((mem, x), axis=1)
        kv = xc @ Wkv
        k, v = jnp.split(kv, 2, axis=-1)

        def to_heads(t):
            bb, nn, _ = t.shape
            return t.reshape(bb, nn, h, d).transpose(0, 2, 1, 3)
        q, k, v = (to_heads(q), to_heads(k), to_heads(v))
        dots = jnp.einsum('bhid,bhjd->bhij', q, k) * scale
        j = dots.shape[-1]
        i_idx = jnp.arange(n)[:, None]
        j_idx = jnp.arange(j)[None, :]
        mask = j_idx > i_idx + mem_len
        dots = jnp.where(mask[None, None], -jnp.inf, dots)
        attn = jax.nn.softmax(dots, axis=-1)
        out = jnp.einsum('bhij,bhjd->bhid', attn, v)
        out = out.transpose(0, 2, 1, 3).reshape(b, n, dim)
        return out @ Wout + bout

    def _L2_ffn_ref(x, w_gate, w_up, w_down):
        import jax, jax.numpy as jnp
        import numpy as np
        HIDDEN = 128
        INNER = 512

        def _weight_quant(w):
            scale = 1.0 / jnp.clip(jnp.mean(jnp.abs(w)), 1e-05)
            wq = jnp.clip(jnp.round(w * scale), -1.0, 1.0) / scale
            return w + jax.lax.stop_gradient(wq - w)

        def _act_quant(x):
            scale = 127.0 / jnp.clip(jnp.max(jnp.abs(x), axis=-1, keepdims=True), 1e-05)
            xq = jnp.clip(jnp.round(x * scale), -128.0, 127.0) / scale
            return x + jax.lax.stop_gradient(xq - x)

        def _bitlinear(x, w):
            return jnp.einsum('bsi,oi->bso', _act_quant(x), _weight_quant(w))
        gate = jax.nn.silu(_bitlinear(x, w_gate))
        up = _bitlinear(x, w_up)
        return _bitlinear(gate * up, w_down)

    def _L3_xattn_ref(query_input, key_value_input, key_padding_mask, Wq, bq, Wk, bk, Wv, bv, Wo, bo):
        import jax, jax.numpy as jnp
        import numpy as np
        import math
        B, SQ, SKV = (2, 256, 256)
        DQ, DKV, H, NH = (128, 128, 128, 16)
        HD = H // NH
        b, sq, _ = query_input.shape
        skv = key_value_input.shape[1]
        Q = query_input @ Wq + bq
        K = key_value_input @ Wk + bk
        V = key_value_input @ Wv + bv
        Q = Q.reshape(b, sq, NH, HD).transpose(0, 2, 1, 3)
        K = K.reshape(b, skv, NH, HD).transpose(0, 2, 1, 3)
        V = V.reshape(b, skv, NH, HD).transpose(0, 2, 1, 3)
        scores = jnp.einsum('bhqd,bhkd->bhqk', Q, K) / math.sqrt(HD)
        mask = key_padding_mask[:, None, None, :]
        scores = jnp.where(mask, -jnp.inf, scores)
        attn = jax.nn.softmax(scores, axis=-1)
        out = jnp.einsum('bhqk,bhkd->bhqd', attn, V)
        out = out.transpose(0, 2, 1, 3).reshape(b, sq, H)
        return out @ Wo + bo

    def _L3_ffn_ref(x, router_w, w1, b1, w2, b2):
        import jax, jax.numpy as jnp
        import numpy as np
        MIN_EXPERT_CAPACITY = 4
        CAPACITY_FACTOR = 1.0

        def _moe_forward(x, router_w, w1, b1, w2, b2):
            B, S, D = x.shape
            E = router_w.shape[1]
            G = 1
            T = B * S
            C = max(int(round(CAPACITY_FACTOR * T / E)), MIN_EXPERT_CAPACITY)
            xt = x.reshape(G, T, D)
            logits = jnp.einsum('gtd,de->gte', xt, router_w)
            probs = jax.nn.softmax(logits, axis=-1)
            gate = jnp.max(probs, axis=-1)
            idx = jnp.argmax(probs, axis=-1)
            emask = jax.nn.one_hot(idx, E, dtype=x.dtype)
            pos = jnp.cumsum(emask, axis=1) * emask - 1.0
            pos = pos.astype(jnp.int32)
            slot = jax.nn.one_hot(pos, C, dtype=x.dtype)
            dispatch = emask[..., None] * slot
            combine = dispatch * gate[..., None, None]
            expert_inputs = jnp.einsum('gtd,gtec->gecd', xt, dispatch)
            h = jax.nn.relu(jnp.einsum('gecd,edf->gecf', expert_inputs, w1) + b1[None, :, None, :])
            expert_outputs = jnp.einsum('gecf,efd->gecd', h, w2) + b2[None, :, None, :]
            out = jnp.einsum('gecd,gtec->gtd', expert_outputs, combine)
            return out.reshape(B, S, D)
        return _moe_forward(x, router_w, w1, b1, w2, b2)
    x = x + jnp.tanh(g_xattn[0]) * _L0_xattn_ref(_layernorm(x, axis=-1), ctx_1024, L0_xattn_Wq, L0_xattn_Wk, L0_xattn_Wv, L0_xattn_Wo, L0_xattn_bo, L0_xattn_gq, L0_xattn_gk)
    x = x + jnp.tanh(g_ffn[0]) * _L0_ffn_ref(_layernorm(x, axis=-1), L0_ffn_norm_g, L0_ffn_norm_b, L0_ffn_slot_g, L0_ffn_slot_b, L0_ffn_scale, L0_ffn_slot_embeds, L0_ffn_Wg, L0_ffn_bg, L0_ffn_Wu, L0_ffn_bu, L0_ffn_Wd, L0_ffn_bd)
    x = x + jnp.tanh(g_xattn[1]) * _L1_xattn_ref(_layernorm(x, axis=-1), ctx_1024, ctx_1024, L1_xattn_Wq, L1_xattn_bq, L1_xattn_Wk, L1_xattn_bk, L1_xattn_Wv, L1_xattn_bv)
    x = x + jnp.tanh(g_ffn[1]) * _L1_ffn_ref(_layernorm(x, axis=-1), L1_ffn_Wg, L1_ffn_W1, L1_ffn_W2, L1_ffn_W3)
    x = x + jnp.tanh(g_xattn[2]) * _L2_xattn_ref(_layernorm(x, axis=-1), ctx_1024, L2_xattn_Wq, L2_xattn_Wkv, L2_xattn_Wout, L2_xattn_bout)
    x = x + jnp.tanh(g_ffn[2]) * _L2_ffn_ref(_layernorm(x, axis=-1), L2_ffn_w_gate, L2_ffn_w_up, L2_ffn_w_down)
    x = x + jnp.tanh(g_xattn[3]) * _L3_xattn_ref(_layernorm(x, axis=-1), ctx_1024, mask_BxS2_bk0, L3_xattn_Wq, L3_xattn_bq, L3_xattn_Wk, L3_xattn_bk, L3_xattn_Wv, L3_xattn_bv, L3_xattn_Wo, L3_xattn_bo)
    x = x + jnp.tanh(g_ffn[3]) * _L3_ffn_ref(_layernorm(x, axis=-1), L3_ffn_router_w, L3_ffn_w1, L3_ffn_b1, L3_ffn_w2, L3_ffn_b2)
    return x

_drawn_inputs = setup_inputs


def setup_inputs(seed=0):
    import zlib

    import numpy as np

    out = dict(_drawn_inputs(seed))
    spreads = {'L0_xattn_bo': (0.0, 0.1),
     'L0_xattn_gq': (1.0, 0.2),
     'L0_xattn_gk': (1.0, 0.2),
     'L0_ffn_norm_g': (1.0, 0.2),
     'L0_ffn_norm_b': (0.0, 0.1),
     'L0_ffn_slot_g': (1.0, 0.2),
     'L0_ffn_slot_b': (0.0, 0.1),
     'L0_ffn_bg': (0.0, 0.1),
     'L0_ffn_bu': (0.0, 0.1),
     'L0_ffn_bd': (0.0, 0.1),
     'L2_xattn_bout': (0.0, 0.403),
     'L3_xattn_bq': (0.0, 0.8),
     'L3_xattn_bk': (0.0, 2.0),
     'L3_xattn_bv': (0.0, 0.603),
     'L3_xattn_bo': (0.0, 0.387),
     'L3_ffn_b1': (0.0, 0.626),
     'L3_ffn_b2': (0.0, 0.448)}
    factors = {'g_ffn': 8.0,
     'L1_xattn_Wq': 8.0,
     'L1_xattn_bq': 8.0,
     'L1_xattn_Wk': 8.0,
     'L1_xattn_bk': 64.0,
     'L1_xattn_bv': 3.589,
     'L1_ffn_Wg': 8.0,
     'L1_ffn_W1': 7.675,
     'L1_ffn_W2': 8.0,
     'L1_ffn_W3': 8.0,
     'L3_xattn_Wq': 8.0,
     'L3_xattn_Wk': 8.0,
     'L3_xattn_Wv': 3.615,
     'L3_xattn_Wo': 2.823}
    for name, (base, spread) in spreads.items():
        noise = np.random.default_rng([zlib.crc32(name.encode()), seed]).standard_normal(out[name].shape)
        drawn = base * np.exp(spread * noise) if base else spread * noise
        out[name] = jnp.asarray(drawn.astype(out[name].dtype))
    for name, factor in factors.items():
        out[name] = (out[name] * factor).astype(out[name].dtype)
    return out
```

```python
from collections import namedtuple
from contextlib import ExitStack

import concourse.bass as bass
from concourse import mybir

F32 = mybir.dt.float32
BF16 = mybir.dt.bfloat16
U8 = mybir.dt.uint8
U32 = mybir.dt.uint32
ALU = mybir.AluOpType
ACT = mybir.ActivationFunctionType
AX = mybir.AxisListType

B, S, D = 32, 128, 128
SC = 77
LN_EPS = 1e-5
NEG = -1e30


class Shared:
    pass


def Names(**named):
    return namedtuple("Names", sorted(named))(**named)


def semaphores(nc, own, phase, names):
    found = {n: nc.alloc_semaphore(name=f"{phase}_{n}") for n in names.split()}
    own += found.values()
    return Names(**found)


def bcast(ap, n):
    return ap.unsqueeze(2).broadcast_to([ap.shape[0], ap.shape[1], n])


def sublayer(build):
    def scoped(nc, m, *args):
        own = []
        build(nc, own, m, *args)
        nc.clear_and_free_semaphores(own)
        nc.all_engine_barrier()
    return scoped


def staggered(eng, turns, lanes, steps):
    n = len(steps)
    lag = n // lanes
    for i in range(n):
        for l in range(lanes):
            if i >= lag * l:
                steps[i - lag * l](0, l)
    with eng.Fori(0, turns - 1) as t:
        for i in range(n):
            for l in range(lanes):
                if i >= lag * l:
                    steps[i - lag * l](t + 1, l)
                else:
                    steps[i - lag * l + n](t, l)
    for i in range(lag * (lanes - 1)):
        for l in range(lanes):
            if i < lag * l:
                steps[i - lag * l + n](turns - 1, l)


def rest(turn, lane):
    pass
PHASES = range(8)


def token_stats(dve, m, s, l, batch, n):
    dve.bn_stats(l.stats[:], m.x[:, bass.ds(batch * D, D)]).then_inc(s.stats, 1)
    dve.wait_ge(s.stats, n)
    dve.memset(m.wait_pad[:], 0.0)
    dve.bn_aggr(l.mv[:], l.stats[:]).then_inc(s.mv, 1)
    dve.wait_ge(s.mv, n)
    dve.tensor_scalar(l.var_eps[:], l.mv[:, 1:2], LN_EPS, None, ALU.add).then_inc(s.var_eps, 1)


def layer_norm_stats(dve, m, s, turn, lanes, lane_offset=0):
    L = len(lanes)
    for i, l in enumerate(lanes):
        dve.bn_stats(l.stats[:], m.x[:, bass.ds((turn * L + i) * D, D)]).then_inc(s.stats, 1)
    dve.wait_ge(s.stats, turn * L + L)
    dve.memset(m.wait_pad[:], 0.0)
    for i, l in enumerate(lanes):
        dve.bn_aggr(l.mv[:], l.stats[:]).then_inc(s.mv, 1)
    for i, l in enumerate(lanes):
        dve.wait_ge(s.mv, turn * L + i + 1)
        dve.tensor_scalar(l.var_eps[:], l.mv[:, 1:2], LN_EPS, None, ALU.add).then_inc(s.var_eps, 1)


def load_context(sp, io, s, lane, c_in, turns):
    L = len(lane)
    for l in range(L):
        sp.dma_start(lane[l].c[:], io.ctx[l]).then_inc(c_in[l], 16)
    with sp.Fori(0, turns - 1) as t:
        for l in range(L):
            sp.wait_ge(s.xt_ps, t * L + l + 1)
            sp.dma_start(lane[l].c[:], io.ctx[bass.ds((t + 1) * L + l, 1)].rearrange("a s d -> (a s) d")
                         ).then_inc(c_in[l], 16)


def inverse_root(pool, out, in_, m, done):
    n = in_.shape[1]
    pool.tensor_tensor(out, in_, m.minus_half[0:in_.shape[0], 0:n], ALU.pow).then_inc(done, 1)


@sublayer
def l0_attention(nc, ctx, m, io):
    H, HD = 16, 64
    HH = H // 2
    LANES = 4
    TURNS = B // LANES
    s = semaphores(nc, ctx, "a0", "stats mv var_eps rstd xn xt_ps xt q_ps q_sq q_ss q_ms q_r q_n v_ps v k_ps k_sq k_ss "
                   "k_ms k_r k_n qt_ps qt kt_ps kt at_ps at y_ps x "
                   "c0 c1 c2 c3 ones")
    c_in = [s.c0, s.c1, s.c2, s.c3]

    def nth(turn, lane):
        return turn * LANES + lane + 1

    half = [semaphores(nc, ctx, f"a0h{k}", "s_ps s_max s_sub p pt_ps pt o_ps o_r o") for k in range(2)]

    with ExitStack() as mem:
        def sb(name, shape, dt=F32):
            return mem.enter_context(nc.sbuf_tensor("a0_" + name, shape, dt))

        def lane_buffers(l):
            return Names(
                stats=sb(f"stats{l}", [S, 6]), mv=sb(f"mv{l}", [S, 2]), var_eps=sb(f"var{l}", [S, 1]),
                rstd=sb(f"rstd{l}", [S, 1]), xn=sb(f"xn{l}", [S, D]), xt=sb(f"xt{l}", [D, S]),
                c=sb(f"c{l}", [SC, D]), ct=sb(f"ct{l}", [D, SC]),
                sq=sb(f"sq{l}", [128, H * HD]),
                ss=sb(f"ss{l}", [S, H]), ms=sb(f"ms{l}", [S, H]), r=sb(f"r{l}", [S, H]),
                kss=sb(f"kss{l}", [SC, H]), kms=sb(f"kms{l}", [SC, H]), kr=sb(f"kr{l}", [SC, H]),
                qn=sb(f"qn{l}", [S, H * HD]),
                kn=sb(f"kn{l}", [128, H * HD]),
                v=sb(f"v{l}", [SC, H, HD + 1]),
                qt=sb(f"qt{l}", [128, HH, S]), kt=sb(f"kt{l}", [128, HH, SC]),
                mx=sb(f"mx{l}", [S, 2, HH]), p=sb(f"p{l}", [S, 2, HH, SC]), rs=sb(f"rs{l}", [S, 2, HH]))

        lane = [lane_buffers(l) for l in range(LANES)]
        pt = [b.sq[0:SC, :].rearrange("p (i q) -> p i q", q=S) for b in lane]
        heads_out = [b.qn[:].rearrange("p (i a e) -> p i a e", a=2, e=HD) for b in lane]
        out_t = [b.kn[:].rearrange("p (i q) -> p i q", q=S) for b in lane]
        ps = [mem.enter_context(nc.psum_tensor(f"a0_ps{l}", [128, 2, 512], F32)) for l in range(LANES)]
        block = mem.enter_context(nc.Block())

        def by_chunk(l, n):
            return ps[l][:, :, 0:4 * n].rearrange("p b (j n) -> p b j n", n=n)

        @block.sync
        def _(sp):
            load_context(sp, io, s, lane, c_in, TURNS)

        @block.tensor
        def _(pe):
            pe.wait_ge(m.s_w0, m.n_w0)

            def inputs(t, l):
                pe.wait_ge(s.xn, nth(t, l))
                pe.wait_ge(c_in[l], 16 * t + 16)
                pe.transpose(ps[l][:, 0, 0:S], lane[l].xn[:], m.ident[:])
                pe.transpose(ps[l][:, 0, S:S + SC], lane[l].c[:], m.ident[0:SC, 0:SC]).then_inc(s.xt_ps, 1)

            def project(l, out, lhs, w, done):
                for n in range(2):
                    mm = pe.matmul(out[:, n, :], lhs, w[:, 512 * n:512 * n + 512], start=True, stop=True)
                mm.then_inc(done, 1)

            def project_k(t, l):
                pe.wait_ge(s.xt, nth(t, l))
                project(l, ps[l][0:SC], lane[l].ct[:], m.wk0, s.k_ps)

            def project_v(t, l):
                pe.wait_ge(s.k_n, nth(t, l))
                project(l, ps[l][0:SC], lane[l].ct[:], m.wv0, s.v_ps)

            def project_q(t, l):
                pe.wait_ge(s.v, nth(t, l))
                project(l, ps[l], lane[l].xt[:], m.wq0, s.q_ps)

            def transpose_q(t, l):
                pe.wait_ge(s.q_n, nth(t, l))
                for j in range(HH):
                    mm = pe.transpose(ps[l][:, j // 4, j % 4 * S:j % 4 * S + S],
                                      lane[l].qn[:, 128 * j:128 * j + 128], m.ident[:])
                mm.then_inc(s.qt_ps, 1)

            def transpose_k(t, l):
                pe.wait_ge(s.qt, nth(t, l))
                for j in range(HH):
                    mm = pe.transpose(ps[l][:, j // 4, j % 4 * SC:j % 4 * SC + SC],
                                      lane[l].kn[0:SC, 128 * j:128 * j + 128], m.ident[0:SC, 0:SC])
                mm.then_inc(s.kt_ps, 1)

            def scores(odd):
                def step(t, l):
                    if odd:
                        pe.wait_ge(half[0].s_sub, nth(t, l))
                    else:
                        pe.wait_ge(s.kt, nth(t, l))
                    row = slice(HD * odd, HD * odd + HD)
                    for j in range(HH):
                        mm = pe.matmul(ps[l][:, j // 4, j % 4 * SC:j % 4 * SC + SC],
                                       lane[l].qt[row, j, :], lane[l].kt[row, j, :], start=True, stop=True)
                    mm.then_inc(half[odd].s_ps, 1)
                return step

            def transpose_p(odd):
                def step(t, l):
                    pe.wait_ge(half[odd].p, nth(t, l))
                    if odd:
                        pe.wait_ge(half[0].o, nth(t, l))
                    else:
                        pe.wait_ge(half[1].s_sub, nth(t, l))
                    for j in range(HH):
                        mm = pe.transpose(ps[l][0:SC, j // 4, j % 4 * S:j % 4 * S + S], lane[l].p[:, odd, j, :],
                                          m.ident[:])
                    mm.then_inc(half[odd].pt_ps, 1)
                return step

            def mix_v(odd):
                def step(t, l):
                    pe.wait_ge(half[odd].pt, nth(t, l))
                    for j in range(HH):
                        mm = pe.matmul(ps[l][:, j // 4, j % 4 * (HD + 1):j % 4 * (HD + 1) + HD + 1],
                                       pt[l][:, j, :], lane[l].v[:, 2 * j + odd, :], start=True, stop=True)
                    mm.then_inc(half[odd].o_ps, 1)
                return step

            def transpose_o(t, l):
                pe.wait_ge(half[1].o, nth(t, l))
                for j in range(HH):
                    mm = pe.transpose(ps[l][:, j // 4, j % 4 * S:j % 4 * S + S], lane[l].qn[:, 128 * j:128 * j + 128],
                                      m.ident[:])
                mm.then_inc(s.at_ps, 1)

            def project_o(t, l):
                pe.wait_ge(s.at, nth(t, l))
                for j in range(HH):
                    pe.matmul(ps[l][:, 0, 0:D], out_t[l][:, j, :], m.wo0[:, j, :], start=(j == 0), stop=False)
                pe.matmul(ps[l][:, 0, 0:D], m.ones_row[:], m.rows[0:1, m.row_bo0, :], start=False, stop=True
                          ).then_inc(s.y_ps, 1)

            staggered(pe, TURNS, LANES, [
                rest, rest, inputs, project_k, rest,
                rest, project_v, project_q, rest, rest,
                transpose_q, transpose_k, scores(0), scores(1), transpose_p(0),
                mix_v(0), transpose_p(1), mix_v(1), transpose_o, project_o])

        @block.scalar
        def _(act):
            def inputs(t, l):
                act.wait_ge(s.xt_ps, nth(t, l))
                act.copy(lane[l].xt[:], ps[l][:, 0, 0:S])
                act.copy(lane[l].ct[:], ps[l][:, 0, S:S + SC]).then_inc(s.xt, 1)

            def square_k(t, l):
                act.wait_ge(s.k_ps, nth(t, l))
                act.activation(lane[l].sq[0:SC, :], ps[l][0:SC].rearrange("p b n -> p (b n)"), ACT.Square
                               ).then_inc(s.k_sq, 1)

            def copy_v(t, l):
                act.wait_ge(s.v_ps, nth(t, l))
                act.copy(lane[l].v[:, :, 0:HD],
                         ps[l][0:SC].rearrange("p b (h e) -> p (b h) e", e=HD)).then_inc(s.v, 1)

            def square_q(t, l):
                act.wait_ge(s.q_ps, nth(t, l))
                act.activation(lane[l].sq[:], ps[l][:].rearrange("p b n -> p (b n)"), ACT.Square).then_inc(s.q_sq, 1)

            def copy_qt(t, l):
                act.wait_ge(s.qt_ps, nth(t, l))
                act.copy(lane[l].qt[:].rearrange("p (b j) q -> p b j q", b=2), by_chunk(l, S)).then_inc(s.qt, 1)

            def exponential(odd):
                def step(t, l):
                    act.wait_ge(half[odd].s_sub, nth(t, l))
                    act.activation(lane[l].p[:, odd], lane[l].p[:, odd], ACT.Exp, scale=HD ** -0.5
                                   ).then_inc(half[odd].p, 1)
                return step

            def copy_pt(odd):
                def step(t, l):
                    act.wait_ge(half[odd].pt_ps, nth(t, l))
                    act.copy(pt[l].rearrange("p (b j) q -> p b j q", b=2), by_chunk(l, S)[0:SC]).then_inc(half[odd].pt, 1)
                return step

            def copy_ot(t, l):
                act.wait_ge(s.at_ps, nth(t, l))
                act.copy(out_t[l].rearrange("p (b j) q -> p b j q", b=2), by_chunk(l, S)).then_inc(s.at, 1)

            staggered(act, TURNS, LANES, [
                rest, rest, inputs, square_k, rest,
                rest, copy_v, square_q, rest, rest,
                copy_qt, rest, rest, exponential(0), exponential(1),
                copy_pt(0), rest, copy_pt(1), copy_ot, rest])

        @block.gpsimd
        def _(pool):
            def root_ln(t, l):
                pool.wait_ge(s.var_eps, nth(t, l))
                inverse_root(pool, lane[l].rstd[:], lane[l].var_eps[:], m, s.rstd)

            def root_k(t, l):
                pool.wait_ge(s.k_ms, nth(t, l))
                inverse_root(pool, lane[l].kr[:], lane[l].kms[:], m, s.k_r)

            def root_q(t, l):
                pool.wait_ge(s.q_ms, nth(t, l))
                inverse_root(pool, lane[l].r[:], lane[l].ms[:], m, s.q_r)

            staggered(pool, TURNS, LANES, [
                root_ln, rest, rest, root_k, rest,
                rest, rest, root_q, rest, rest,
                rest, rest, rest, rest, rest,
                rest, rest, rest, rest, rest])

        @block.vector
        def _(dve):
            for l in range(LANES):
                dve.memset(lane[l].v[:, :, HD:HD + 1], 1.0).then_inc(s.ones, 1)
            dve.wait_ge(s.ones, LANES)

            def stats(t, l):
                token_stats(dve, m, s, lane[l], t * LANES + l, nth(t, l))

            def normalise(t, l):
                dve.wait_ge(s.rstd, nth(t, l))
                dve.tensor_scalar(lane[l].xn[:], m.x[:, bass.ds((t * LANES + l) * D, D)], lane[l].mv[:, 0:1],
                                  lane[l].rstd[:], ALU.subtract, ALU.mult).then_inc(s.xn, 1)

            def mean_square_k(t, l):
                dve.wait_ge(s.k_sq, nth(t, l))
                dve.tensor_reduce(lane[l].kss[:], lane[l].sq[0:SC].rearrange("p (h e) -> p h e", e=HD), AX.X,
                                  ALU.add).then_inc(s.k_ss, 1)
                dve.wait_ge(s.k_ss, nth(t, l))
                dve.tensor_scalar(lane[l].kms[:], lane[l].kss[:], 1.0 / HD, 1e-6, ALU.mult, ALU.add).then_inc(s.k_ms, 1)

            def scale_k(t, l):
                dve.wait_ge(s.k_r, nth(t, l))
                dve.tensor_tensor(lane[l].kn[0:SC].rearrange("p (h e) -> p h e", e=HD),
                                  ps[l][0:SC].rearrange("p b (h e) -> p (b h) e", e=HD),
                                  bcast(lane[l].kr[:], HD), ALU.mult).then_inc(s.k_n, 1)

            def mean_square_q(t, l):
                dve.wait_ge(s.q_sq, nth(t, l))
                dve.tensor_reduce(lane[l].ss[:], lane[l].sq[:].rearrange("p (h e) -> p h e", e=HD), AX.X, ALU.add
                                  ).then_inc(s.q_ss, 1)
                dve.wait_ge(s.q_ss, nth(t, l))
                dve.tensor_scalar(lane[l].ms[:], lane[l].ss[:], 1.0 / HD, 1e-6, ALU.mult, ALU.add).then_inc(s.q_ms, 1)

            def scale_q(t, l):
                dve.wait_ge(s.q_r, nth(t, l))
                dve.tensor_tensor(lane[l].qn[:].rearrange("p (h e) -> p h e", e=HD),
                                  ps[l][:].rearrange("p b (h e) -> p (b h) e", e=HD),
                                  bcast(lane[l].r[:], HD), ALU.mult).then_inc(s.q_n, 1)

            def scale_kt(t, l):
                dve.wait_ge(s.kt_ps, nth(t, l))
                dve.tensor_scalar(lane[l].kt[:].rearrange("p (b j) n -> p b j n", b=2), by_chunk(l, SC),
                                  m.gqk[:], None, ALU.mult).then_inc(s.kt, 1)

            def less_maximum(odd):
                def step(t, l):
                    mx = lane[l].mx[:, odd].rearrange("p (b j) -> p b j", b=2)
                    dve.wait_ge(half[odd].s_ps, nth(t, l))
                    dve.tensor_reduce(mx, by_chunk(l, SC), AX.X, ALU.max).then_inc(half[odd].s_max, 1)
                    dve.wait_ge(half[odd].s_max, nth(t, l))
                    dve.tensor_tensor(lane[l].p[:, odd].rearrange("p (b j) n -> p b j n", b=2), by_chunk(l, SC),
                                      mx.unsqueeze(3).broadcast_to([S, 2, 4, SC]), ALU.subtract
                                      ).then_inc(half[odd].s_sub, 1)
                return step

            def divide(odd):
                def step(t, l):
                    rs = lane[l].rs[:, odd].rearrange("p (b j) -> p b j", b=2)
                    out = by_chunk(l, HD + 1)
                    dve.wait_ge(half[odd].o_ps, nth(t, l))
                    dve.reciprocal(rs, out[:, :, :, HD]).then_inc(half[odd].o_r, 1)
                    dve.wait_ge(half[odd].o_r, nth(t, l))
                    dve.tensor_tensor(heads_out[l][:, :, odd, :].rearrange("p (b j) e -> p b j e", b=2), out[:, :, :, 0:HD],
                                      rs.unsqueeze(3).broadcast_to([S, 2, 4, HD]), ALU.mult).then_inc(half[odd].o, 1)
                return step

            def residual(t, l):
                xb = m.x[:, bass.ds((t * LANES + l) * D, D)]
                dve.wait_ge(s.y_ps, nth(t, l))
                dve.scalar_tensor_tensor(xb, ps[l][:, 0, 0:D], m.tg[:, 0:1], xb, ALU.mult, ALU.add).then_inc(s.x, 1)

            staggered(dve, TURNS, LANES, [
                stats, normalise, rest, mean_square_k, rest,
                scale_k, rest, mean_square_q, rest, scale_q,
                rest, scale_kt, less_maximum(0), less_maximum(1), rest,
                divide(0), rest, divide(1), rest, residual])


@sublayer
def l0_ffn(nc, ctx, m, io):
    E, SE, F = 16, 64, 256
    NS = E * SE
    NC = NS // 128
    LANES = 4
    TURNS = B // LANES
    s = semaphores(nc, ctx, "f0", "w vecs se se_stats se_mv se_ve se_r se_n se_ps gs bs set stats mv var_eps rstd x1 "
                   "stats2 mv2 var_eps2 rstd2 x2 xg xs xst_ps xst lt_ps lt_max lt_sub lt_exp lt_sum lt_r dt d_ps d "
                   "sl_ps sl l_ps l_max l_neg c ct_ps ct gu_ps gelu h eo_ps eot eoe_ps eo y_ps yr yg x")

    def nth(turn, lane):
        return turn * LANES + lane + 1

    def nth_e(turn, e):
        return turn * E + e + 1

    with ExitStack() as mem:
        def sb(name, shape, dt=F32):
            return mem.enter_context(nc.sbuf_tensor("f0_" + name, shape, dt))

        wg, wu, wd = sb("wg", [D, E, F]), sb("wu", [D, E, F]), sb("wd", [128, E, 2, D])
        bg, bu, bd = sb("bg", [128, E, 2]), sb("bu", [128, E, 2]), sb("bd", [D, E])
        g_row, b_row = sb("g_row", [128, D]), sb("b_row", [128, D])
        slot_g, slot_b, scale = sb("slot_g", [D, 1]), sb("slot_b", [D, 1]), sb("scale", [D, 1])
        gs, bs = sb("gs", [D, 1]), sb("bs", [D, 1])
        set_ = sb("set", [D, NC, 128])
        se_stats, se_mv, se_ve, se_r = (sb("se_stats", [128, NC, 6]), sb("se_mv", [128, NC, 2]), sb("se_ve", [128, NC]),
                                        sb("se_r", [128, NC]))
        d_all = sb("d_all", [128, LANES, NS])
        t_all = sb("t_all", [128, LANES, NC, S])
        sl_all = sb("sl_all", [D, LANES, NS])
        hg = [sb(f"hg{k}", [128, 2, LANES * SE]) for k in range(2)]
        hh = [sb(f"hh{k}", [128, 2, LANES * SE]) for k in range(2)]
        se = d_all[:, 0, :].rearrange("p (c d) -> p c d", d=D)
        lane = [Names(
            stats=sb(f"stats{l}", [S, 6]), mv=sb(f"mv{l}", [S, 2]), var_eps=sb(f"var{l}", [S, 1]),
            rstd=sb(f"rstd{l}", [S, 1]), stats2=sb(f"stats2{l}", [S, 6]), mv2=sb(f"mv2{l}", [S, 2]),
            var_eps2=sb(f"var2{l}", [S, 1]), rstd2=sb(f"rstd2{l}", [S, 1]),
            x1=sb(f"x1{l}", [S, D]), xs=sb(f"xs{l}", [S, D]), xst=sb(f"xst{l}", [D, S]),
            mx=sb(f"mx{l}", [128, NC]), sum=sb(f"sum{l}", [128, NC]), r=sb(f"r{l}", [128, NC]),
            cmx=sb(f"cmx{l}", [S, 1]), neg=sb(f"neg{l}", [S, 1]), csum=sb(f"csum{l}", [S, 1]),
            cr=sb(f"cr{l}", [S, 1]), cg=sb(f"cg{l}", [S, 1]),
            t=t_all[:, l], d=d_all[:, l, :], sl=sl_all[:, l, :]) for l in range(LANES)]
        ps = [mem.enter_context(nc.psum_tensor(f"f0_ps{l}", [128, 2, 512], F32)) for l in range(LANES)]
        gate_ps = [ps[2 * k][:, 0, :].rearrange("p (c n) -> p c n", c=2) for k in range(2)]
        up_ps = [ps[2 * k][:, 1, :].rearrange("p (c n) -> p c n", c=2) for k in range(2)]
        eo_ps = [ps[2 * k + 1][:, 0, 0:LANES * SE] for k in range(2)]
        block = mem.enter_context(nc.Block())

        def flat(p):
            return p.rearrange("p b n -> p (b n)")

        @block.sync
        def _(sp):
            sp.dma_start(se, io.slot_embeds.rearrange("e s d -> (e s) d").rearrange("(c p) d -> p c d", p=128)
                         ).then_inc(s.se, 16)
            for dst, src in ((g_row[:], io.norm_g.partition_broadcast(128)), (b_row[:], io.norm_b.partition_broadcast(128)),
                             (slot_g[:], io.slot_g.unsqueeze(1)), (slot_b[:], io.slot_b.unsqueeze(1)),
                             (scale[:], io.scale.partition_broadcast(128))):
                sp.dma_start(dst, src).then_inc(s.vecs, 16)
            for dst, src in ((wg[:], io.Wg), (wu[:], io.Wu), (wd[:], io.Wd), (bg[:], io.bg), (bu[:], io.bu), (bd[:], io.bd)):
                sp.dma_start(dst, src).then_inc(s.w, 16)

        @block.tensor
        def _(pe):
            pe.wait_ge(s.se_n, NC)
            for c in range(NC):
                mm = pe.transpose(ps[0][:, c // 4, c % 4 * 128:c % 4 * 128 + 128], se[:, c, :], m.ident[:])
            mm.then_inc(s.se_ps, 1)
            pe.wait_ge(s.set, 1)
            pe.wait_ge(s.w, 96)
            with pe.Fori(0, TURNS) as t:
                for l in range(LANES):
                    pe.wait_ge(s.xs, nth(t, l))
                    pe.transpose(ps[l][:, 0, 0:S], lane[l].xs[:], m.ident[:]).then_inc(s.xst_ps, 1)
                for l in range(LANES):
                    pe.wait_ge(s.xst, nth(t, l))
                    for c in range(NC):
                        mm = pe.matmul(ps[l][:, c // 4, c % 4 * S:c % 4 * S + S], set_[:, c, :], lane[l].xst[:],
                                       start=True, stop=True)
                    mm.then_inc(s.lt_ps, 1)
                for l in range(LANES):
                    pe.wait_ge(s.dt, nth(t, l))
                    for c in range(NC):
                        mm = pe.transpose(ps[l][:, c // 4, c % 4 * 128:c % 4 * 128 + 128], lane[l].t[:, c, :], m.ident[:])
                    mm.then_inc(s.d_ps, 1)
                for l in range(LANES):
                    pe.wait_ge(s.d, nth(t, l))
                    for n in range(2):
                        mm = pe.matmul(ps[l][:, n, :], lane[l].xs[:], lane[l].d[:, 512 * n:512 * n + 512],
                                       start=True, stop=True)
                    mm.then_inc(s.sl_ps, 1)
                for l in range(LANES):
                    pe.wait_ge(s.sl, nth(t, l))
                    for n in range(2):
                        mm = pe.matmul(ps[l][:, n, :], lane[l].xst[:], set_[:, 4 * n:4 * n + 4, :], start=True, stop=True)
                    mm.then_inc(s.l_ps, 1)
                for l in range(LANES):
                    pe.wait_ge(s.c, nth(t, l))
                    for c in range(NC):
                        mm = pe.transpose(ps[l][:, c // 4, c % 4 * S:c % 4 * S + S], lane[l].d[:, 128 * c:128 * c + 128],
                                          m.ident[:])
                    mm.then_inc(s.ct_ps, 1)

                def gate_up(e):
                    k = e % 2
                    if e < 2:
                        pe.wait_ge(s.ct, nth(t, 2 * k + 1))
                    else:
                        pe.wait_ge(s.h, nth_e(t, e - 2))
                    rhs = sl_all[:, :, SE * e:SE * e + SE]
                    for w, out in ((wg, gate_ps[k]), (wu, up_ps[k])):
                        for c in range(2):
                            mm = pe.matmul(out[:, c, :], w[:, e, 128 * c:128 * c + 128], rhs, start=True, stop=True)
                    mm.then_inc(s.gu_ps, 1)

                def down(e):
                    k = e % 2
                    pe.wait_ge(s.h, nth_e(t, e))
                    if e >= 2:
                        pe.wait_ge(s.eot, nth_e(t, e - 2))
                    for c in range(2):
                        mm = pe.matmul(eo_ps[k], wd[:, e, c, :], hh[k][:, c, :], start=(c == 0), stop=(c == 1))
                    mm.then_inc(s.eo_ps, 1)

                gate_up(0)
                for e in range(E):
                    if e + 1 < E:
                        gate_up(e + 1)
                    down(e)
                pe.wait_ge(s.eot, nth_e(t, E - 1))
                for l in range(LANES):
                    for c in range(NC):
                        mm = pe.transpose(ps[l][:, c // 4, c % 4 * 128:c % 4 * 128 + 128],
                                          lane[l].sl[:, 128 * c:128 * c + 128], m.ident[:])
                    mm.then_inc(s.eoe_ps, 1)
                for l in range(LANES):
                    pe.wait_ge(s.eo, nth(t, l))
                    for c in range(NC):
                        mm = pe.matmul(ps[l][:, 0, 0:D], lane[l].t[:, c, :], lane[l].d[:, 128 * c:128 * c + 128],
                                       start=(c == 0), stop=(c == NC - 1))
                    mm.then_inc(s.y_ps, 1)

        @block.scalar
        def _(act):
            with act.Fori(0, TURNS) as t:
                for l in range(LANES):
                    act.wait_ge(s.xst_ps, nth(t, l))
                    act.copy(lane[l].xst[:], ps[l][:, 0, 0:S]).then_inc(s.xst, 1)
                for l in range(LANES):
                    act.wait_ge(s.lt_sub, nth(t, l))
                    act.activation(lane[l].t, lane[l].t, ACT.Exp).then_inc(s.lt_exp, 1)
                for l in range(LANES):
                    act.wait_ge(s.d_ps, nth(t, l))
                    act.copy(lane[l].d, flat(ps[l])).then_inc(s.d, 1)
                for l in range(LANES):
                    act.wait_ge(s.sl_ps, nth(t, l))
                    act.copy(lane[l].sl, flat(ps[l])).then_inc(s.sl, 1)
                for l in range(LANES):
                    act.wait_ge(s.l_neg, nth(t, l))
                    act.activation(lane[l].d, flat(ps[l]), ACT.Exp, bias=lane[l].neg[:], accum_out=lane[l].csum[:]
                                   ).then_inc(s.c, 1)
                for l in range(LANES):
                    act.wait_ge(s.ct_ps, nth(t, l))
                    act.copy(lane[l].t, ps[l][:].rearrange("p b (c n) -> p (b c) n", c=4)).then_inc(s.ct, 1)
                for e in range(E):
                    act.wait_ge(s.gu_ps, nth_e(t, e))
                    for c in range(2):
                        ge = act.activation(hg[e % 2][:, c, :], gate_ps[e % 2][:, c, :], ACT.Gelu, bias=bg[:, e, c:c + 1])
                    ge.then_inc(s.gelu, 1)
                for l in range(LANES):
                    act.wait_ge(s.eoe_ps, nth(t, l))
                    act.copy(lane[l].d, flat(ps[l])).then_inc(s.eo, 1)

        @block.gpsimd
        def _(pool):
            pool.wait_ge(s.se_ve, NC)
            inverse_root(pool, se_r[:], se_ve[:], m, s.se_r)
            with pool.Fori(0, TURNS) as t:
                for l in range(LANES):
                    pool.wait_ge(s.var_eps, nth(t, l))
                    inverse_root(pool, lane[l].rstd[:], lane[l].var_eps[:], m, s.rstd)
                for l in range(LANES):
                    pool.wait_ge(s.var_eps2, nth(t, l))
                    inverse_root(pool, lane[l].rstd2[:], lane[l].var_eps2[:], m, s.rstd2)

        @block.vector
        def _(dve):
            dve.wait_ge(s.se, 16)
            for c in range(NC):
                dve.bn_stats(se_stats[:, c, :], se[:, c, :]).then_inc(s.se_stats, 1)
            for c in range(NC):
                dve.wait_ge(s.se_stats, c + 1)
                dve.bn_aggr(se_mv[:, c, :], se_stats[:, c, :]).then_inc(s.se_mv, 1)
            for c in range(NC):
                dve.wait_ge(s.se_mv, c + 1)
                dve.tensor_scalar(se_ve[:, c:c + 1], se_mv[:, c, 1:2], LN_EPS, None, ALU.add).then_inc(s.se_ve, 1)
            dve.wait_ge(s.vecs, 80)
            dve.tensor_tensor(gs[:], slot_g[:], scale[:], ALU.mult).then_inc(s.gs, 1)
            dve.tensor_tensor(bs[:], slot_b[:], scale[:], ALU.mult).then_inc(s.bs, 1)
            dve.wait_ge(s.se_r, 1)
            for c in range(NC):
                dve.tensor_scalar(se[:, c, :], se[:, c, :], se_mv[:, c, 0:1], se_r[:, c:c + 1], ALU.subtract, ALU.mult
                                  ).then_inc(s.se_n, 1)
            dve.wait_ge(s.se_ps, 1)
            dve.wait_ge(s.gs, 1)
            dve.wait_ge(s.bs, 1)
            dve.tensor_scalar(set_[:].rearrange("p c n -> p (c n)"), flat(ps[0]), gs[:], bs[:], ALU.mult, ALU.add
                              ).then_inc(s.set, 1)
            with dve.Fori(0, TURNS) as t:
                layer_norm_stats(dve, m, s, t, lane)
                for l in range(LANES):
                    dve.wait_ge(s.rstd, nth(t, l))
                    dve.tensor_scalar(lane[l].x1[:], m.x[:, bass.ds((t * LANES + l) * D, D)], lane[l].mv[:, 0:1],
                                      lane[l].rstd[:], ALU.subtract, ALU.mult).then_inc(s.x1, 1)
                for l in range(LANES):
                    dve.wait_ge(s.x1, nth(t, l))
                    dve.bn_stats(lane[l].stats2[:], lane[l].x1[:]).then_inc(s.stats2, 1)
                dve.wait_ge(s.stats2, nth(t, LANES - 1))
                dve.memset(m.wait_pad[:], 0.0)
                for l in range(LANES):
                    dve.bn_aggr(lane[l].mv2[:], lane[l].stats2[:]).then_inc(s.mv2, 1)
                for l in range(LANES):
                    dve.wait_ge(s.mv2, nth(t, l))
                    dve.tensor_scalar(lane[l].var_eps2[:], lane[l].mv2[:, 1:2], LN_EPS, None, ALU.add).then_inc(s.var_eps2, 1)
                for l in range(LANES):
                    dve.wait_ge(s.rstd2, nth(t, l))
                    dve.tensor_scalar(lane[l].x1[:], lane[l].x1[:], lane[l].mv2[:, 0:1], lane[l].rstd2[:],
                                      ALU.subtract, ALU.mult).then_inc(s.x2, 1)
                for l in range(LANES):
                    dve.wait_ge(s.x2, nth(t, l))
                    dve.tensor_tensor(lane[l].x1[:], lane[l].x1[:], g_row[:], ALU.mult).then_inc(s.xg, 1)
                for l in range(LANES):
                    dve.wait_ge(s.xg, nth(t, l))
                    dve.tensor_tensor(lane[l].xs[:], lane[l].x1[:], b_row[:], ALU.add).then_inc(s.xs, 1)
                for l in range(LANES):
                    logits = ps[l][:].rearrange("p b (c n) -> p (b c) n", c=4)
                    dve.wait_ge(s.lt_ps, nth(t, l))
                    dve.tensor_reduce(lane[l].mx[:], logits, AX.X, ALU.max).then_inc(s.lt_max, 1)
                    dve.wait_ge(s.lt_max, nth(t, l))
                    dve.tensor_tensor(lane[l].t, logits, bcast(lane[l].mx[:], S), ALU.subtract).then_inc(s.lt_sub, 1)
                for l in range(LANES):
                    dve.wait_ge(s.lt_exp, nth(t, l))
                    dve.tensor_reduce(lane[l].sum[:], lane[l].t, AX.X, ALU.add).then_inc(s.lt_sum, 1)
                    dve.wait_ge(s.lt_sum, nth(t, l))
                    dve.reciprocal(lane[l].r[:], lane[l].sum[:]).then_inc(s.lt_r, 1)
                    dve.wait_ge(s.lt_r, nth(t, l))
                    dve.tensor_tensor(lane[l].t, lane[l].t, bcast(lane[l].r[:], S), ALU.mult).then_inc(s.dt, 1)
                for l in range(LANES):
                    dve.wait_ge(s.l_ps, nth(t, l))
                    dve.tensor_reduce(lane[l].cmx[:], ps[l][:], AX.XY, ALU.max).then_inc(s.l_max, 1)
                    dve.wait_ge(s.l_max, nth(t, l))
                    dve.tensor_scalar(lane[l].neg[:], lane[l].cmx[:], -1.0, None, ALU.mult).then_inc(s.l_neg, 1)

                def hidden(e):
                    k = e % 2
                    dve.wait_ge(s.gelu, nth_e(t, e))
                    if e >= 2:
                        dve.wait_ge(s.eo_ps, nth_e(t, e - 2))
                    for c in range(2):
                        mul = dve.scalar_tensor_tensor(hh[k][:, c, :], up_ps[k][:, c, :], bu[:, e, c:c + 1],
                                                       hg[k][:, c, :], ALU.add, ALU.mult)
                    mul.then_inc(s.h, 1)

                def outputs(e):
                    k = e % 2
                    dve.wait_ge(s.eo_ps, nth_e(t, e))
                    dve.tensor_scalar(sl_all[:, :, SE * e:SE * e + SE], eo_ps[k].rearrange("p (b n) -> p b n", n=SE),
                                      bd[:, e:e + 1], None, ALU.add).then_inc(s.eot, 1)

                hidden(0)
                for e in range(E):
                    if e + 1 < E:
                        hidden(e + 1)
                    outputs(e)
                for l in range(LANES):
                    dve.wait_ge(s.c, nth(t, l))
                    dve.reciprocal(lane[l].cr[:], lane[l].csum[:]).then_inc(s.yr, 1)
                for l in range(LANES):
                    dve.wait_ge(s.yr, nth(t, l))
                    dve.tensor_tensor(lane[l].cg[:], lane[l].cr[:], m.tg[:, 4:5], ALU.mult).then_inc(s.yg, 1)
                for l in range(LANES):
                    xb = m.x[:, bass.ds((t * LANES + l) * D, D)]
                    dve.wait_ge(s.yg, nth(t, l))
                    dve.wait_ge(s.y_ps, nth(t, l))
                    dve.scalar_tensor_tensor(xb, ps[l][:, 0, 0:D], lane[l].cg[:], xb, ALU.mult, ALU.add).then_inc(s.x, 1)
                dve.wait_ge(s.x, nth(t, LANES - 1))


@sublayer
def l1_attention(nc, ctx, m, io):
    LANES = 4
    TURNS = B // LANES
    SCALE = D ** -0.5
    s = semaphores(nc, ctx, "a1", "stats mv var_eps rstd xn xt_ps xt qkv_ps qk v s_ps s_max neg p pt_ps pt "
                   "o_ps r g x c0 c1 c2 c3")
    c_in = [s.c0, s.c1, s.c2, s.c3]

    def nth(turn, lane):
        return turn * LANES + lane + 1

    with ExitStack() as mem:
        def sb(name, shape, dt=F32):
            return mem.enter_context(nc.sbuf_tensor("a1_" + name, shape, dt))

        lane = [Names(
            stats=sb(f"stats{l}", [S, 6]), mv=sb(f"mv{l}", [S, 2]), var_eps=sb(f"var{l}", [S, 1]),
            rstd=sb(f"rstd{l}", [S, 1]), xn=sb(f"xn{l}", [S, D]), xt=sb(f"xt{l}", [D, S]),
            c=sb(f"c{l}", [SC, D]), ct=sb(f"ct{l}", [D, SC]), qt=sb(f"qt{l}", [D, S]), kt=sb(f"kt{l}", [D, SC]),
            v=sb(f"v{l}", [SC, D]), mx=sb(f"mx{l}", [S, 1]), neg=sb(f"neg{l}", [S, 1]), p=sb(f"p{l}", [S, SC]),
            sum=sb(f"sum{l}", [S, 1]), r=sb(f"r{l}", [S, 1]), g=sb(f"g{l}", [S, 1]), pt=sb(f"pt{l}", [SC, S]))
            for l in range(LANES)]
        ps = [mem.enter_context(nc.psum_tensor(f"a1_ps{l}", [128, 2, 512], F32)) for l in range(LANES)]
        block = mem.enter_context(nc.Block())

        @block.sync
        def _(sp):
            if m.prefetch_a1:
                m.prefetch_a1(sp)
            load_context(sp, io, s, lane, c_in, TURNS)

        @block.tensor
        def _(pe):
            with pe.Fori(0, TURNS) as t:
                for l in range(LANES):
                    pe.wait_ge(s.xn, nth(t, l))
                    pe.wait_ge(c_in[l], 16 * t + 16)
                    pe.transpose(ps[l][:, 0, 0:S], lane[l].xn[:], m.ident[:])
                    pe.transpose(ps[l][:, 0, S:S + SC], lane[l].c[:], m.ident[0:SC, 0:SC]).then_inc(s.xt_ps, 1)
                for l in range(LANES):
                    pe.wait_ge(s.xt, nth(t, l))
                    pe.matmul(ps[l][:, 1, 0:S], m.wq1[:], lane[l].xt[:], start=True, stop=True)
                    pe.matmul(ps[l][:, 1, S:S + SC], m.wk1[:], lane[l].ct[:], start=True, stop=True)
                    pe.matmul(ps[l][0:SC, 1, 256:256 + D], lane[l].ct[:], m.wv1[:], start=True, stop=False)
                    pe.matmul(ps[l][0:SC, 1, 256:256 + D], m.ones_row[:, 0:SC], m.rows[0:1, m.row_bv1, :],
                              start=False, stop=True).then_inc(s.qkv_ps, 1)
                for l in range(LANES):
                    pe.wait_ge(s.qk, nth(t, l))
                    pe.matmul(ps[l][:, 0, 0:SC], lane[l].qt[:], lane[l].kt[:], start=True, stop=True
                              ).then_inc(s.s_ps, 1)
                for l in range(LANES):
                    pe.wait_ge(s.v, nth(t, l))
                    pe.wait_ge(s.p, nth(t, l))
                    pe.transpose(ps[l][0:SC, 1, 0:S], lane[l].p[:], m.ident[:]).then_inc(s.pt_ps, 1)
                for l in range(LANES):
                    pe.wait_ge(s.pt, nth(t, l))
                    pe.matmul(ps[l][:, 0, 0:D], lane[l].pt[:], lane[l].v[:], start=True, stop=True).then_inc(s.o_ps, 1)

        @block.scalar
        def _(act):
            with act.Fori(0, TURNS) as t:
                for l in range(LANES):
                    act.wait_ge(s.xt_ps, nth(t, l))
                    act.copy(lane[l].xt[:], ps[l][:, 0, 0:S])
                    act.copy(lane[l].ct[:], ps[l][:, 0, S:S + SC]).then_inc(s.xt, 1)
                for l in range(LANES):
                    act.wait_ge(s.qkv_ps, nth(t, l))
                    act.activation(lane[l].qt[:], ps[l][:, 1, 0:S], ACT.Identity, bias=m.bqk1[:, 0:1])
                    act.activation(lane[l].kt[:], ps[l][:, 1, S:S + SC], ACT.Identity, bias=m.bqk1[:, 1:2]
                                   ).then_inc(s.qk, 1)
                for l in range(LANES):
                    act.wait_ge(s.neg, nth(t, l))
                    act.activation(lane[l].p[:], ps[l][:, 0, 0:SC], ACT.Exp, bias=lane[l].neg[:], scale=SCALE,
                                   accum_out=lane[l].sum[:]).then_inc(s.p, 1)
                for l in range(LANES):
                    act.wait_ge(s.pt_ps, nth(t, l))
                    act.copy(lane[l].pt[:], ps[l][0:SC, 1, 0:S]).then_inc(s.pt, 1)

        @block.gpsimd
        def _(pool):
            with pool.Fori(0, TURNS) as t:
                for l in range(LANES):
                    pool.wait_ge(s.var_eps, nth(t, l))
                    inverse_root(pool, lane[l].rstd[:], lane[l].var_eps[:], m, s.rstd)

        @block.vector
        def _(dve):
            with dve.Fori(0, TURNS) as t:
                layer_norm_stats(dve, m, s, t, lane)
                for l in range(LANES):
                    dve.wait_ge(s.rstd, nth(t, l))
                    dve.tensor_scalar(lane[l].xn[:], m.x[:, bass.ds((t * LANES + l) * D, D)], lane[l].mv[:, 0:1],
                                      lane[l].rstd[:], ALU.subtract, ALU.mult).then_inc(s.xn, 1)
                for l in range(LANES):
                    dve.wait_ge(s.qk, nth(t, l))
                    dve.tensor_copy(lane[l].v[:], ps[l][0:SC, 1, 256:256 + D]).then_inc(s.v, 1)
                for l in range(LANES):
                    dve.wait_ge(s.s_ps, nth(t, l))
                    dve.reduce_max(lane[l].mx[:], ps[l][:, 0, 0:SC], AX.X).then_inc(s.s_max, 1)
                for l in range(LANES):
                    dve.wait_ge(s.s_max, nth(t, l))
                    dve.tensor_scalar(lane[l].neg[:], lane[l].mx[:], -SCALE, None, ALU.mult).then_inc(s.neg, 1)
                for l in range(LANES):
                    dve.wait_ge(s.p, nth(t, l))
                    dve.reciprocal(lane[l].r[:], lane[l].sum[:]).then_inc(s.r, 1)
                for l in range(LANES):
                    dve.wait_ge(s.r, nth(t, l))
                    dve.tensor_tensor(lane[l].g[:], lane[l].r[:], m.tg[:, 1:2], ALU.mult).then_inc(s.g, 1)
                for l in range(LANES):
                    xb = m.x[:, bass.ds((t * LANES + l) * D, D)]
                    dve.wait_ge(s.g, nth(t, l))
                    dve.wait_ge(s.o_ps, nth(t, l))
                    dve.scalar_tensor_tensor(xb, ps[l][:, 0, 0:D], lane[l].g[:], xb, ALU.mult, ALU.add
                                             ).then_inc(s.x, 1)
                dve.wait_ge(s.x, nth(t, LANES - 1))


@sublayer
def routed_ffn(nc, ctx, m, io, kind):
    top2 = kind == "top2"
    tag = "f1" if top2 else "f3"
    E = 8
    FC = 2 if top2 else 4
    CAP = B * S // E
    LANES = 4
    TURNS = B // LANES
    GATE = 5 if top2 else 7
    s = semaphores(nc, ctx, tag, "w stats mv var_eps rstd xn xt_ps xt r_ps r top idx sub exp den rden onehot oh2 cnt_ps kept "
                   "wt wt1 total up_ps up h y_ps acc x iota tri one")

    def nth(turn, lane):
        return turn * LANES + lane + 1

    def nth_c(turn, e, c):
        return turn * (E * FC) + e * FC + c + 1

    def nth_e(turn, e):
        return turn * E + e + 1

    with ExitStack() as mem:
        def sb(name, shape, dt=F32):
            return mem.enter_context(nc.sbuf_tensor(f"{tag}_" + name, shape, dt))

        wr = sb("wr", [D, E])
        if top2:
            w1, w2, w3 = sb("w1", [D, E, FC, 128]), sb("w2", [D, E, FC, 128]), sb("w3", [128, E, FC, D])
        else:
            w1, w3 = sb("w1", [D, E, FC, 128]), sb("w3", [128, E, FC, D])
            b1, b2 = sb("b1", [128, E, FC]), sb("b2", [1, E, D])
            total = sb("total", [S, E])
            tri = sb("tri", [S, S])
            ones = sb("ones", [S, S])
        experts = sb("experts", [S, E])
        xt = sb("xt", [D, LANES, S])
        NH = 2 * FC
        act1 = [sb(f"act{k}", [128, LANES * S]) for k in range(NH if not top2 else 2)]
        hid = [sb(f"hid{k}", [128, LANES * S]) for k in range(NH)] if top2 else act1
        acc = sb("acc", [S, LANES, D])
        lane = [Names(
            stats=sb(f"stats{l}", [S, 6]), mv=sb(f"mv{l}", [S, 2]), var_eps=sb(f"var{l}", [S, 1]),
            rstd=sb(f"rstd{l}", [S, 1]), xn=sb(f"xn{l}", [S, D]), r=sb(f"r{l}", [S, E]), top=sb(f"top{l}", [S, 8]),
            idx=sb(f"idx{l}", [S, 8], U32), idxf=sb(f"idxf{l}", [S, 8]), sub=sb(f"sub{l}", [S, E]),
            exp=sb(f"exp{l}", [S, E]), den=sb(f"den{l}", [S, 1]), rden=sb(f"rden{l}", [S, 1]),
            oh=sb(f"oh{l}", [S, E]), oh2=sb(f"oh2{l}", [S, E]), wt=sb(f"wt{l}", [S, E])) for l in range(LANES)]
        misc = mem.enter_context(nc.psum_tensor(f"{tag}_misc", [128, 2, 512], F32))
        up = mem.enter_context(nc.psum_tensor(f"{tag}_up", [128, 4, 512], F32))
        yps = mem.enter_context(nc.psum_tensor(f"{tag}_y", [128, 2, 512], F32))
        block = mem.enter_context(nc.Block())

        @block.sync
        def _(sp):
            loads = [(wr[:], io.router), (w1[:], io.w1), (w3[:], io.w3)]
            loads += [(w2[:], io.w2)] if top2 else [(b1[:], io.b1), (b2[:], io.b2.rearrange("e d -> (e d)").unsqueeze(0).rearrange("a (e d) -> a e d", e=E))]
            for dst, src in loads:
                sp.dma_start(dst, src).then_inc(s.w, 16)

        @block.tensor
        def _(pe):
            pe.wait_ge(s.w, 64 if top2 else 80)
            if not top2:
                pe.wait_ge(s.tri, 1)
            with pe.Fori(0, TURNS) as t:
                for l in range(LANES):
                    pe.wait_ge(s.xn, nth(t, l))
                    pe.transpose(misc[:, 0, S * l:S * l + S], lane[l].xn[:], m.ident[:]).then_inc(s.xt_ps, 1)
                for l in range(LANES):
                    pe.wait_ge(s.xt, t + 1)
                    pe.matmul(misc[:, 1, E * l:E * l + E], xt[:, l, :], wr[:], start=True, stop=True).then_inc(s.r_ps, 1)

                def first(e, c):
                    n = e * FC + c
                    if top2:
                        k = n % 2
                        if n >= 2:
                            pe.wait_ge(s.h, nth_c(t, e, c) - 2)
                        pe.matmul(up[:, 2 * k, :], w1[:, e, c, :], xt[:], start=True, stop=True)
                        pe.matmul(up[:, 2 * k + 1, :], w2[:, e, c, :], xt[:], start=True, stop=True).then_inc(s.up_ps, 1)
                    else:
                        k = n % 4
                        if n >= 4:
                            pe.wait_ge(s.h, nth_c(t, e, c) - 4)
                        pe.matmul(up[:, k, :], w1[:, e, c, :], xt[:], start=True, stop=True).then_inc(s.up_ps, 1)

                def second(e):
                    pe.wait_ge(s.h, nth_c(t, e, FC - 1))
                    if e >= 2:
                        pe.wait_ge(s.acc, nth_e(t, e - 2))
                    for l in range(LANES):
                        for c in range(FC):
                            mm = pe.matmul(yps[:, e % 2, D * l:D * l + D], hid[(e * FC + c) % NH][:, S * l:S * l + S],
                                           w3[:, e, c, :], start=(c == 0), stop=(top2 and c == FC - 1))
                        if not top2:
                            mm = pe.matmul(yps[:, e % 2, D * l:D * l + D], m.ones_row[:], b2[0:1, e, :],
                                           start=False, stop=True)
                    mm.then_inc(s.y_ps, 1)

                for c in range(FC):
                    first(0, c)
                    if not top2:
                        pe.wait_ge(s.onehot, nth(t, c))
                        pe.wait_ge(s.total, nth(t, c))
                        if c:
                            pe.wait_ge(s.kept, nth(t, c - 1))
                        place = misc[:, 1, 64 + E * c:64 + E * c + E]
                        pe.matmul(place, tri[:], lane[c].oh[:], start=True, stop=False)
                        pe.matmul(place, ones[:], total[:], start=False, stop=True).then_inc(s.cnt_ps, 1)
                for e in range(E):
                    if e + 1 < E:
                        for c in range(FC):
                            first(e + 1, c)
                    second(e)

        @block.scalar
        def _(act):
            with act.Fori(0, TURNS) as t:
                act.wait_ge(s.xt_ps, nth(t, LANES - 1))
                act.copy(xt[:], misc[:, 0, :].rearrange("p (l n) -> p l n", n=S)).then_inc(s.xt, 1)
                if not top2:
                    for l in range(LANES):
                        act.wait_ge(s.sub, nth(t, l))
                        act.activation(lane[l].exp[:], lane[l].sub[:], ACT.Exp, accum_out=lane[l].den[:]).then_inc(s.exp, 1)
                else:
                    for l in range(LANES):
                        act.wait_ge(s.sub, nth(t, l))
                        act.activation(lane[l].exp[:, 0:1], lane[l].sub[:, 0:1], ACT.Sigmoid).then_inc(s.exp, 1)
                for n in range(E * FC):
                    e, c = n // FC, n % FC
                    act.wait_ge(s.up_ps, nth_c(t, e, c))
                    if top2:
                        if n >= 2:
                            act.wait_ge(s.h, nth_c(t, e, c) - 2)
                        act.activation(act1[n % 2][:], up[:, 2 * (n % 2), :], ACT.Silu).then_inc(s.up, 1)
                    else:
                        if e >= 2:
                            act.wait_ge(s.y_ps, nth_e(t, e - 2))
                        act.activation(act1[n % NH][:], up[:, n % 4, :], ACT.Relu, bias=b1[:, e, c:c + 1]).then_inc(s.h, 1)

        @block.gpsimd
        def _(pool):
            pool.iota(experts[:], [[1, E]], base=0, channel_multiplier=0, allow_small_or_imprecise_dtypes=True
                      ).then_inc(s.iota, 1)
            if not top2:
                pool.memset(ones[:], 1.0).then_inc(s.one, 1)
                pool.wait_ge(s.one, 1)
                pool.affine_select(tri[:], ones[:], [[1, S]], ALU.is_ge, 0.0, 0, -1).then_inc(s.tri, 1)
            with pool.Fori(0, TURNS) as t:
                for l in range(LANES):
                    pool.wait_ge(s.var_eps, nth(t, l))
                    inverse_root(pool, lane[l].rstd[:], lane[l].var_eps[:], m, s.rstd)

        @block.vector
        def _(dve):
            dve.wait_ge(s.iota, 1)
            if not top2:
                dve.memset(total[:], 0.0).then_inc(s.total, 1)
            with dve.Fori(0, TURNS) as t:
                layer_norm_stats(dve, m, s, t, lane)
                for l in range(LANES):
                    dve.wait_ge(s.rstd, nth(t, l))
                    dve.tensor_scalar(lane[l].xn[:], m.x[:, bass.ds((t * LANES + l) * D, D)], lane[l].mv[:, 0:1],
                                      lane[l].rstd[:], ALU.subtract, ALU.mult).then_inc(s.xn, 1)
                for l in range(LANES):
                    dve.wait_ge(s.r_ps, nth(t, LANES - 1))
                    dve.tensor_copy(lane[l].r[:], misc[:, 1, E * l:E * l + E]).then_inc(s.r, 1)
                dve.wait_ge(s.r, nth(t, LANES - 1))
                dve.memset(m.wait_pad[:], 0.0)
                for l in range(LANES):
                    dve.max(lane[l].top[:], lane[l].r[:]).then_inc(s.top, 1)
                dve.wait_ge(s.top, nth(t, LANES - 1))
                dve.memset(m.wait_pad[:], 0.0)
                for l in range(LANES):
                    dve.max_index(lane[l].idx[:], lane[l].top[:], lane[l].r[:]).then_inc(s.idx, 1)
                for l in range(LANES):
                    if top2:
                        dve.tensor_scalar(lane[l].sub[:, 0:1], lane[l].top[:, 0:1], lane[l].top[:, 1:2], None,
                                          ALU.subtract).then_inc(s.sub, 1)
                    else:
                        dve.tensor_scalar(lane[l].sub[:], lane[l].r[:], lane[l].top[:, 0:1], None, ALU.subtract
                                          ).then_inc(s.sub, 1)
                for l in range(LANES):
                    dve.wait_ge(s.idx, nth(t, l))
                    dve.tensor_copy(lane[l].idxf[:], lane[l].idx[:]).then_inc(s.oh2, 1)
                for l in range(LANES):
                    dve.wait_ge(s.oh2, nth(t, l))
                    dve.tensor_scalar(lane[l].oh[:], experts[:], lane[l].idxf[:, 0:1], None, ALU.is_equal
                                      ).then_inc(s.onehot, 1)
                if top2:
                    for l in range(LANES):
                        dve.wait_ge(s.exp, nth(t, l))
                        dve.tensor_scalar(lane[l].exp[:, 1:2], lane[l].exp[:, 0:1], -1.0, 1.0, ALU.mult, ALU.add
                                          ).then_inc(s.den, 1)
                    for l in range(LANES):
                        dve.wait_ge(s.den, nth(t, l))
                        dve.tensor_scalar(lane[l].oh2[:], experts[:], lane[l].idxf[:, 1:2], lane[l].exp[:, 1:2],
                                          ALU.is_equal, ALU.mult).then_inc(s.wt1, 1)
                    for l in range(LANES):
                        dve.wait_ge(s.onehot, nth(t, l))
                        dve.wait_ge(s.wt1, nth(t, l))
                        dve.scalar_tensor_tensor(lane[l].wt[:], lane[l].oh[:], lane[l].exp[:, 0:1], lane[l].oh2[:],
                                                 ALU.mult, ALU.add).then_inc(s.wt, 1)
                else:
                    for l in range(LANES):
                        dve.wait_ge(s.exp, nth(t, l))
                        dve.reciprocal(lane[l].rden[:], lane[l].den[:]).then_inc(s.rden, 1)
                    for l in range(LANES):
                        dve.wait_ge(s.cnt_ps, nth(t, l))
                        dve.wait_ge(s.onehot, nth(t, l))
                        dve.tensor_tensor(total[:], total[:], lane[l].oh[:], ALU.add).then_inc(s.total, 1)
                        dve.scalar_tensor_tensor(lane[l].oh2[:], misc[:, 1, 64 + E * l:64 + E * l + E], float(CAP),
                                                 lane[l].oh[:], ALU.is_le, ALU.mult).then_inc(s.kept, 1)
                    for l in range(LANES):
                        dve.wait_ge(s.rden, nth(t, l))
                        dve.wait_ge(s.kept, nth(t, l))
                        dve.tensor_scalar(lane[l].wt[:], lane[l].oh2[:], lane[l].rden[:], None, ALU.mult).then_inc(s.wt, 1)

                def product(n):
                    e, c = n // FC, n % FC
                    dve.wait_ge(s.up, nth_c(t, e, c))
                    if e >= 2:
                        dve.wait_ge(s.y_ps, nth_e(t, e - 2))
                    dve.tensor_tensor(hid[n % NH][:], act1[n % 2][:], up[:, 2 * (n % 2) + 1, :], ALU.mult).then_inc(s.h, 1)

                def add(e):
                    dve.wait_ge(s.y_ps, nth_e(t, e))
                    if e == 0:
                        dve.wait_ge(s.wt, nth(t, LANES - 1))
                    else:
                        dve.wait_ge(s.acc, nth_e(t, e - 1))
                    for l in range(LANES):
                        y = yps[:, e % 2, D * l:D * l + D]
                        if e == 0:
                            a = dve.tensor_scalar(acc[:, l, :], y, lane[l].wt[:, 0:1], None, ALU.mult)
                        else:
                            a = dve.scalar_tensor_tensor(acc[:, l, :], y, lane[l].wt[:, e:e + 1], acc[:, l, :],
                                                         ALU.mult, ALU.add)
                    a.then_inc(s.acc, 1)

                for e in range(E):
                    if top2:
                        for c in range(FC):
                            product(e * FC + c)
                    if e:
                        add(e - 1)
                add(E - 1)
                dve.wait_ge(s.acc, nth_e(t, E - 1))
                xg = m.x[:, bass.ds(t * (LANES * D), LANES * D)]
                dve.scalar_tensor_tensor(xg, acc[:].rearrange("p l d -> p (l d)"), m.tg[:, GATE:GATE + 1], xg,
                                         ALU.mult, ALU.add).then_inc(s.x, 1)
                dve.wait_ge(s.x, t + 1)


@sublayer
def l2_attention(nc, ctx, m, io):
    H, HD = 16, 8
    SK = SC + S
    LANES = 2
    TURNS = B // LANES
    s = semaphores(nc, ctx, "a2", "stats mv var_eps rstd xn xt_ps xt q_ps qm kt v_ps v s_ps s_max s_sub p pta_ps "
                   "pta ptb_ps ptb o_ps o_r o at_ps at y_ps x c0 c1 ones")
    c_in = [s.c0, s.c1]

    def nth(turn, lane):
        return turn * LANES + lane + 1

    def head_of(i):
        half, quad, jj = i // 8, i // 2 % 4, i % 2
        return 4 * quad + 2 * half + jj

    def nth_half(turn, lane, half):
        return turn * (2 * LANES) + half * LANES + lane + 1

    with ExitStack() as mem:
        def sb(name, shape, dt=F32):
            return mem.enter_context(nc.sbuf_tensor("a2_" + name, shape, dt))

        lane = [Names(
            stats=sb(f"stats{l}", [S, 6]), mv=sb(f"mv{l}", [S, 2]), var_eps=sb(f"var{l}", [S, 1]),
            rstd=sb(f"rstd{l}", [S, 1]), xn=sb(f"xn{l}", [S, D]), xct=sb(f"xct{l}", [D, SK]),
            c=sb(f"c{l}", [SC, D]), qm=sb(f"qm{l}", [D, 4, S]), kt=sb(f"kt{l}", [D, SK]),
            vc=sb(f"vc{l}", [SC, H, HD + 1]), vx=sb(f"vx{l}", [S, H, HD + 1]),
            mx=sb(f"mx{l}", [S, H]), p=sb(f"p{l}", [S, H, SK]),
            ptc=sb(f"ptc{l}", [SC, H, S]), ptx=sb(f"ptx{l}", [S, H, S]),
            rs=sb(f"rs{l}", [S, H]), o=sb(f"o{l}", [S, D]), ot=sb(f"ot{l}", [D, S])) for l in range(LANES)]
        ps = [mem.enter_context(nc.psum_tensor(f"a2_ps{l}", [128, 4, 512], F32)) for l in range(LANES)]
        block = mem.enter_context(nc.Block())

        @block.sync
        def _(sp):
            if m.prefetch_a2:
                m.prefetch_a2(sp)
            load_context(sp, io, s, lane, c_in, TURNS)

        @block.tensor
        def _(pe):
            with pe.Fori(0, TURNS) as t:
                for l in range(LANES):
                    pe.wait_ge(s.xn, nth(t, l))
                    pe.wait_ge(c_in[l], 16 * t + 16)
                    pe.transpose(ps[l][:, 0, 0:SC], lane[l].c[:], m.ident[0:SC, 0:SC])
                    pe.transpose(ps[l][:, 0, SC:SK], lane[l].xn[:], m.ident[:]).then_inc(s.xt_ps, 1)
                for l in range(LANES):
                    pe.wait_ge(s.xt, nth(t, l))
                    pe.matmul(ps[l][:, 1, 0:S], m.wq2[:], lane[l].xct[:, SC:SK], start=True, stop=True
                              ).then_inc(s.q_ps, 1)
                    pe.matmul(ps[l][:, 2, 0:SK], m.wkv2[:, 0:D], lane[l].xct[:], start=True, stop=True)
                    pe.matmul(ps[l][0:SC, 3, 0:D], lane[l].xct[:, 0:SC], m.wkv2[:, D:2 * D], start=True, stop=True)
                    pe.matmul(ps[l][:, 3, D:2 * D], lane[l].xct[:, SC:SK], m.wkv2[:, D:2 * D], start=True, stop=True
                              ).then_inc(s.v_ps, 1)
                for half in range(2):
                    for l in range(LANES):
                        if half == 0:
                            pe.wait_ge(s.qm, nth(t, l))
                            pe.wait_ge(s.v, nth(t, l))
                        else:
                            pe.wait_ge(s.s_sub, nth_half(t, l, 0))
                        for quad in range(4):
                            pe.matmul(ps[l][:, quad, :].rearrange("p (j n) -> p j n", n=256)[:, :, 0:SK], m.identb[:],
                                      m.causal[:].unsqueeze(1).broadcast_to([S, 2, SK]), start=True, stop=False)
                        for jj in range(2):
                            for quad in range(4):
                                row = slice(32 * quad, 32 * quad + 32)
                                mm = pe.matmul(ps[l][:, quad, 256 * jj:256 * jj + SK], lane[l].qm[row, 2 * half + jj, :],
                                               lane[l].kt[row, :], start=False, stop=(jj == 1))
                        mm.then_inc(s.s_ps, 1)
                for half in range(2):
                    for l in range(LANES):
                        if half == 0:
                            pe.wait_ge(s.p, nth_half(t, l, 1))
                        else:
                            pe.wait_ge(s.pta, nth_half(t, l, 0))
                            pe.wait_ge(s.ptb, nth_half(t, l, 0))
                        for i in range(H):
                            if half == 0:
                                mm = pe.transpose(ps[l][0:SC, i // 4, i % 4 * S:i % 4 * S + S], lane[l].p[:, i, 0:SC],
                                                  m.ident[:])
                            else:
                                mm = pe.transpose(ps[l][:, i // 4, i % 4 * S:i % 4 * S + S], lane[l].p[:, i, SC:SK],
                                                  m.ident[:])
                            if i == H // 2 - 1:
                                mm.then_inc(s.pta_ps, 1)
                        mm.then_inc(s.ptb_ps, 1)
                for l in range(LANES):
                    pe.wait_ge(s.pta, nth_half(t, l, 1))
                    pe.wait_ge(s.ptb, nth_half(t, l, 1))
                    for i in range(H):
                        h = head_of(i)
                        out = ps[l][:, 0, (HD + 1) * h:(HD + 1) * h + HD + 1]
                        pe.matmul(out, lane[l].ptc[:, i, :], lane[l].vc[:, h, :], start=True, stop=False)
                        mm = pe.matmul(out, lane[l].ptx[:, i, :], lane[l].vx[:, h, :], start=False, stop=True)
                    mm.then_inc(s.o_ps, 1)
                for l in range(LANES):
                    pe.wait_ge(s.o, nth(t, l))
                    pe.transpose(ps[l][:, 1, 0:S], lane[l].o[:], m.ident[:]).then_inc(s.at_ps, 1)
                for l in range(LANES):
                    pe.wait_ge(s.at, nth(t, l))
                    pe.matmul(ps[l][:, 2, 0:D], lane[l].ot[:], m.wout2[:], start=True, stop=False)
                    pe.matmul(ps[l][:, 2, 0:D], m.ones_row[:], m.rows[0:1, m.row_bout2, :], start=False, stop=True
                              ).then_inc(s.y_ps, 1)

        @block.scalar
        def _(act):
            with act.Fori(0, TURNS) as t:
                for l in range(LANES):
                    act.wait_ge(s.xt_ps, nth(t, l))
                    act.copy(lane[l].xct[:], ps[l][:, 0, 0:SK]).then_inc(s.xt, 1)
                for l in range(LANES):
                    act.wait_ge(s.v_ps, nth(t, l))
                    act.copy(lane[l].kt[:], ps[l][:, 2, 0:SK])
                    act.copy(lane[l].vc[:, :, 0:HD], ps[l][0:SC, 3, 0:D].rearrange("p (h e) -> p h e", e=HD))
                    act.copy(lane[l].vx[:, :, 0:HD], ps[l][:, 3, D:2 * D].rearrange("p (h e) -> p h e", e=HD)
                             ).then_inc(s.v, 1)
                for half in range(2):
                    for l in range(LANES):
                        act.wait_ge(s.s_sub, nth_half(t, l, half))
                        part = lane[l].p[:, 8 * half:8 * half + 8, :]
                        act.activation(part, part, ACT.Exp, scale=HD ** -0.5).then_inc(s.p, 1)
                for half in range(2):
                    for l in range(LANES):
                        dst = (lane[l].ptc, lane[l].ptx)[half]
                        act.wait_ge(s.pta_ps, nth_half(t, l, half))
                        act.copy(dst[:, 0:H // 2, :],
                                 ps[l][0:(SC, S)[half], 0:2, :].rearrange("p b (j q) -> p (b j) q", q=S)).then_inc(s.pta, 1)
                for l in range(LANES):
                    act.wait_ge(s.at_ps, nth(t, l))
                    act.copy(lane[l].ot[:], ps[l][:, 1, 0:S]).then_inc(s.at, 1)

        @block.gpsimd
        def _(pool):
            with pool.Fori(0, TURNS) as t:
                for l in range(LANES):
                    pool.wait_ge(s.var_eps, nth(t, l))
                    inverse_root(pool, lane[l].rstd[:], lane[l].var_eps[:], m, s.rstd)

        @block.vector
        def _(dve):
            for l in range(LANES):
                dve.memset(lane[l].vc[:, :, HD:HD + 1], 1.0).then_inc(s.ones, 1)
                dve.memset(lane[l].vx[:, :, HD:HD + 1], 1.0).then_inc(s.ones, 1)
            dve.wait_ge(s.ones, 2 * LANES)
            with dve.Fori(0, TURNS) as t:
                layer_norm_stats(dve, m, s, t, lane)
                for l in range(LANES):
                    dve.wait_ge(s.rstd, nth(t, l))
                    dve.tensor_scalar(lane[l].xn[:], m.x[:, bass.ds((t * LANES + l) * D, D)], lane[l].mv[:, 0:1],
                                      lane[l].rstd[:], ALU.subtract, ALU.mult).then_inc(s.xn, 1)
                for l in range(LANES):
                    dve.wait_ge(s.q_ps, nth(t, l))
                    dve.tensor_tensor(lane[l].qm[:], ps[l][:, 1, 0:S].unsqueeze(1).broadcast_to([D, 4, S]),
                                      bcast(m.headmask[:], S), ALU.mult).then_inc(s.qm, 1)
                for half in range(2):
                    for l in range(LANES):
                        scores = ps[l][:, :, :].rearrange("p b (j n) -> p b j n", n=256)[:, :, :, 0:SK]
                        dve.wait_ge(s.s_ps, nth_half(t, l, half))
                        dve.tensor_reduce(lane[l].mx[:, 8 * half:8 * half + 8].rearrange("p (b j) -> p b j", j=2),
                                          scores, AX.X, ALU.max).then_inc(s.s_max, 1)
                    for l in range(LANES):
                        scores = ps[l][:, :, :].rearrange("p b (j n) -> p b j n", n=256)[:, :, :, 0:SK]
                        dve.wait_ge(s.s_max, nth_half(t, l, half))
                        dve.tensor_tensor(lane[l].p[:, 8 * half:8 * half + 8, :].rearrange("p (b j) n -> p b j n", j=2),
                                          scores, bcast(lane[l].mx[:, 8 * half:8 * half + 8], SK
                                                        ).rearrange("p (b j) n -> p b j n", j=2),
                                          ALU.subtract).then_inc(s.s_sub, 1)
                for half in range(2):
                    for l in range(LANES):
                        dst = (lane[l].ptc, lane[l].ptx)[half]
                        dve.wait_ge(s.ptb_ps, nth_half(t, l, half))
                        dve.tensor_copy(dst[:, H // 2:H, :],
                                        ps[l][0:(SC, S)[half], 2:4, :].rearrange("p b (j q) -> p (b j) q", q=S)
                                        ).then_inc(s.ptb, 1)
                for l in range(LANES):
                    out = ps[l][:, 0, 0:H * (HD + 1)].rearrange("p (h e) -> p h e", e=HD + 1)
                    dve.wait_ge(s.o_ps, nth(t, l))
                    dve.reciprocal(lane[l].rs[:], out[:, :, HD]).then_inc(s.o_r, 1)
                for l in range(LANES):
                    out = ps[l][:, 0, 0:H * (HD + 1)].rearrange("p (h e) -> p h e", e=HD + 1)
                    dve.wait_ge(s.o_r, nth(t, l))
                    dve.tensor_tensor(lane[l].o[:].rearrange("p (h e) -> p h e", e=HD), out[:, :, 0:HD],
                                      bcast(lane[l].rs[:], HD), ALU.mult).then_inc(s.o, 1)
                for l in range(LANES):
                    xb = m.x[:, bass.ds((t * LANES + l) * D, D)]
                    dve.wait_ge(s.y_ps, nth(t, l))
                    dve.scalar_tensor_tensor(xb, ps[l][:, 2, 0:D], m.tg[:, 2:3], xb, ALU.mult, ALU.add).then_inc(s.x, 1)
                dve.wait_ge(s.x, nth(t, LANES - 1))


@sublayer
def l3_attention(nc, ctx, m, io):
    H, HD = 16, 8
    LANES = 2
    TURNS = B // LANES
    s = semaphores(nc, ctx, "a3", "stats mv var_eps rstd xn xt_ps xt q_ps qb qm kv_ps kt v s_ps s_max s_sub p pta_ps "
                   "pta ptb_ps ptb o_ps o_r o at_ps at y_ps x c0 c1 ones")
    c_in = [s.c0, s.c1]

    def nth(turn, lane):
        return turn * LANES + lane + 1

    with ExitStack() as mem:
        def sb(name, shape, dt=F32):
            return mem.enter_context(nc.sbuf_tensor("a3_" + name, shape, dt))

        lane = [Names(
            stats=sb(f"stats{l}", [S, 6]), mv=sb(f"mv{l}", [S, 2]), var_eps=sb(f"var{l}", [S, 1]),
            rstd=sb(f"rstd{l}", [S, 1]), xn=sb(f"xn{l}", [S, D]), xt=sb(f"xt{l}", [D, S]), ct=sb(f"ct{l}", [D, SC]),
            c=sb(f"c{l}", [SC, D]), q=sb(f"q{l}", [D, S]), qm=sb(f"qm{l}", [D, 4, S]), kt=sb(f"kt{l}", [D, SC]),
            v=sb(f"v{l}", [SC, H, HD + 1]), mx=sb(f"mx{l}", [S, H]), p=sb(f"p{l}", [S, H, SC]),
            pt=sb(f"pt{l}", [SC, H, S]), rs=sb(f"rs{l}", [S, H]), o=sb(f"o{l}", [S, D]), ot=sb(f"ot{l}", [D, S]))
            for l in range(LANES)]
        ps = [mem.enter_context(nc.psum_tensor(f"a3_ps{l}", [128, 4, 512], F32)) for l in range(LANES)]
        block = mem.enter_context(nc.Block())

        @block.sync
        def _(sp):
            load_context(sp, io, s, lane, c_in, TURNS)

        @block.tensor
        def _(pe):
            with pe.Fori(0, TURNS) as t:
                for l in range(LANES):
                    pe.wait_ge(s.xn, nth(t, l))
                    pe.wait_ge(c_in[l], 16 * t + 16)
                    pe.transpose(ps[l][:, 0, 0:S], lane[l].xn[:], m.ident[:])
                    pe.transpose(ps[l][:, 0, S:S + SC], lane[l].c[:], m.ident[0:SC, 0:SC]).then_inc(s.xt_ps, 1)
                for l in range(LANES):
                    pe.wait_ge(s.xt, nth(t, l))
                    pe.matmul(ps[l][:, 1, 0:S], m.wq3[:], lane[l].xt[:], start=True, stop=True).then_inc(s.q_ps, 1)
                    pe.matmul(ps[l][:, 2, 0:SC], m.wk3[:], lane[l].ct[:], start=True, stop=True)
                    pe.matmul(ps[l][0:SC, 3, 0:D], lane[l].ct[:], m.wv3[:], start=True, stop=False)
                    pe.matmul(ps[l][0:SC, 3, 0:D], m.ones_row[:, 0:SC], m.rows[0:1, m.row_bv3, :],
                              start=False, stop=True).then_inc(s.kv_ps, 1)
                for l in range(LANES):
                    pe.wait_ge(s.qm, nth(t, l))
                    pe.wait_ge(s.v, nth(t, l))
                    for quad in range(4):
                        for j in range(4):
                            pe.matmul(ps[l][:, quad, SC * j:SC * j + SC], m.first_row[:],
                                      m.maskneg[:, bass.ds((t * LANES + l) * SC, SC)], start=(j == 0), stop=False)
                    for j in range(4):
                        for quad in range(4):
                            row = slice(32 * quad, 32 * quad + 32)
                            mm = pe.matmul(ps[l][:, quad, SC * j:SC * j + SC], lane[l].qm[row, j, :], lane[l].kt[row, :],
                                           start=False, stop=(j == 3))
                    mm.then_inc(s.s_ps, 1)
                for l in range(LANES):
                    pe.wait_ge(s.p, nth(t, l))
                    for i in range(H):
                        mm = pe.transpose(ps[l][0:SC, i // 4, i % 4 * S:i % 4 * S + S], lane[l].p[:, i, :], m.ident[:])
                        if i == H // 2 - 1:
                            mm.then_inc(s.pta_ps, 1)
                    mm.then_inc(s.ptb_ps, 1)
                for l in range(LANES):
                    pe.wait_ge(s.pta, nth(t, l))
                    pe.wait_ge(s.ptb, nth(t, l))
                    for h in range(H):
                        mm = pe.matmul(ps[l][:, 0, (HD + 1) * h:(HD + 1) * h + HD + 1], lane[l].pt[:, h, :],
                                       lane[l].v[:, h, :], start=True, stop=True)
                    mm.then_inc(s.o_ps, 1)
                for l in range(LANES):
                    pe.wait_ge(s.o, nth(t, l))
                    pe.transpose(ps[l][:, 1, 0:S], lane[l].o[:], m.ident[:]).then_inc(s.at_ps, 1)
                for l in range(LANES):
                    pe.wait_ge(s.at, nth(t, l))
                    pe.matmul(ps[l][:, 2, 0:D], lane[l].ot[:], m.wo3[:], start=True, stop=False)
                    pe.matmul(ps[l][:, 2, 0:D], m.ones_row[:], m.rows[0:1, m.row_bo3, :], start=False, stop=True
                              ).then_inc(s.y_ps, 1)

        @block.scalar
        def _(act):
            with act.Fori(0, TURNS) as t:
                for l in range(LANES):
                    act.wait_ge(s.xt_ps, nth(t, l))
                    act.copy(lane[l].xt[:], ps[l][:, 0, 0:S])
                    act.copy(lane[l].ct[:], ps[l][:, 0, S:S + SC]).then_inc(s.xt, 1)
                for l in range(LANES):
                    act.wait_ge(s.q_ps, nth(t, l))
                    act.activation(lane[l].q[:], ps[l][:, 1, 0:S], ACT.Identity, bias=m.bqk3[:, 0:1]).then_inc(s.qb, 1)
                    act.wait_ge(s.kv_ps, nth(t, l))
                    act.activation(lane[l].kt[:], ps[l][:, 2, 0:SC], ACT.Identity, bias=m.bqk3[:, 1:2])
                    act.copy(lane[l].v[:, :, 0:HD], ps[l][0:SC, 3, 0:D].rearrange("p (h e) -> p h e", e=HD)
                             ).then_inc(s.v, 1)
                for l in range(LANES):
                    act.wait_ge(s.s_sub, nth(t, l))
                    act.activation(lane[l].p[:], lane[l].p[:], ACT.Exp, scale=HD ** -0.5).then_inc(s.p, 1)
                for l in range(LANES):
                    act.wait_ge(s.pta_ps, nth(t, l))
                    act.copy(lane[l].pt[:, 0:H // 2, :], ps[l][0:SC, 0:2, :].rearrange("p b (j q) -> p (b j) q", q=S)
                             ).then_inc(s.pta, 1)
                for l in range(LANES):
                    act.wait_ge(s.at_ps, nth(t, l))
                    act.copy(lane[l].ot[:], ps[l][:, 1, 0:S]).then_inc(s.at, 1)

        @block.gpsimd
        def _(pool):
            with pool.Fori(0, TURNS) as t:
                for l in range(LANES):
                    pool.wait_ge(s.var_eps, nth(t, l))
                    inverse_root(pool, lane[l].rstd[:], lane[l].var_eps[:], m, s.rstd)

        @block.vector
        def _(dve):
            for l in range(LANES):
                dve.memset(lane[l].v[:, :, HD:HD + 1], 1.0).then_inc(s.ones, 1)
            dve.wait_ge(s.ones, LANES)
            with dve.Fori(0, TURNS) as t:
                layer_norm_stats(dve, m, s, t, lane)
                for l in range(LANES):
                    dve.wait_ge(s.rstd, nth(t, l))
                    dve.tensor_scalar(lane[l].xn[:], m.x[:, bass.ds((t * LANES + l) * D, D)], lane[l].mv[:, 0:1],
                                      lane[l].rstd[:], ALU.subtract, ALU.mult).then_inc(s.xn, 1)
                for l in range(LANES):
                    dve.wait_ge(s.qb, nth(t, l))
                    dve.tensor_tensor(lane[l].qm[:], lane[l].q[:].unsqueeze(1).broadcast_to([D, 4, S]),
                                      bcast(m.headmask[:], S), ALU.mult).then_inc(s.qm, 1)
                for l in range(LANES):
                    scores = ps[l][:, :, 0:4 * SC].rearrange("p b (j n) -> p b j n", n=SC)
                    dve.wait_ge(s.s_ps, nth(t, l))
                    dve.tensor_reduce(lane[l].mx[:].rearrange("p (b j) -> p b j", j=4), scores, AX.X, ALU.max
                                      ).then_inc(s.s_max, 1)
                for l in range(LANES):
                    scores = ps[l][:, :, 0:4 * SC].rearrange("p b (j n) -> p b j n", n=SC)
                    dve.wait_ge(s.s_max, nth(t, l))
                    dve.tensor_tensor(lane[l].p[:].rearrange("p (b j) n -> p b j n", j=4), scores,
                                      bcast(lane[l].mx[:], SC).rearrange("p (b j) n -> p b j n", j=4), ALU.subtract
                                      ).then_inc(s.s_sub, 1)
                for l in range(LANES):
                    dve.wait_ge(s.ptb_ps, nth(t, l))
                    dve.tensor_copy(lane[l].pt[:, H // 2:H, :],
                                    ps[l][0:SC, 2:4, :].rearrange("p b (j q) -> p (b j) q", q=S)).then_inc(s.ptb, 1)
                for l in range(LANES):
                    out = ps[l][:, 0, 0:H * (HD + 1)].rearrange("p (h e) -> p h e", e=HD + 1)
                    dve.wait_ge(s.o_ps, nth(t, l))
                    dve.reciprocal(lane[l].rs[:], out[:, :, HD]).then_inc(s.o_r, 1)
                for l in range(LANES):
                    out = ps[l][:, 0, 0:H * (HD + 1)].rearrange("p (h e) -> p h e", e=HD + 1)
                    dve.wait_ge(s.o_r, nth(t, l))
                    dve.tensor_tensor(lane[l].o[:].rearrange("p (h e) -> p h e", e=HD), out[:, :, 0:HD],
                                      bcast(lane[l].rs[:], HD), ALU.mult).then_inc(s.o, 1)
                for l in range(LANES):
                    xb = m.x[:, bass.ds((t * LANES + l) * D, D)]
                    dve.wait_ge(s.y_ps, nth(t, l))
                    dve.scalar_tensor_tensor(xb, ps[l][:, 2, 0:D], m.tg[:, 3:4], xb, ALU.mult, ALU.add).then_inc(s.x, 1)
                dve.wait_ge(s.x, nth(t, LANES - 1))


@sublayer
def l2_ffn(nc, ctx, m, io):
    F = 512
    FC = F // 128
    LANES = 4
    TURNS = B // LANES
    ROUND = 1.5 * 2 ** 23
    NW = 3 * D * F // D
    s = semaphores(nc, ctx, "f2", "w wsum wsum_ps wmean wclip wscale wr1 wr2 wq wg stats mv var_eps rstd xn mx clip rcp qs dq xa "
                   "xb xq xt_ps xt gu_ps sg h hmx hclip hrcp hqs hdq ha hb hq ht_ps ht y_ps x")

    def nth(turn, lane):
        return turn * LANES + lane + 1

    with ExitStack() as mem:
        def sb(name, shape, dt=F32):
            return mem.enter_context(nc.sbuf_tensor("f2_" + name, shape, dt))

        w = sb("w", [128, 3, F])
        wr = sb("wr", [128, 3, F])
        wq = sb("wq", [128, 3, F], BF16)
        wsum, wmean, wscale = sb("wsum", [128, 3]), sb("wmean", [128, 3]), sb("wscale", [128, 3])
        wdg = sb("wdg", [128, 1])
        ones = sb("ones", [128, 128])
        lane = [Names(
            stats=sb(f"stats{l}", [S, 6]), mv=sb(f"mv{l}", [S, 2]), var_eps=sb(f"var{l}", [S, 1]),
            rstd=sb(f"rstd{l}", [S, 1]), xn=sb(f"xn{l}", [S, D]), mx=sb(f"mx{l}", [S, 2]), clip=sb(f"clip{l}", [S, 2]),
            rcp=sb(f"rcp{l}", [S, 2]), qs=sb(f"qs{l}", [S, 2]), dq=sb(f"dq{l}", [S, 3]), xa=sb(f"xa{l}", [S, D]),
            xq=sb(f"xq{l}", [S, D], BF16), xt=sb(f"xt{l}", [D, S], BF16), sg=sb(f"sg{l}", [S, F]), h=sb(f"h{l}", [S, F]),
            hq=sb(f"hq{l}", [S, F], BF16), ht=sb(f"ht{l}", [128, FC, S], BF16)) for l in range(LANES)]
        ps = [mem.enter_context(nc.psum_tensor(f"f2_ps{l}", [128, 2, 512], F32)) for l in range(LANES)]
        ps_b = [p[:, 0, :].bitcast(BF16) for p in ps]
        block = mem.enter_context(nc.Block())

        @block.sync
        def _(sp):
            sp.dma_start(w[:, 0, :], io.w_gate).then_inc(s.w, 16)
            sp.dma_start(w[:, 1, :], io.w_up).then_inc(s.w, 16)
            sp.dma_start(w[:, 2, :].rearrange("p (c n) -> p c n", c=FC), io.w_down).then_inc(s.w, 16)

        @block.tensor
        def _(pe):
            pe.wait_ge(s.wsum, 2)
            pe.matmul(ps[0][:, 0, 0:3], ones[:], wsum[:], start=True, stop=True).then_inc(s.wsum_ps, 1)
            pe.wait_ge(s.wq, 1)
            with pe.Fori(0, TURNS) as t:
                for l in range(LANES):
                    pe.wait_ge(s.xq, nth(t, l))
                    pe.transpose(ps_b[l][:, 0:S], lane[l].xq[:], m.identb[:]).then_inc(s.xt_ps, 1)
                for l in range(LANES):
                    pe.wait_ge(s.xt, nth(t, l))
                    for n in range(2):
                        mm = pe.matmul(ps[l][:, n, :], lane[l].xt[:], wq[:, n, :], start=True, stop=True)
                    mm.then_inc(s.gu_ps, 1)
                for l in range(LANES):
                    pe.wait_ge(s.hq, nth(t, l))
                    for c in range(FC):
                        mm = pe.transpose(ps_b[l][:, S * c:S * c + S], lane[l].hq[:, 128 * c:128 * c + 128], m.identb[:])
                    mm.then_inc(s.ht_ps, 1)
                for l in range(LANES):
                    pe.wait_ge(s.ht, nth(t, l))
                    for c in range(FC):
                        mm = pe.matmul(ps[l][:, 1, 0:D], lane[l].ht[:, c, :], wq[:, 2, D * c:D * c + D],
                                       start=(c == 0), stop=(c == FC - 1))
                    mm.then_inc(s.y_ps, 1)

        @block.scalar
        def _(act):
            with act.Fori(0, TURNS) as t:
                for l in range(LANES):
                    act.wait_ge(s.xt_ps, nth(t, l))
                    act.copy(lane[l].xt[:], ps_b[l][:, 0:S]).then_inc(s.xt, 1)
                for l in range(LANES):
                    act.wait_ge(s.dq, nth(t, l))
                    act.wait_ge(s.gu_ps, nth(t, l))
                    act.activation(lane[l].sg[:], ps[l][:, 0, :], ACT.Silu, scale=lane[l].dq[:, 0:1]).then_inc(s.sg, 1)
                for l in range(LANES):
                    act.wait_ge(s.ht_ps, nth(t, l))
                    act.copy(lane[l].ht[:], ps_b[l][:, 0:FC * S].rearrange("p (c n) -> p c n", c=FC)).then_inc(s.ht, 1)

        @block.gpsimd
        def _(pool):
            pool.memset(ones[:], 1.0).then_inc(s.wsum, 1)
            with pool.Fori(0, TURNS) as t:
                for l in range(LANES):
                    pool.wait_ge(s.var_eps, nth(t, l))
                    inverse_root(pool, lane[l].rstd[:], lane[l].var_eps[:], m, s.rstd)

        @block.vector
        def _(dve):
            dve.wait_ge(s.w, 48)
            dve.tensor_reduce(wsum[:], w[:], AX.X, ALU.add, apply_absolute_value=True).then_inc(s.wsum, 1)
            dve.wait_ge(s.wsum_ps, 1)
            dve.tensor_scalar(wmean[:], ps[0][:, 0, 0:3], 1.0 / (D * F), 1e-5, ALU.mult, ALU.max).then_inc(s.wmean, 1)
            dve.wait_ge(s.wmean, 1)
            dve.reciprocal(wscale[:], wmean[:]).then_inc(s.wscale, 1)
            dve.tensor_tensor(wdg[:], wmean[:, 2:3], m.tg[:, 6:7], ALU.mult).then_inc(s.wg, 1)
            dve.wait_ge(s.wscale, 1)
            for n in range(3):
                dve.tensor_scalar(wr[:, n, :], w[:, n, :], wscale[:, n:n + 1], ROUND, ALU.mult, ALU.add).then_inc(s.wr1, 1)
            dve.wait_ge(s.wr1, 3)
            dve.tensor_scalar(w[:], wr[:], ROUND, -1.0, ALU.subtract, ALU.max).then_inc(s.wr2, 1)
            dve.wait_ge(s.wr2, 1)
            dve.tensor_scalar(wq[:], w[:], 1.0, None, ALU.min).then_inc(s.wq, 1)
            dve.wait_ge(s.wg, 1)
            with dve.Fori(0, TURNS) as t:
                layer_norm_stats(dve, m, s, t, lane)
                for l in range(LANES):
                    dve.wait_ge(s.rstd, nth(t, l))
                    dve.tensor_scalar(lane[l].xn[:], m.x[:, bass.ds((t * LANES + l) * D, D)], lane[l].mv[:, 0:1],
                                      lane[l].rstd[:], ALU.subtract, ALU.mult).then_inc(s.xn, 1)

                def scales(k, source, waited, sems):
                    mx, clip, rcp, qs = sems
                    for l in range(LANES):
                        dve.wait_ge(waited, nth(t, l))
                        dve.tensor_reduce(lane[l].mx[:, k:k + 1], source(l), AX.X, ALU.max, apply_absolute_value=True
                                          ).then_inc(mx, 1)
                    for l in range(LANES):
                        dve.wait_ge(mx, nth(t, l))
                        dve.tensor_scalar(lane[l].clip[:, k:k + 1], lane[l].mx[:, k:k + 1], 1e-5, None, ALU.max
                                          ).then_inc(clip, 1)
                    for l in range(LANES):
                        dve.wait_ge(clip, nth(t, l))
                        dve.reciprocal(lane[l].rcp[:, k:k + 1], lane[l].clip[:, k:k + 1]).then_inc(rcp, 1)
                    for l in range(LANES):
                        dve.wait_ge(rcp, nth(t, l))
                        dve.tensor_scalar(lane[l].qs[:, k:k + 1], lane[l].rcp[:, k:k + 1], 127.0, None, ALU.mult
                                          ).then_inc(qs, 1)

                scales(0, lambda l: lane[l].xn[:], s.xn, (s.mx, s.clip, s.rcp, s.qs))
                for l in range(LANES):
                    dve.tensor_scalar(lane[l].dq[:, 0:2], wmean[:, 0:2], lane[l].clip[:, 0:1], 1.0 / 127, ALU.mult, ALU.mult
                                      ).then_inc(s.dq, 1)
                for l in range(LANES):
                    dve.wait_ge(s.qs, nth(t, l))
                    dve.tensor_scalar(lane[l].xa[:], lane[l].xn[:], lane[l].qs[:, 0:1], ROUND, ALU.mult, ALU.add
                                      ).then_inc(s.xa, 1)
                for l in range(LANES):
                    dve.wait_ge(s.xa, nth(t, l))
                    dve.tensor_scalar(lane[l].xn[:], lane[l].xa[:], ROUND, -128.0, ALU.subtract, ALU.max).then_inc(s.xb, 1)
                for l in range(LANES):
                    dve.wait_ge(s.xb, nth(t, l))
                    dve.tensor_scalar(lane[l].xq[:], lane[l].xn[:], 127.0, None, ALU.min).then_inc(s.xq, 1)
                for l in range(LANES):
                    dve.wait_ge(s.dq, nth(t, l))
                    dve.wait_ge(s.sg, nth(t, l))
                    dve.scalar_tensor_tensor(lane[l].h[:], ps[l][:, 1, :], lane[l].dq[:, 1:2], lane[l].sg[:],
                                             ALU.mult, ALU.mult).then_inc(s.h, 1)
                scales(1, lambda l: lane[l].h[:], s.h, (s.hmx, s.hclip, s.hrcp, s.hqs))
                for l in range(LANES):
                    dve.tensor_scalar(lane[l].dq[:, 2:3], wdg[:], lane[l].clip[:, 1:2], 1.0 / 127, ALU.mult, ALU.mult
                                      ).then_inc(s.hdq, 1)
                for l in range(LANES):
                    dve.wait_ge(s.hqs, nth(t, l))
                    dve.tensor_scalar(lane[l].sg[:], lane[l].h[:], lane[l].qs[:, 1:2], ROUND, ALU.mult, ALU.add
                                      ).then_inc(s.ha, 1)
                for l in range(LANES):
                    dve.wait_ge(s.ha, nth(t, l))
                    dve.tensor_scalar(lane[l].h[:], lane[l].sg[:], ROUND, -128.0, ALU.subtract, ALU.max).then_inc(s.hb, 1)
                for l in range(LANES):
                    dve.wait_ge(s.hb, nth(t, l))
                    dve.tensor_scalar(lane[l].hq[:], lane[l].h[:], 127.0, None, ALU.min).then_inc(s.hq, 1)
                for l in range(LANES):
                    xb = m.x[:, bass.ds((t * LANES + l) * D, D)]
                    dve.wait_ge(s.hdq, nth(t, l))
                    dve.wait_ge(s.y_ps, nth(t, l))
                    dve.scalar_tensor_tensor(xb, ps[l][:, 1, 0:D], lane[l].dq[:, 2:3], xb, ALU.mult, ALU.add).then_inc(s.x, 1)
                dve.wait_ge(s.x, nth(t, LANES - 1))


HOST_LAYOUT = {
    "L0_ffn_Wg": (1, 0, 2), "L0_ffn_Wu": (1, 0, 2),
    "L1_ffn_Wg": (1, 0), "L1_ffn_W1": (2, 0, 1), "L1_ffn_W2": (2, 0, 1), "L1_ffn_W3": (2, 0, 1),
    "L2_ffn_w_gate": (1, 0), "L2_ffn_w_up": (1, 0), "L2_ffn_w_down": (1, 0),
    "L3_ffn_w1": (1, 0, 2), "L0_ffn_bd": (1, 0),
    "L0_ffn_bg": (2, 0, 1), "L0_ffn_bu": (2, 0, 1), "L3_ffn_b1": (2, 0, 1),
}
HOST_SHAPE = {"L0_ffn_bg": (16, 2, 128), "L0_ffn_bu": (16, 2, 128), "L3_ffn_b1": (8, 4, 128)}


def run_phases(nc, ctx, m, io):
    ios = Names(ctx=io["ctx_1024"])
    m.prefetch_a1 = m.prefetch_a2 = None
    if 1 in PHASES:
        f = {n: io["L0_ffn_" + n] for n in ("norm_g", "norm_b", "slot_g", "slot_b", "scale", "slot_embeds", "Wg", "Wu")}
        l0_ffn(nc, m, Names(
            Wd=io["L0_ffn_Wd"].rearrange("e (c p) n -> p e c n", p=128),
            bg=io["L0_ffn_bg"], bu=io["L0_ffn_bu"], bd=io["L0_ffn_bd"], **f))
    if 2 in PHASES:
        l1_attention(nc, m, ios)
    if 3 in PHASES:
        routed_ffn(nc, m, Names(
            router=io["L1_ffn_Wg"], w1=io["L1_ffn_W1"].rearrange("d e (c p) -> d e c p", p=128),
            w2=io["L1_ffn_W2"].rearrange("d e (c p) -> d e c p", p=128),
            w3=io["L1_ffn_W3"].rearrange("(c p) e n -> p e c n", p=128)), "top2")
    if 4 in PHASES:
        l2_attention(nc, m, ios)
    if 5 in PHASES:
        l2_ffn(nc, m, Names(
            w_gate=io["L2_ffn_w_gate"], w_up=io["L2_ffn_w_up"],
            w_down=io["L2_ffn_w_down"].rearrange("(c p) n -> p c n", p=128)))
    if 6 in PHASES:
        l3_attention(nc, m, ios)
    if 7 in PHASES:
        routed_ffn(nc, m, Names(
            router=io["L3_ffn_router_w"], w1=io["L3_ffn_w1"].rearrange("d e (c p) -> d e c p", p=128),
            b1=io["L3_ffn_b1"],
            w3=io["L3_ffn_w2"].rearrange("e (c p) n -> p e c n", p=128), b2=io["L3_ffn_b2"]), "switch")


def bass_flamingo_gated_stack(nc, io, out):
    with ExitStack() as ctx:
        def sb(name, shape, dt=F32):
            return ctx.enter_context(nc.sbuf_tensor(name, shape, dt))

        m = Shared()
        m.x = sb("x_res", [S, B * D])
        m.ident = sb("ident", [128, 128])
        m.identb = sb("identb", [128, 128], BF16)
        m.causal = sb("causal", [S, SC + S], BF16)
        m.first_row = sb("first_row", [128, 128], BF16)
        m.minus_half = sb("minus_half", [128, 16])
        m.ones_row = sb("ones_row", [1, 128])
        m.wait_pad = sb("wait_pad", [128, 1])
        m.zero = sb("zero", [128, 1])
        m.g_raw = sb("g_raw", [128, 8])
        m.tg = sb("tg", [128, 8])
        m.mask = sb("mask", [128, B * SC], U8)
        m.maskneg = sb("maskneg", [128, B * SC], BF16)
        ROWS = "bo0 bv1 bout2 bv3 bo3".split()
        m.rows = sb("rows", [1, len(ROWS), D])
        m.row_bo0, m.row_bv1, m.row_bout2, m.row_bv3, m.row_bo3 = range(5)
        m.gq = sb("gq", [128, 1])
        m.gk = sb("gk", [128, 1])
        m.gqk = sb("gqk", [128, 1])
        m.bqk1 = sb("bqk1", [128, 2])
        m.bqk3 = sb("bqk3", [128, 2])
        m.headmask = sb("headmask", [128, 4])
        m.wq1, m.wk1, m.wv1 = (sb(n, [D, D]) for n in ("wq1", "wk1", "wv1"))
        m.wq2, m.wkv2, m.wout2 = sb("wq2", [D, D]), sb("wkv2", [D, 2 * D]), sb("wout2", [D, D])
        m.wq3, m.wk3, m.wv3, m.wo3 = (sb(n, [D, D]) for n in ("wq3", "wk3", "wv3", "wo3"))

        m.s_small = ctx.enter_context(nc.semaphore("small_in"))
        m.s_x = ctx.enter_context(nc.semaphore("x_in"))
        m.s_w0 = ctx.enter_context(nc.semaphore("w0_in"))
        m.s_out = ctx.enter_context(nc.semaphore("out_done"))
        m.s_ready = ctx.enter_context(nc.semaphore("ready"))
        setup = semaphores(nc, [], "setup", "zero ident identb causal misc tanh vec hm")
        small = []
        for i, n in enumerate(("L0_xattn_bo", "L1_xattn_bv", "L2_xattn_bout", "L3_xattn_bv", "L3_xattn_bo")):
            small.append((m.rows[0:1, i, :], io[n].unsqueeze(0)))
        small += [(m.g_raw[:, 0:4], io["g_xattn"].partition_broadcast(128)),
                  (m.g_raw[:, 4:8], io["g_ffn"].partition_broadcast(128)),
                  (m.mask[:], io["mask_BxS2_bk0"].rearrange("b s -> (b s)").partition_broadcast(128)),
                  (m.bqk1[:, 0:1], io["L1_xattn_bq"].unsqueeze(1)), (m.bqk1[:, 1:2], io["L1_xattn_bk"].unsqueeze(1)),
                  (m.bqk3[:, 0:1], io["L3_xattn_bq"].unsqueeze(1)), (m.bqk3[:, 1:2], io["L3_xattn_bk"].unsqueeze(1)),
                  (m.wq1[:], io["L1_xattn_Wq"]), (m.wk1[:], io["L1_xattn_Wk"]), (m.wv1[:], io["L1_xattn_Wv"]),
                  (m.wq2[:], io["L2_xattn_Wq"]), (m.wkv2[:], io["L2_xattn_Wkv"]), (m.wout2[:], io["L2_xattn_Wout"]),
                  (m.wq3[:], io["L3_xattn_Wq"]), (m.wk3[:], io["L3_xattn_Wk"]), (m.wv3[:], io["L3_xattn_Wv"]),
                  (m.wo3[:], io["L3_xattn_Wo"])]
        for half in range(2):
            row = slice(64 * half, 64 * half + 64)
            small += [(m.gq[row], io["L0_xattn_gq"].unsqueeze(1)), (m.gk[row], io["L0_xattn_gk"].unsqueeze(1))]

        with ExitStack() as mem0:
            if 0 in PHASES:
                m.wq0, m.wk0, m.wv0 = (mem0.enter_context(nc.sbuf_tensor(n, [D, 1024], F32)) for n in ("wq0", "wk0", "wv0"))
                m.wo0 = mem0.enter_context(nc.sbuf_tensor("wo0", [128, 8, D], F32))
            m.n_w0 = 64
            m.prefetch_a0 = None
            with nc.Block() as block:
                @block.sync
                def _(sp):
                    for dst, src in small:
                        sp.dma_start(dst, src).then_inc(m.s_small, 16)
                    xv = io["x"].rearrange("b s d -> s b d")
                    sp.dma_start(m.x[:].rearrange("p (b d) -> p b d", d=D), xv).then_inc(m.s_x, 16)
                    if 0 in PHASES:
                        sp.dma_start(m.wq0[:], io["L0_xattn_Wq"].rearrange("d h e -> d (h e)")).then_inc(m.s_w0, 16)
                        sp.dma_start(m.wk0[:], io["L0_xattn_Wk"].rearrange("d h e -> d (h e)")).then_inc(m.s_w0, 16)
                        sp.dma_start(m.wv0[:], io["L0_xattn_Wv"].rearrange("d h e -> d (h e)")).then_inc(m.s_w0, 16)
                        sp.dma_start(m.wo0[:], io["L0_xattn_Wo"].rearrange("(j a) e n -> (a e) j n", a=2)).then_inc(m.s_w0, 16)

                @block.gpsimd
                def _(pool):
                    pool.memset(m.ident[:], 0.0).then_inc(setup.zero, 1)
                    pool.memset(m.causal[:], 0.0).then_inc(setup.zero, 1)
                    pool.memset(m.minus_half[:], -0.5)
                    pool.memset(m.ones_row[:], 1.0)
                    pool.memset(m.first_row[:], 0.0).then_inc(setup.zero, 1)
                    pool.memset(m.headmask[:], 1.0).then_inc(setup.zero, 1)
                    pool.wait_ge(setup.zero, 4)
                    pool.memset(m.first_row[0:1, :], 1.0).then_inc(setup.misc, 1)
                    pool.wait_ge(setup.misc, 1)
                    pool.affine_select(m.ident[:], m.ident[:], [[-1, 128]], ALU.not_equal, 1.0, 0, 1).then_inc(setup.ident, 1)
                    pool.affine_select(m.causal[:, SC:SC + S], m.causal[:, SC:SC + S], [[-1, S]], ALU.is_ge, NEG, 0, 1).then_inc(setup.causal, 1)
                    for quad in range(4):
                        if quad:
                            pool.wait_ge(setup.hm, 2 * quad)
                        part = m.headmask[32 * quad:32 * quad + 32, :]
                        pool.affine_select(part, part, [[-8, 4]], ALU.is_ge, 0.0, 0, 1).then_inc(setup.hm, 1)
                        pool.wait_ge(setup.hm, 2 * quad + 1)
                        pool.affine_select(part, part, [[8, 4]], ALU.is_ge, 0.0, 7, -1).then_inc(setup.hm, 1)
                    pool.wait_ge(setup.hm, 8)
                    pool.wait_ge(setup.ident, 1)
                    pool.tensor_copy(m.identb[:], m.ident[:]).then_inc(setup.identb, 1)

                @block.scalar
                def _(act):
                    act.wait_ge(m.s_small, 16 * len(small))
                    act.activation(m.tg[:], m.g_raw[:], ACT.Tanh).then_inc(setup.tanh, 1)

                @block.vector
                def _(dve):
                    dve.wait_ge(m.s_small, 16 * len(small))
                    dve.tensor_tensor(m.gqk[:], m.gq[:], m.gk[:], ALU.mult).then_inc(setup.vec, 1)
                    dve.tensor_scalar(m.maskneg[:], m.mask[:], NEG, None, ALU.mult).then_inc(setup.vec, 1)
                    dve.memset(m.zero[:], 0.0).then_inc(m.s_ready, 1)
                    dve.wait_ge(m.s_x, 16)
            ios = Names(ctx=io["ctx_1024"])
            if 0 in PHASES:
                l0_attention(nc, m, ios)
        run_phases(nc, ctx, m, io)

        with nc.Block() as block:
            @block.sync
            def _(sp):
                sp.dma_start(out.rearrange("b s d -> s b d"), m.x[:].rearrange("p (b d) -> p b d", d=D)
                             ).then_inc(m.s_out, 16)
                sp.wait_ge(m.s_out, 16)


def kernel(**inputs):
    import numpy as np
    import concourse.bacc as bacc
    from concourse.bass_utils import run_bass_kernel_spmd

    nc = bacc.Bacc("TRN2", target_bir_lowering=False, num_devices=1)
    arrays, io = {}, {}
    for name, value in inputs.items():
        a = np.ascontiguousarray(value)
        if name in HOST_SHAPE:
            a = a.reshape(HOST_SHAPE[name])
        if name in HOST_LAYOUT:
            a = np.ascontiguousarray(np.transpose(a, HOST_LAYOUT[name]))
        arrays[f"in_{name}"] = a
        io[name] = nc.dram_tensor(f"in_{name}", a.shape, mybir.dt.from_np(a.dtype), kind="ExternalInput").ap()
    out = nc.dram_tensor("out_x", (B, S, D), F32, kind="ExternalOutput").ap()
    bass_flamingo_gated_stack(nc, io, out)
    result = run_bass_kernel_spmd(nc, [arrays], core_ids=[0])
    return result.results[0]["out_x"]
```

```python
from collections import namedtuple
from contextlib import ExitStack

import concourse.bass as bass
from concourse import mybir

F32 = mybir.dt.float32
BF16 = mybir.dt.bfloat16
U8 = mybir.dt.uint8
U32 = mybir.dt.uint32
ALU = mybir.AluOpType
ACT = mybir.ActivationFunctionType
AX = mybir.AxisListType

B, S, D = 32, 128, 128
SC = 77
LN_EPS = 1e-5
NEG = -1e30


class Shared:
    pass


def Names(**named):
    return namedtuple("Names", sorted(named))(**named)


def semaphores(nc, own, phase, names):
    found = {n: nc.alloc_semaphore(name=f"{phase}_{n}") for n in names.split()}
    own += found.values()
    return Names(**found)


def bcast(ap, n):
    return ap.unsqueeze(2).broadcast_to([ap.shape[0], ap.shape[1], n])


def sublayer(build):
    def scoped(nc, m, *args):
        own = []
        build(nc, own, m, *args)
        nc.clear_and_free_semaphores(own)
        nc.all_engine_barrier()
    return scoped


def staggered(eng, turns, lanes, places, steps):
    lag = places // lanes

    def part(i, turn, every):
        for l in sorted(range(lanes), key=lambda l: (i - lag * l) % places):
            place = (i - lag * l) % places
            own_turn = turn if i >= lag * l else turn - 1
            if place - places in steps and (every or 0 <= own_turn + 1 < turns):
                steps[place - places](own_turn + 1, l)
            if place in steps and (every or 0 <= own_turn < turns):
                steps[place](own_turn, l)

    for i in range(places + min(steps), places):
        part(i, -1, False)
    for i in range(places):
        part(i, 0, False)
    with eng.Fori(0, turns - 2) as t:
        for i in range(places):
            part(i, t + 1, True)
    for i in range(places):
        part(i, turns - 1, False)
    for i in range(lag * (lanes - 1)):
        part(i, turns, False)


PHASES = range(8)


def token_stats(dve, m, s, l, batch, n):
    dve.bn_stats(l.stats[:], m.x[:, bass.ds(batch * D, D)]).then_inc(s.stats, 1)
    dve.wait_ge(s.stats, n)
    dve.memset(m.wait_pad[:], 0.0)
    dve.bn_aggr(l.mv[:], l.stats[:]).then_inc(s.mv, 1)
    dve.wait_ge(s.mv, n)
    dve.tensor_scalar(l.var_eps[:], l.mv[:, 1:2], LN_EPS, None, ALU.add).then_inc(s.var_eps, 1)


def layer_norm_stats(dve, m, s, turn, lanes, lane_offset=0):
    L = len(lanes)
    for i, l in enumerate(lanes):
        dve.bn_stats(l.stats[:], m.x[:, bass.ds((turn * L + i) * D, D)]).then_inc(s.stats, 1)
    dve.wait_ge(s.stats, turn * L + L)
    dve.memset(m.wait_pad[:], 0.0)
    for i, l in enumerate(lanes):
        dve.bn_aggr(l.mv[:], l.stats[:]).then_inc(s.mv, 1)
    for i, l in enumerate(lanes):
        dve.wait_ge(s.mv, turn * L + i + 1)
        dve.tensor_scalar(l.var_eps[:], l.mv[:, 1:2], LN_EPS, None, ALU.add).then_inc(s.var_eps, 1)


def load_context(sp, io, s, lane, c_in, turns):
    L = len(lane)
    for l in range(L):
        sp.dma_start(lane[l].c[:], io.ctx[l]).then_inc(c_in[l], 16)
    with sp.Fori(0, turns - 1) as t:
        for l in range(L):
            sp.wait_ge(s.xt_ps, t * L + l + 1)
            sp.dma_start(lane[l].c[:], io.ctx[bass.ds((t + 1) * L + l, 1)].rearrange("a s d -> (a s) d")
                         ).then_inc(c_in[l], 16)


def inverse_root(pool, out, in_, m, done):
    n = in_.shape[1]
    pool.tensor_tensor(out, in_, m.minus_half[0:in_.shape[0], 0:n], ALU.pow).then_inc(done, 1)


@sublayer
def l0_attention(nc, ctx, m, io):
    H, HD = 16, 64
    HH = H // 2
    LANES = 4
    TURNS = B // LANES
    PLACES = 24
    CH = H // 2
    s = semaphores(nc, ctx, "a0", "stats mv var_eps rstd xn xt_ps xt q_ps q q_sq q_ss q_ms q_r v_ps v k_ps k k_sq k_ss "
                   "k_ms k_r k_n qt_ps qt kt_ps km y_ps x "
                   "c0 c1 c2 c3 gzero gain")
    c_in = [s.c0, s.c1, s.c2, s.c3]

    def nth(turn, lane):
        return turn * LANES + lane + 1

    half = [semaphores(nc, ctx, f"a0h{k}", "s_ps s_max s_sub s_q e sum rs p pt_ps pt ot_ps ot") for k in range(2)]

    with ExitStack() as mem:
        def sb(name, shape, dt=F32):
            return mem.enter_context(nc.sbuf_tensor("a0_" + name, shape, dt))

        def lane_buffers(l):
            return Names(
                stats=sb(f"stats{l}", [S, 6]), mv=sb(f"mv{l}", [S, 2]), var_eps=sb(f"var{l}", [S, 1]),
                rstd=sb(f"rstd{l}", [S, 1]), xn=sb(f"xn{l}", [S, D]), xt=sb(f"xt{l}", [D, S]),
                c=sb(f"c{l}", [SC, D]), ct=sb(f"ct{l}", [D, SC]),
                sq=sb(f"sq{l}", [128, H * HD]),
                ss=sb(f"ss{l}", [S, H]), ms=sb(f"ms{l}", [S, H]), r=sb(f"r{l}", [S, H]),
                kss=sb(f"kss{l}", [SC, H]), kms=sb(f"kms{l}", [SC, H]), kr=sb(f"kr{l}", [SC, H]),
                q=sb(f"q{l}", [S, H * HD]),
                kn=sb(f"kn{l}", [128, H * HD]),
                v=sb(f"v{l}", [SC, H, HD]),
                qt=sb(f"qt{l}", [128, CH, S]), km=sb(f"km{l}", [128, CH, 2, SC]),
                mx=sb(f"mx{l}", [S, 2, HH]), p=sb(f"p{l}", [S, 2, HH, SC]), sm=sb(f"sm{l}", [S, 2, HH]),
                rs=sb(f"rs{l}", [S, 2, HH]))

        lane = [lane_buffers(l) for l in range(LANES)]
        pt = [b.sq[0:SC, :].rearrange("p (i q) -> p i q", q=S) for b in lane]
        gain = sb("gain", [128, 2])
        out_t = [b.kn[:].rearrange("p (i q) -> p i q", q=S) for b in lane]
        ps = [mem.enter_context(nc.psum_tensor(f"a0_ps{l}", [128, 2, 512], F32)) for l in range(LANES)]
        block = mem.enter_context(nc.Block())

        def by_chunk(l, n):
            return ps[l][:, :, 0:4 * n].rearrange("p b (j n) -> p b j n", n=n)

        @block.sync
        def _(sp):
            load_context(sp, io, s, lane, c_in, TURNS)

        @block.tensor
        def _(pe):
            pe.wait_ge(m.s_w0, m.n_w0)

            def inputs(t, l):
                pe.wait_ge(s.xn, nth(t, l))
                pe.wait_ge(c_in[l], 16 * t + 16)
                pe.transpose(ps[l][:, 0, 0:S], lane[l].xn[:], m.ident[:])
                pe.transpose(ps[l][:, 0, S:S + SC], lane[l].c[:], m.ident[0:SC, 0:SC]).then_inc(s.xt_ps, 1)

            def project(l, out, lhs, w, done):
                for n in range(2):
                    mm = pe.matmul(out[:, n, :], lhs, w[:, 512 * n:512 * n + 512], start=True, stop=True)
                mm.then_inc(done, 1)

            def project_k(t, l):
                pe.wait_ge(s.xt, nth(t, l))
                project(l, ps[l][0:SC], lane[l].ct[:], m.wk0, s.k_ps)

            def project_v(t, l):
                pe.wait_ge(s.k, nth(t, l))
                project(l, ps[l][0:SC], lane[l].ct[:], m.wv0, s.v_ps)

            def project_q(t, l):
                pe.wait_ge(s.v, nth(t, l))
                project(l, ps[l], lane[l].xt[:], m.wq0, s.q_ps)

            def transpose_q(t, l):
                pe.wait_ge(s.q, nth(t, l))
                for j in range(HH):
                    mm = pe.transpose(ps[l][:, j // 4, j % 4 * S:j % 4 * S + S],
                                      lane[l].q[:, 128 * j:128 * j + 128], m.ident[:])
                mm.then_inc(s.qt_ps, 1)

            def transpose_k(t, l):
                pe.wait_ge(s.k_n, nth(t, l))
                pe.wait_ge(s.qt, nth(t, l))
                for j in range(CH):
                    mm = pe.transpose(ps[l][:, j // 4, j % 4 * 128:j % 4 * 128 + SC],
                                      lane[l].kn[0:SC, 128 * j:128 * j + 128], m.ident[0:SC, 0:SC])
                mm.then_inc(s.kt_ps, 1)

            def scores(k):
                def step(t, l):
                    if k:
                        pe.wait_ge(half[0].s_sub, nth(t, l))
                    else:
                        pe.wait_ge(s.km, nth(t, l))
                    for c in range(CH // 2):
                        mm = pe.matmul(ps[l][:, c // 2, c % 2 * 2 * SC:(c % 2 + 1) * 2 * SC],
                                       lane[l].qt[:, CH // 2 * k + c, :], lane[l].km[:, CH // 2 * k + c],
                                       start=True, stop=True)
                    mm.then_inc(half[k].s_ps, 1)
                return step

            def transpose_p(k):
                def step(t, l):
                    pe.wait_ge(half[k].p, nth(t, l))
                    if k:
                        pe.wait_ge(half[0].ot, nth(t, l))
                    else:
                        pe.wait_ge(half[1].s_sub, nth(t, l))
                    for i in range(HH):
                        mm = pe.transpose(ps[l][0:SC, i // 4, i % 4 * S:i % 4 * S + S], lane[l].p[:, k, i, :],
                                          m.ident[:])
                    mm.then_inc(half[k].pt_ps, 1)
                return step

            def mix_v(k):
                def step(t, l):
                    pe.wait_ge(half[k].pt, nth(t, l))
                    for i in range(HH):
                        mm = pe.matmul(ps[l][HD * (i % 2):HD * (i % 2) + HD, k, i // 2 * S:i // 2 * S + S],
                                       lane[l].v[:, HH * k + i, :], pt[l][:, i, :], start=True, stop=True)
                    mm.then_inc(half[k].ot_ps, 1)
                return step

            def project_o(t, l):
                pe.wait_ge(half[1].ot, nth(t, l))
                for j in range(HH):
                    pe.matmul(ps[l][:, 0, 0:D], out_t[l][:, j, :], m.wo0[:, j, :], start=(j == 0), stop=False)
                pe.matmul(ps[l][:, 0, 0:D], m.ones_row[:], m.rows[0:1, m.row_bo0, :], start=False, stop=True
                          ).then_inc(s.y_ps, 1)

            staggered(pe, TURNS, LANES, PLACES, {
                0: inputs, 1: project_k, 2: project_v, 4: project_q, 6: transpose_q, 7: transpose_k,
                10: scores(0), 12: scores(1), 15: transpose_p(0), 16: mix_v(0), 18: transpose_p(1), 19: mix_v(1),
                20: project_o})

        @block.scalar
        def _(act):
            def inputs(t, l):
                act.wait_ge(s.xt_ps, nth(t, l))
                act.copy(lane[l].xt[:], ps[l][:, 0, 0:S])
                act.copy(lane[l].ct[:], ps[l][:, 0, S:S + SC]).then_inc(s.xt, 1)

            def copy_k(t, l):
                act.wait_ge(s.k_ps, nth(t, l))
                act.copy(lane[l].kn[0:SC, :], ps[l][0:SC].rearrange("p b n -> p (b n)")).then_inc(s.k, 1)

            def square_k(t, l):
                act.wait_ge(s.k, nth(t, l))
                act.activation(lane[l].sq[0:SC, :], lane[l].kn[0:SC, :], ACT.Square).then_inc(s.k_sq, 1)

            def copy_v(t, l):
                act.wait_ge(s.v_ps, nth(t, l))
                act.copy(lane[l].v[:, :, 0:HD],
                         ps[l][0:SC].rearrange("p b (h e) -> p (b h) e", e=HD)).then_inc(s.v, 1)

            def copy_q(t, l):
                act.wait_ge(s.q_ps, nth(t, l))
                act.copy(lane[l].q[:], ps[l][:].rearrange("p b n -> p (b n)")).then_inc(s.q, 1)

            def square_q(t, l):
                act.wait_ge(s.q, nth(t, l))
                act.wait_ge(s.k_ss, nth(t, l))
                act.activation(lane[l].sq[:], lane[l].q[:], ACT.Square).then_inc(s.q_sq, 1)

            def copy_qt(t, l):
                act.wait_ge(s.qt_ps, nth(t, l))
                act.copy(lane[l].qt[:].rearrange("p (b j) q -> p b j q", b=2), by_chunk(l, S)).then_inc(s.qt, 1)

            def exponential(k):
                def step(t, l):
                    act.wait_ge(half[k].s_q, nth(t, l))
                    act.activation(lane[l].p[:, k], lane[l].p[:, k], ACT.Exp, scale=HD ** -0.5
                                   ).then_inc(half[k].e, 1)
                return step

            def copy_pt(k):
                def step(t, l):
                    act.wait_ge(half[k].pt_ps, nth(t, l))
                    act.copy(pt[l].rearrange("p (b j) q -> p b j q", b=2), by_chunk(l, S)[0:SC]).then_inc(half[k].pt, 1)
                return step

            def copy_ot(k):
                def step(t, l):
                    act.wait_ge(half[k].ot_ps, nth(t, l))
                    act.copy(out_t[l][:, CH // 2 * k:CH // 2 * (k + 1), :],
                             ps[l][:, k, :].rearrange("p (c q) -> p c q", q=S)).then_inc(half[k].ot, 1)
                return step

            staggered(act, TURNS, LANES, PLACES, {
                0: inputs, 1: copy_k, 2: copy_v, 3: square_k, 4: copy_q, 5: square_q, 6: copy_qt,
                12: exponential(0), 14: exponential(1), 15: copy_pt(0), 16: copy_ot(0), 18: copy_pt(1), 19: copy_ot(1)})

        @block.gpsimd
        def _(pool):
            def root_ln(t, l):
                pool.wait_ge(s.var_eps, nth(t, l))
                inverse_root(pool, lane[l].rstd[:], lane[l].var_eps[:], m, s.rstd)

            def root_k(t, l):
                pool.wait_ge(s.k_ms, nth(t, l))
                inverse_root(pool, lane[l].kr[:], lane[l].kms[:], m, s.k_r)

            def root_q(t, l):
                pool.wait_ge(s.q_ms, nth(t, l))
                inverse_root(pool, lane[l].r[:], lane[l].ms[:], m, s.q_r)

            staggered(pool, TURNS, LANES, PLACES, {
                -6: root_ln, 4: root_k, 7: root_q})

        @block.vector
        def _(dve):
            dve.memset(gain[:], 0.0).then_inc(s.gzero, 1)
            dve.wait_ge(s.gzero, 1)
            for odd in range(2):
                row = slice(HD * odd, HD * odd + HD)
                dve.tensor_copy(gain[row, odd:odd + 1], m.gqk[row, :]).then_inc(s.gain, 1)
            dve.wait_ge(s.gain, 2)

            def stats(t, l):
                token_stats(dve, m, s, lane[l], t * LANES + l, nth(t, l))

            def normalise(t, l):
                dve.wait_ge(s.rstd, nth(t, l))
                dve.tensor_scalar(lane[l].xn[:], m.x[:, bass.ds((t * LANES + l) * D, D)], lane[l].mv[:, 0:1],
                                  lane[l].rstd[:], ALU.subtract, ALU.mult).then_inc(s.xn, 1)

            def mean_square_k(t, l):
                dve.wait_ge(s.k_sq, nth(t, l))
                dve.tensor_reduce(lane[l].kss[:], lane[l].sq[0:SC].rearrange("p (h e) -> p h e", e=HD), AX.X,
                                  ALU.add).then_inc(s.k_ss, 1)
                dve.wait_ge(s.k_ss, nth(t, l))
                dve.tensor_scalar(lane[l].kms[:], lane[l].kss[:], 1.0 / HD, 1e-6, ALU.mult, ALU.add).then_inc(s.k_ms, 1)

            def scale_k(t, l):
                dve.wait_ge(s.k_r, nth(t, l))
                kn = lane[l].kn[0:SC].rearrange("p (h e) -> p h e", e=HD)
                dve.tensor_tensor(kn, kn, bcast(lane[l].kr[:], HD), ALU.mult).then_inc(s.k_n, 1)

            def mean_square_q(t, l):
                dve.wait_ge(s.q_sq, nth(t, l))
                dve.tensor_reduce(lane[l].ss[:], lane[l].sq[:].rearrange("p (h e) -> p h e", e=HD), AX.X, ALU.add
                                  ).then_inc(s.q_ss, 1)
                dve.wait_ge(s.q_ss, nth(t, l))
                dve.tensor_scalar(lane[l].ms[:], lane[l].ss[:], 1.0 / HD, 1e-6, ALU.mult, ALU.add).then_inc(s.q_ms, 1)

            def mask_k(t, l):
                dve.wait_ge(s.kt_ps, nth(t, l))
                dve.tensor_tensor(lane[l].km[:], ps[l][:].rearrange("p b (j n) -> p (b j) n", n=128)[:, :, 0:SC]
                                  .unsqueeze(2).broadcast_to([128, CH, 2, SC]),
                                  gain[:].unsqueeze(1).unsqueeze(3).broadcast_to([128, CH, 2, SC]), ALU.mult
                                  ).then_inc(s.km, 1)

            def less_maximum(k):
                def step(t, l):
                    mx = lane[l].mx[:, k].rearrange("p (b j) -> p b j", b=2)
                    dve.wait_ge(half[k].s_ps, nth(t, l))
                    dve.tensor_reduce(mx, by_chunk(l, SC), AX.X, ALU.max).then_inc(half[k].s_max, 1)
                    dve.wait_ge(half[k].s_max, nth(t, l))
                    dve.tensor_tensor(lane[l].p[:, k].rearrange("p (b j) n -> p b j n", b=2), by_chunk(l, SC),
                                      mx.unsqueeze(3).broadcast_to([S, 2, 4, SC]), ALU.subtract
                                      ).then_inc(half[k].s_sub, 1)
                return step

            def scale_scores(k):
                def step(t, l):
                    dve.wait_ge(s.q_r, nth(t, l))
                    dve.wait_ge(half[k].s_sub, nth(t, l))
                    dve.tensor_tensor(lane[l].p[:, k], lane[l].p[:, k], bcast(lane[l].r[:, HH * k:HH * k + HH], SC),
                                      ALU.mult).then_inc(half[k].s_q, 1)
                return step

            def normalise_p(k):
                def step(t, l):
                    dve.wait_ge(half[k].e, nth(t, l))
                    dve.tensor_reduce(lane[l].sm[:, k], lane[l].p[:, k], AX.X, ALU.add).then_inc(half[k].sum, 1)
                    dve.wait_ge(half[k].sum, nth(t, l))
                    dve.reciprocal(lane[l].rs[:, k], lane[l].sm[:, k]).then_inc(half[k].rs, 1)
                    dve.wait_ge(half[k].rs, nth(t, l))
                    dve.tensor_tensor(lane[l].p[:, k], lane[l].p[:, k], bcast(lane[l].rs[:, k], SC), ALU.mult
                                      ).then_inc(half[k].p, 1)
                return step

            def residual(t, l):
                xb = m.x[:, bass.ds((t * LANES + l) * D, D)]
                dve.wait_ge(s.y_ps, nth(t, l))
                dve.scalar_tensor_tensor(xb, ps[l][:, 0, 0:D], m.tg[:, 0:1], xb, ALU.mult, ALU.add).then_inc(s.x, 1)

            staggered(dve, TURNS, LANES, PLACES, {
                -6: stats, -3: normalise, 3: mean_square_k, 5: scale_k, 6: mean_square_q, 7: mask_k,
                10: less_maximum(0), 11: scale_scores(0), 12: less_maximum(1), 13: scale_scores(1),
                14: normalise_p(0), 16: normalise_p(1), 20: residual})


@sublayer
def l0_ffn(nc, ctx, m, io):
    E, SE, F = 16, 64, 256
    NS = E * SE
    NC = NS // 128
    LANES = 4
    TURNS = B // LANES
    s = semaphores(nc, ctx, "f0", "w vecs se se_stats se_mv se_ve se_r se_n se_ps gs bs set stats mv var_eps rstd x1 "
                   "stats2 mv2 var_eps2 rstd2 x2 xg xs xst_ps xst lt_ps lt_max lt_neg lt_exp lt_r dt d_ps d "
                   "sl_ps sl l_ps l_max l_neg c ct_ps ct gu_ps gelu h eo_ps eot eoe_ps eo y_ps yr yg free")

    def nth(turn, lane):
        return turn * LANES + lane + 1

    def nth_e(turn, e):
        return turn * E + e + 1

    with ExitStack() as mem:
        def sb(name, shape, dt=F32):
            return mem.enter_context(nc.sbuf_tensor("f0_" + name, shape, dt))

        wg, wu, wd = sb("wg", [D, E, F]), sb("wu", [D, E, F]), sb("wd", [128, E, 2, D])
        bg, bu, bd = sb("bg", [128, E, 2]), sb("bu", [128, E, 2]), sb("bd", [D, E])
        g_row, b_row = sb("g_row", [128, D]), sb("b_row", [128, D])
        slot_g, slot_b, scale = sb("slot_g", [D, 1]), sb("slot_b", [D, 1]), sb("scale", [D, 1])
        gs, bs = sb("gs", [D, 1]), sb("bs", [D, 1])
        set_ = sb("set", [D, NC, 128])
        se_stats, se_mv, se_ve, se_r = (sb("se_stats", [128, NC, 6]), sb("se_mv", [128, NC, 2]), sb("se_ve", [128, NC]),
                                        sb("se_r", [128, NC]))
        d_all = sb("d_all", [128, LANES, NS])
        t_all = sb("t_all", [128, LANES, NC, S])
        sl_all = sb("sl_all", [D, LANES, NS])
        hg = [sb(f"hg{k}", [128, 2, LANES * SE]) for k in range(2)]
        hh = [sb(f"hh{k}", [128, 2, LANES * SE]) for k in range(2)]
        se = d_all[:, 0, :].rearrange("p (c d) -> p c d", d=D)
        lane = [Names(
            stats=sb(f"stats{l}", [S, 6]), mv=sb(f"mv{l}", [S, 2]), var_eps=sb(f"var{l}", [S, 1]),
            rstd=sb(f"rstd{l}", [S, 1]), stats2=sb(f"stats2{l}", [S, 6]), mv2=sb(f"mv2{l}", [S, 2]),
            var_eps2=sb(f"var2{l}", [S, 1]), rstd2=sb(f"rstd2{l}", [S, 1]),
            x1=sb(f"x1{l}", [S, D]), xs=sb(f"xs{l}", [S, D]), xst=sb(f"xst{l}", [D, S]),
            mx=sb(f"mx{l}", [128, NC]), tneg=sb(f"tneg{l}", [128, NC]), sum=sb(f"sum{l}", [128, NC]), r=sb(f"r{l}", [128, NC]),
            cmx=sb(f"cmx{l}", [S, 1]), neg=sb(f"neg{l}", [S, 1]), csum=sb(f"csum{l}", [S, 1]),
            cr=sb(f"cr{l}", [S, 1]), cg=sb(f"cg{l}", [S, 1]),
            t=t_all[:, l], d=d_all[:, l, :], sl=sl_all[:, l, :]) for l in range(LANES)]
        ps = [mem.enter_context(nc.psum_tensor(f"f0_ps{l}", [128, 2, 512], F32)) for l in range(LANES)]
        gate_ps = [ps[2 * k][:, 0, :].rearrange("p (c n) -> p c n", c=2) for k in range(2)]
        up_ps = [ps[2 * k][:, 1, :].rearrange("p (c n) -> p c n", c=2) for k in range(2)]
        eo_ps = [ps[2 * k + 1][:, 0, 0:LANES * SE] for k in range(2)]
        block = mem.enter_context(nc.Block())

        def flat(p):
            return p.rearrange("p b n -> p (b n)")

        @block.sync
        def _(sp):
            sp.dma_start(se, io.slot_embeds.rearrange("e s d -> (e s) d").rearrange("(c p) d -> p c d", p=128)
                         ).then_inc(s.se, 16)
            for dst, src in ((g_row[:], io.norm_g.partition_broadcast(128)), (b_row[:], io.norm_b.partition_broadcast(128)),
                             (slot_g[:], io.slot_g.unsqueeze(1)), (slot_b[:], io.slot_b.unsqueeze(1)),
                             (scale[:], io.scale.partition_broadcast(128))):
                sp.dma_start(dst, src).then_inc(s.vecs, 16)
            for dst, src in ((wg[:], io.Wg), (wu[:], io.Wu), (wd[:], io.Wd), (bg[:], io.bg), (bu[:], io.bu), (bd[:], io.bd)):
                sp.dma_start(dst, src).then_inc(s.w, 16)

        @block.tensor
        def _(pe):
            pe.wait_ge(s.se_n, NC)
            for c in range(NC):
                mm = pe.transpose(ps[0][:, c // 4, c % 4 * 128:c % 4 * 128 + 128], se[:, c, :], m.ident[:])
            mm.then_inc(s.se_ps, 1)
            pe.wait_ge(s.set, 1)
            pe.wait_ge(s.w, 96)
            with pe.Fori(0, TURNS) as t:
                for l in range(LANES):
                    pe.wait_ge(s.xs, nth(t, l))
                    pe.wait_ge(s.free, nth(t, l))
                    pe.transpose(ps[l][:, 0, 0:S], lane[l].xs[:], m.ident[:]).then_inc(s.xst_ps, 1)
                for l in range(LANES):
                    pe.wait_ge(s.xst, nth(t, l))
                    for c in range(NC):
                        mm = pe.matmul(ps[l][:, c // 4, c % 4 * S:c % 4 * S + S], set_[:, c, :], lane[l].xst[:],
                                       start=True, stop=True)
                    mm.then_inc(s.lt_ps, 1)
                for l in range(LANES):
                    pe.wait_ge(s.dt, nth(t, l))
                    for c in range(NC):
                        mm = pe.transpose(ps[l][:, c // 4, c % 4 * 128:c % 4 * 128 + 128], lane[l].t[:, c, :], m.ident[:])
                    mm.then_inc(s.d_ps, 1)
                for l in range(LANES):
                    pe.wait_ge(s.d, nth(t, l))
                    for n in range(2):
                        mm = pe.matmul(ps[l][:, n, :], lane[l].xs[:], lane[l].d[:, 512 * n:512 * n + 512],
                                       start=True, stop=True)
                    mm.then_inc(s.sl_ps, 1)
                for l in range(LANES):
                    pe.wait_ge(s.sl, nth(t, l))
                    for n in range(2):
                        mm = pe.matmul(ps[l][:, n, :], lane[l].xst[:], set_[:, 4 * n:4 * n + 4, :], start=True, stop=True)
                    mm.then_inc(s.l_ps, 1)
                for l in range(LANES):
                    pe.wait_ge(s.c, nth(t, l))
                    for c in range(NC):
                        mm = pe.transpose(ps[l][:, c // 4, c % 4 * S:c % 4 * S + S], lane[l].d[:, 128 * c:128 * c + 128],
                                          m.ident[:])
                    mm.then_inc(s.ct_ps, 1)

                def gate_up(e):
                    k = e % 2
                    if e < 2:
                        pe.wait_ge(s.ct, nth(t, 2 * k + 1))
                    else:
                        pe.wait_ge(s.h, nth_e(t, e - 2))
                    rhs = sl_all[:, :, SE * e:SE * e + SE]
                    for w, out in ((wg, gate_ps[k]), (wu, up_ps[k])):
                        for c in range(2):
                            mm = pe.matmul(out[:, c, :], w[:, e, 128 * c:128 * c + 128], rhs, start=True, stop=True)
                    mm.then_inc(s.gu_ps, 1)

                def down(e):
                    k = e % 2
                    pe.wait_ge(s.h, nth_e(t, e))
                    if e >= 2:
                        pe.wait_ge(s.eot, nth_e(t, e - 2))
                    for c in range(2):
                        mm = pe.matmul(eo_ps[k], wd[:, e, c, :], hh[k][:, c, :], start=(c == 0), stop=(c == 1))
                    mm.then_inc(s.eo_ps, 1)

                gate_up(0)
                for e in range(E):
                    if e + 1 < E:
                        gate_up(e + 1)
                    down(e)
                pe.wait_ge(s.eot, nth_e(t, E - 1))
                for l in range(LANES):
                    for c in range(NC):
                        mm = pe.transpose(ps[l][:, c // 4, c % 4 * 128:c % 4 * 128 + 128],
                                          lane[l].sl[:, 128 * c:128 * c + 128], m.ident[:])
                    mm.then_inc(s.eoe_ps, 1)
                for l in range(LANES):
                    pe.wait_ge(s.eo, nth(t, l))
                    for c in range(NC):
                        mm = pe.matmul(ps[l][:, 0, 0:D], lane[l].t[:, c, :], lane[l].d[:, 128 * c:128 * c + 128],
                                       start=(c == 0), stop=(c == NC - 1))
                    mm.then_inc(s.y_ps, 1)

        @block.scalar
        def _(act):
            with act.Fori(0, TURNS) as t:
                for l in range(LANES):
                    act.wait_ge(s.xst_ps, nth(t, l))
                    act.copy(lane[l].xst[:], ps[l][:, 0, 0:S]).then_inc(s.xst, 1)
                for l in range(LANES):
                    act.wait_ge(s.lt_neg, nth(t, l))
                    for c in range(NC):
                        ex = act.activation(lane[l].t[:, c, :], ps[l][:, c // 4, c % 4 * S:c % 4 * S + S], ACT.Exp,
                                            bias=lane[l].tneg[:, c:c + 1], accum_out=lane[l].sum[:, c:c + 1])
                    ex.then_inc(s.lt_exp, 1)
                for l in range(LANES):
                    act.wait_ge(s.d_ps, nth(t, l))
                    act.copy(lane[l].d, flat(ps[l])).then_inc(s.d, 1)
                for l in range(LANES):
                    act.wait_ge(s.sl_ps, nth(t, l))
                    act.copy(lane[l].sl, flat(ps[l])).then_inc(s.sl, 1)
                for l in range(LANES):
                    act.wait_ge(s.l_neg, nth(t, l))
                    act.activation(lane[l].d, flat(ps[l]), ACT.Exp, bias=lane[l].neg[:], accum_out=lane[l].csum[:]
                                   ).then_inc(s.c, 1)
                for l in range(LANES):
                    act.wait_ge(s.ct_ps, nth(t, l))
                    act.copy(lane[l].t, ps[l][:].rearrange("p b (c n) -> p (b c) n", c=4)).then_inc(s.ct, 1)
                for e in range(E):
                    act.wait_ge(s.gu_ps, nth_e(t, e))
                    for c in range(2):
                        ge = act.activation(hg[e % 2][:, c, :], gate_ps[e % 2][:, c, :], ACT.Gelu, bias=bg[:, e, c:c + 1])
                    ge.then_inc(s.gelu, 1)
                for l in range(LANES):
                    act.wait_ge(s.eoe_ps, nth(t, l))
                    act.copy(lane[l].d, flat(ps[l])).then_inc(s.eo, 1)

        @block.gpsimd
        def _(pool):
            pool.wait_ge(s.se_ve, NC)
            inverse_root(pool, se_r[:], se_ve[:], m, s.se_r)
            with pool.Fori(0, TURNS) as t:
                for l in range(LANES):
                    pool.wait_ge(s.var_eps, nth(t, l))
                    inverse_root(pool, lane[l].rstd[:], lane[l].var_eps[:], m, s.rstd)
                for l in range(LANES):
                    pool.wait_ge(s.var_eps2, nth(t, l))
                    inverse_root(pool, lane[l].rstd2[:], lane[l].var_eps2[:], m, s.rstd2)

        @block.vector
        def _(dve):
            dve.wait_ge(s.se, 16)
            for c in range(NC):
                dve.bn_stats(se_stats[:, c, :], se[:, c, :]).then_inc(s.se_stats, 1)
            for c in range(NC):
                dve.wait_ge(s.se_stats, c + 1)
                dve.bn_aggr(se_mv[:, c, :], se_stats[:, c, :]).then_inc(s.se_mv, 1)
            for c in range(NC):
                dve.wait_ge(s.se_mv, c + 1)
                dve.tensor_scalar(se_ve[:, c:c + 1], se_mv[:, c, 1:2], LN_EPS, None, ALU.add).then_inc(s.se_ve, 1)
            dve.wait_ge(s.vecs, 80)
            dve.tensor_tensor(gs[:], slot_g[:], scale[:], ALU.mult).then_inc(s.gs, 1)
            dve.tensor_tensor(bs[:], slot_b[:], scale[:], ALU.mult).then_inc(s.bs, 1)
            dve.wait_ge(s.se_r, 1)
            for c in range(NC):
                dve.tensor_scalar(se[:, c, :], se[:, c, :], se_mv[:, c, 0:1], se_r[:, c:c + 1], ALU.subtract, ALU.mult
                                  ).then_inc(s.se_n, 1)
            dve.wait_ge(s.se_ps, 1)
            dve.wait_ge(s.gs, 1)
            dve.wait_ge(s.bs, 1)
            dve.tensor_scalar(set_[:].rearrange("p c n -> p (c n)"), flat(ps[0]), gs[:], bs[:], ALU.mult, ALU.add
                              ).then_inc(s.set, 1)
            def first_stats(t):
                layer_norm_stats(dve, m, s, t, lane)

            def first_norm(t):
                for l in range(LANES):
                    dve.wait_ge(s.rstd, nth(t, l))
                    dve.tensor_scalar(lane[l].x1[:], m.x[:, bass.ds((t * LANES + l) * D, D)], lane[l].mv[:, 0:1],
                                      lane[l].rstd[:], ALU.subtract, ALU.mult).then_inc(s.x1, 1)

            def second_stats(t):
                for l in range(LANES):
                    dve.wait_ge(s.x1, nth(t, l))
                    dve.bn_stats(lane[l].stats2[:], lane[l].x1[:]).then_inc(s.stats2, 1)

            def second_variance(t):
                dve.wait_ge(s.stats2, nth(t, LANES - 1))
                dve.memset(m.wait_pad[:], 0.0)
                for l in range(LANES):
                    dve.bn_aggr(lane[l].mv2[:], lane[l].stats2[:]).then_inc(s.mv2, 1)
                for l in range(LANES):
                    dve.wait_ge(s.mv2, nth(t, l))
                    dve.tensor_scalar(lane[l].var_eps2[:], lane[l].mv2[:, 1:2], LN_EPS, None, ALU.add).then_inc(s.var_eps2, 1)

            def second_norm(t):
                for l in range(LANES):
                    dve.wait_ge(s.rstd2, nth(t, l))
                    dve.tensor_scalar(lane[l].x1[:], lane[l].x1[:], lane[l].mv2[:, 0:1], lane[l].rstd2[:],
                                      ALU.subtract, ALU.mult).then_inc(s.x2, 1)

            def times_g(t):
                for l in range(LANES):
                    dve.wait_ge(s.x2, nth(t, l))
                    dve.tensor_tensor(lane[l].x1[:], lane[l].x1[:], g_row[:], ALU.mult).then_inc(s.xg, 1)

            def plus_b(t):
                for l in range(LANES):
                    dve.wait_ge(s.xg, nth(t, l))
                    dve.tensor_tensor(lane[l].xs[:], lane[l].x1[:], b_row[:], ALU.add).then_inc(s.xs, 1)

            norms = (first_stats, first_norm, second_stats, second_variance, second_norm, times_g, plus_b)

            def turn(t, ahead):
                for l in range(LANES):
                    logits = ps[l][:].rearrange("p b (c n) -> p (b c) n", c=4)
                    dve.wait_ge(s.lt_ps, nth(t, l))
                    dve.tensor_reduce(lane[l].mx[:], logits, AX.X, ALU.max).then_inc(s.lt_max, 1)
                    dve.wait_ge(s.lt_max, nth(t, l))
                    dve.tensor_scalar(lane[l].tneg[:], lane[l].mx[:], -1.0, None, ALU.mult).then_inc(s.lt_neg, 1)
                for l in range(LANES):
                    dve.wait_ge(s.lt_exp, nth(t, l))
                    dve.reciprocal(lane[l].r[:], lane[l].sum[:]).then_inc(s.lt_r, 1)
                    dve.wait_ge(s.lt_r, nth(t, l))
                    dve.tensor_tensor(lane[l].t, lane[l].t, bcast(lane[l].r[:], S), ALU.mult).then_inc(s.dt, 1)
                for l in range(LANES):
                    dve.wait_ge(s.l_ps, nth(t, l))
                    dve.tensor_reduce(lane[l].cmx[:], ps[l][:], AX.XY, ALU.max).then_inc(s.l_max, 1)
                    dve.wait_ge(s.l_max, nth(t, l))
                    dve.tensor_scalar(lane[l].neg[:], lane[l].cmx[:], -1.0, None, ALU.mult).then_inc(s.l_neg, 1)

                def hidden(e):
                    k = e % 2
                    dve.wait_ge(s.gelu, nth_e(t, e))
                    if e >= 2:
                        dve.wait_ge(s.eo_ps, nth_e(t, e - 2))
                    for c in range(2):
                        mul = dve.scalar_tensor_tensor(hh[k][:, c, :], up_ps[k][:, c, :], bu[:, e, c:c + 1],
                                                       hg[k][:, c, :], ALU.add, ALU.mult)
                    mul.then_inc(s.h, 1)

                def outputs(e):
                    k = e % 2
                    dve.wait_ge(s.eo_ps, nth_e(t, e))
                    dve.tensor_scalar(sl_all[:, :, SE * e:SE * e + SE], eo_ps[k].rearrange("p (b n) -> p b n", n=SE),
                                      bd[:, e:e + 1], None, ALU.add).then_inc(s.eot, 1)

                hidden(0)
                for e in range(E):
                    if e + 1 < E:
                        hidden(e + 1)
                    outputs(e)
                    if ahead and e % 2 and e // 2 < len(norms):
                        norms[e // 2](t + 1)
                for l in range(LANES):
                    dve.wait_ge(s.c, nth(t, l))
                    dve.reciprocal(lane[l].cr[:], lane[l].csum[:]).then_inc(s.yr, 1)
                for l in range(LANES):
                    dve.wait_ge(s.yr, nth(t, l))
                    dve.tensor_tensor(lane[l].cg[:], lane[l].cr[:], m.tg[:, 4:5], ALU.mult).then_inc(s.yg, 1)
                for l in range(LANES):
                    xb = m.x[:, bass.ds((t * LANES + l) * D, D)]
                    dve.wait_ge(s.yg, nth(t, l))
                    dve.wait_ge(s.y_ps, nth(t, l))
                    dve.scalar_tensor_tensor(xb, ps[l][:, 0, 0:D], lane[l].cg[:], xb, ALU.mult, ALU.add).then_inc(s.free, 1)

            for norm in norms:
                norm(0)
            for l in range(LANES):
                dve.memset(lane[l].cg[:], 0.0).then_inc(s.free, 1)
            with dve.Fori(0, TURNS - 1) as t:
                turn(t, ahead=True)
            turn(TURNS - 1, ahead=False)


@sublayer
def l1_attention(nc, ctx, m, io):
    LANES = 4
    TURNS = B // LANES
    SCALE = D ** -0.5
    s = semaphores(nc, ctx, "a1", "stats mv var_eps rstd xn xt_ps xt qkv_ps qk v s_ps s_max neg p pt_ps pt "
                   "o_ps r g x c0 c1 c2 c3")
    c_in = [s.c0, s.c1, s.c2, s.c3]

    def nth(turn, lane):
        return turn * LANES + lane + 1

    with ExitStack() as mem:
        def sb(name, shape, dt=F32):
            return mem.enter_context(nc.sbuf_tensor("a1_" + name, shape, dt))

        lane = [Names(
            stats=sb(f"stats{l}", [S, 6]), mv=sb(f"mv{l}", [S, 2]), var_eps=sb(f"var{l}", [S, 1]),
            rstd=sb(f"rstd{l}", [S, 1]), xn=sb(f"xn{l}", [S, D]), xt=sb(f"xt{l}", [D, S]),
            c=sb(f"c{l}", [SC, D]), ct=sb(f"ct{l}", [D, SC]), qt=sb(f"qt{l}", [D, S]), kt=sb(f"kt{l}", [D, SC]),
            v=sb(f"v{l}", [SC, D]), mx=sb(f"mx{l}", [S, 1]), neg=sb(f"neg{l}", [S, 1]), p=sb(f"p{l}", [S, SC]),
            sum=sb(f"sum{l}", [S, 1]), r=sb(f"r{l}", [S, 1]), g=sb(f"g{l}", [S, 1]), pt=sb(f"pt{l}", [SC, S]))
            for l in range(LANES)]
        ps = [mem.enter_context(nc.psum_tensor(f"a1_ps{l}", [128, 2, 512], F32)) for l in range(LANES)]
        block = mem.enter_context(nc.Block())

        @block.sync
        def _(sp):
            if m.prefetch_a1:
                m.prefetch_a1(sp)
            load_context(sp, io, s, lane, c_in, TURNS)

        @block.tensor
        def _(pe):
            with pe.Fori(0, TURNS) as t:
                for l in range(LANES):
                    pe.wait_ge(s.xn, nth(t, l))
                    pe.wait_ge(c_in[l], 16 * t + 16)
                    pe.transpose(ps[l][:, 0, 0:S], lane[l].xn[:], m.ident[:])
                    pe.transpose(ps[l][:, 0, S:S + SC], lane[l].c[:], m.ident[0:SC, 0:SC]).then_inc(s.xt_ps, 1)
                for l in range(LANES):
                    pe.wait_ge(s.xt, nth(t, l))
                    pe.matmul(ps[l][:, 1, 0:S], m.wq1[:], lane[l].xt[:], start=True, stop=True)
                    pe.matmul(ps[l][:, 1, S:S + SC], m.wk1[:], lane[l].ct[:], start=True, stop=True)
                    pe.matmul(ps[l][0:SC, 1, 256:256 + D], lane[l].ct[:], m.wv1[:], start=True, stop=False)
                    pe.matmul(ps[l][0:SC, 1, 256:256 + D], m.ones_row[:, 0:SC], m.rows[0:1, m.row_bv1, :],
                              start=False, stop=True).then_inc(s.qkv_ps, 1)
                for l in range(LANES):
                    pe.wait_ge(s.qk, nth(t, l))
                    pe.matmul(ps[l][:, 0, 0:SC], lane[l].qt[:], lane[l].kt[:], start=True, stop=True
                              ).then_inc(s.s_ps, 1)
                for l in range(LANES):
                    pe.wait_ge(s.v, nth(t, l))
                    pe.wait_ge(s.p, nth(t, l))
                    pe.transpose(ps[l][0:SC, 1, 0:S], lane[l].p[:], m.ident[:]).then_inc(s.pt_ps, 1)
                for l in range(LANES):
                    pe.wait_ge(s.pt, nth(t, l))
                    pe.matmul(ps[l][:, 0, 0:D], lane[l].pt[:], lane[l].v[:], start=True, stop=True).then_inc(s.o_ps, 1)

        @block.scalar
        def _(act):
            with act.Fori(0, TURNS) as t:
                for l in range(LANES):
                    act.wait_ge(s.xt_ps, nth(t, l))
                    act.copy(lane[l].xt[:], ps[l][:, 0, 0:S])
                    act.copy(lane[l].ct[:], ps[l][:, 0, S:S + SC]).then_inc(s.xt, 1)
                for l in range(LANES):
                    act.wait_ge(s.qkv_ps, nth(t, l))
                    act.activation(lane[l].qt[:], ps[l][:, 1, 0:S], ACT.Identity, bias=m.bqk1[:, 0:1])
                    act.activation(lane[l].kt[:], ps[l][:, 1, S:S + SC], ACT.Identity, bias=m.bqk1[:, 1:2]
                                   ).then_inc(s.qk, 1)
                for l in range(LANES):
                    act.wait_ge(s.neg, nth(t, l))
                    act.activation(lane[l].p[:], ps[l][:, 0, 0:SC], ACT.Exp, bias=lane[l].neg[:], scale=SCALE,
                                   accum_out=lane[l].sum[:]).then_inc(s.p, 1)
                for l in range(LANES):
                    act.wait_ge(s.pt_ps, nth(t, l))
                    act.copy(lane[l].pt[:], ps[l][0:SC, 1, 0:S]).then_inc(s.pt, 1)

        @block.gpsimd
        def _(pool):
            with pool.Fori(0, TURNS) as t:
                for l in range(LANES):
                    pool.wait_ge(s.var_eps, nth(t, l))
                    inverse_root(pool, lane[l].rstd[:], lane[l].var_eps[:], m, s.rstd)

        @block.vector
        def _(dve):
            with dve.Fori(0, TURNS) as t:
                layer_norm_stats(dve, m, s, t, lane)
                for l in range(LANES):
                    dve.wait_ge(s.rstd, nth(t, l))
                    dve.tensor_scalar(lane[l].xn[:], m.x[:, bass.ds((t * LANES + l) * D, D)], lane[l].mv[:, 0:1],
                                      lane[l].rstd[:], ALU.subtract, ALU.mult).then_inc(s.xn, 1)
                for l in range(LANES):
                    dve.wait_ge(s.qk, nth(t, l))
                    dve.tensor_copy(lane[l].v[:], ps[l][0:SC, 1, 256:256 + D]).then_inc(s.v, 1)
                for l in range(LANES):
                    dve.wait_ge(s.s_ps, nth(t, l))
                    dve.reduce_max(lane[l].mx[:], ps[l][:, 0, 0:SC], AX.X).then_inc(s.s_max, 1)
                for l in range(LANES):
                    dve.wait_ge(s.s_max, nth(t, l))
                    dve.tensor_scalar(lane[l].neg[:], lane[l].mx[:], -SCALE, None, ALU.mult).then_inc(s.neg, 1)
                for l in range(LANES):
                    dve.wait_ge(s.p, nth(t, l))
                    dve.reciprocal(lane[l].r[:], lane[l].sum[:]).then_inc(s.r, 1)
                for l in range(LANES):
                    dve.wait_ge(s.r, nth(t, l))
                    dve.tensor_tensor(lane[l].g[:], lane[l].r[:], m.tg[:, 1:2], ALU.mult).then_inc(s.g, 1)
                for l in range(LANES):
                    xb = m.x[:, bass.ds((t * LANES + l) * D, D)]
                    dve.wait_ge(s.g, nth(t, l))
                    dve.wait_ge(s.o_ps, nth(t, l))
                    dve.scalar_tensor_tensor(xb, ps[l][:, 0, 0:D], lane[l].g[:], xb, ALU.mult, ALU.add
                                             ).then_inc(s.x, 1)
                dve.wait_ge(s.x, nth(t, LANES - 1))


@sublayer
def routed_ffn(nc, ctx, m, io, kind):
    top2 = kind == "top2"
    tag = "f1" if top2 else "f3"
    E = 8
    FC = 2 if top2 else 4
    CAP = B * S // E
    LANES = 4
    TURNS = B // LANES
    GATE = 5 if top2 else 7
    s = semaphores(nc, ctx, tag, "w stats mv var_eps rstd xn xt_ps xt r_ps r top idx sub exp den rden onehot oh2 cnt_ps kept "
                   "wt wt1 total up_ps up h y_ps acc x iota tri one")

    def nth(turn, lane):
        return turn * LANES + lane + 1

    def nth_c(turn, e, c):
        return turn * (E * FC) + e * FC + c + 1

    def nth_e(turn, e):
        return turn * E + e + 1

    with ExitStack() as mem:
        def sb(name, shape, dt=F32):
            return mem.enter_context(nc.sbuf_tensor(f"{tag}_" + name, shape, dt))

        wr = sb("wr", [D, E])
        if top2:
            w1, w2, w3 = sb("w1", [D, E, FC, 128]), sb("w2", [D, E, FC, 128]), sb("w3", [128, E, FC, D])
        else:
            w1, w3 = sb("w1", [D, E, FC, 128]), sb("w3", [128, E, FC, D])
            b1, b2 = sb("b1", [128, E, FC]), sb("b2", [1, E, D])
            total = sb("total", [S, E])
            tri = sb("tri", [S, S])
            ones = sb("ones", [S, S])
        experts = sb("experts", [S, E])
        xt = sb("xt", [D, LANES, S])
        NH = 2 * FC
        act1 = [sb(f"act{k}", [128, LANES * S]) for k in range(NH if not top2 else 2)]
        hid = [sb(f"hid{k}", [128, LANES * S]) for k in range(NH)] if top2 else act1
        acc = sb("acc", [S, LANES, D])
        lane = [Names(
            stats=sb(f"stats{l}", [S, 6]), mv=sb(f"mv{l}", [S, 2]), var_eps=sb(f"var{l}", [S, 1]),
            rstd=sb(f"rstd{l}", [S, 1]), xn=sb(f"xn{l}", [S, D]), r=sb(f"r{l}", [S, E]), top=sb(f"top{l}", [S, 8]),
            idx=sb(f"idx{l}", [S, 8], U32), idxf=sb(f"idxf{l}", [S, 8]), sub=sb(f"sub{l}", [S, E]),
            exp=sb(f"exp{l}", [S, E]), den=sb(f"den{l}", [S, 1]), rden=sb(f"rden{l}", [S, 1]),
            oh=sb(f"oh{l}", [S, E]), oh2=sb(f"oh2{l}", [S, E]), wt=sb(f"wt{l}", [S, E])) for l in range(LANES)]
        misc = mem.enter_context(nc.psum_tensor(f"{tag}_misc", [128, 2, 512], F32))
        up = mem.enter_context(nc.psum_tensor(f"{tag}_up", [128, 4, 512], F32))
        yps = mem.enter_context(nc.psum_tensor(f"{tag}_y", [128, 2, 512], F32))
        block = mem.enter_context(nc.Block())

        @block.sync
        def _(sp):
            loads = [(wr[:], io.router), (w1[:], io.w1), (w3[:], io.w3)]
            loads += [(w2[:], io.w2)] if top2 else [(b1[:], io.b1), (b2[:], io.b2.rearrange("e d -> (e d)").unsqueeze(0).rearrange("a (e d) -> a e d", e=E))]
            for dst, src in loads:
                sp.dma_start(dst, src).then_inc(s.w, 16)

        @block.tensor
        def _(pe):
            pe.wait_ge(s.w, 64 if top2 else 80)
            if not top2:
                pe.wait_ge(s.tri, 1)
            with pe.Fori(0, TURNS) as t:
                for l in range(LANES):
                    pe.wait_ge(s.xn, nth(t, l))
                    pe.transpose(misc[:, 0, S * l:S * l + S], lane[l].xn[:], m.ident[:]).then_inc(s.xt_ps, 1)
                for l in range(LANES):
                    pe.wait_ge(s.xt, t + 1)
                    pe.matmul(misc[:, 1, E * l:E * l + E], xt[:, l, :], wr[:], start=True, stop=True).then_inc(s.r_ps, 1)

                def first(e, c):
                    n = e * FC + c
                    if top2:
                        k = n % 2
                        if n >= 2:
                            pe.wait_ge(s.h, nth_c(t, e, c) - 2)
                        pe.matmul(up[:, 2 * k, :], w1[:, e, c, :], xt[:], start=True, stop=True)
                        pe.matmul(up[:, 2 * k + 1, :], w2[:, e, c, :], xt[:], start=True, stop=True).then_inc(s.up_ps, 1)
                    else:
                        k = n % 4
                        if n >= 4:
                            pe.wait_ge(s.h, nth_c(t, e, c) - 4)
                        pe.matmul(up[:, k, :], w1[:, e, c, :], xt[:], start=True, stop=True).then_inc(s.up_ps, 1)

                def second(e):
                    pe.wait_ge(s.h, nth_c(t, e, FC - 1))
                    if e >= 2:
                        pe.wait_ge(s.acc, nth_e(t, e - 2))
                    for l in range(LANES):
                        for c in range(FC):
                            mm = pe.matmul(yps[:, e % 2, D * l:D * l + D], hid[(e * FC + c) % NH][:, S * l:S * l + S],
                                           w3[:, e, c, :], start=(c == 0), stop=(top2 and c == FC - 1))
                        if not top2:
                            mm = pe.matmul(yps[:, e % 2, D * l:D * l + D], m.ones_row[:], b2[0:1, e, :],
                                           start=False, stop=True)
                    mm.then_inc(s.y_ps, 1)

                for c in range(FC):
                    first(0, c)
                    if not top2:
                        pe.wait_ge(s.onehot, nth(t, c))
                        pe.wait_ge(s.total, nth(t, c))
                        if c:
                            pe.wait_ge(s.kept, nth(t, c - 1))
                        place = misc[:, 1, 64 + E * c:64 + E * c + E]
                        pe.matmul(place, tri[:], lane[c].oh[:], start=True, stop=False)
                        pe.matmul(place, ones[:], total[:], start=False, stop=True).then_inc(s.cnt_ps, 1)
                for e in range(E):
                    if e + 1 < E:
                        for c in range(FC):
                            first(e + 1, c)
                    second(e)

        @block.scalar
        def _(act):
            with act.Fori(0, TURNS) as t:
                act.wait_ge(s.xt_ps, nth(t, LANES - 1))
                act.copy(xt[:], misc[:, 0, :].rearrange("p (l n) -> p l n", n=S)).then_inc(s.xt, 1)
                if not top2:
                    for l in range(LANES):
                        act.wait_ge(s.sub, nth(t, l))
                        act.activation(lane[l].exp[:], lane[l].sub[:], ACT.Exp, accum_out=lane[l].den[:]).then_inc(s.exp, 1)
                else:
                    for l in range(LANES):
                        act.wait_ge(s.sub, nth(t, l))
                        act.activation(lane[l].exp[:, 0:1], lane[l].sub[:, 0:1], ACT.Sigmoid).then_inc(s.exp, 1)
                for n in range(E * FC):
                    e, c = n // FC, n % FC
                    act.wait_ge(s.up_ps, nth_c(t, e, c))
                    if top2:
                        if n >= 2:
                            act.wait_ge(s.h, nth_c(t, e, c) - 2)
                        act.activation(act1[n % 2][:], up[:, 2 * (n % 2), :], ACT.Silu).then_inc(s.up, 1)
                    else:
                        if e >= 2:
                            act.wait_ge(s.y_ps, nth_e(t, e - 2))
                        act.activation(act1[n % NH][:], up[:, n % 4, :], ACT.Relu, bias=b1[:, e, c:c + 1]).then_inc(s.h, 1)

        @block.gpsimd
        def _(pool):
            pool.iota(experts[:], [[1, E]], base=0, channel_multiplier=0, allow_small_or_imprecise_dtypes=True
                      ).then_inc(s.iota, 1)
            if not top2:
                pool.memset(ones[:], 1.0).then_inc(s.one, 1)
                pool.wait_ge(s.one, 1)
                pool.affine_select(tri[:], ones[:], [[1, S]], ALU.is_ge, 0.0, 0, -1).then_inc(s.tri, 1)
            with pool.Fori(0, TURNS) as t:
                for l in range(LANES):
                    pool.wait_ge(s.var_eps, nth(t, l))
                    inverse_root(pool, lane[l].rstd[:], lane[l].var_eps[:], m, s.rstd)

        @block.vector
        def _(dve):
            dve.wait_ge(s.iota, 1)
            if not top2:
                dve.memset(total[:], 0.0).then_inc(s.total, 1)
            with dve.Fori(0, TURNS) as t:
                layer_norm_stats(dve, m, s, t, lane)
                for l in range(LANES):
                    dve.wait_ge(s.rstd, nth(t, l))
                    dve.tensor_scalar(lane[l].xn[:], m.x[:, bass.ds((t * LANES + l) * D, D)], lane[l].mv[:, 0:1],
                                      lane[l].rstd[:], ALU.subtract, ALU.mult).then_inc(s.xn, 1)
                for l in range(LANES):
                    dve.wait_ge(s.r_ps, nth(t, LANES - 1))
                    dve.tensor_copy(lane[l].r[:], misc[:, 1, E * l:E * l + E]).then_inc(s.r, 1)
                dve.wait_ge(s.r, nth(t, LANES - 1))
                dve.memset(m.wait_pad[:], 0.0)
                for l in range(LANES):
                    dve.max(lane[l].top[:], lane[l].r[:]).then_inc(s.top, 1)
                dve.wait_ge(s.top, nth(t, LANES - 1))
                dve.memset(m.wait_pad[:], 0.0)
                for l in range(LANES):
                    dve.max_index(lane[l].idx[:], lane[l].top[:], lane[l].r[:]).then_inc(s.idx, 1)
                for l in range(LANES):
                    if top2:
                        dve.tensor_scalar(lane[l].sub[:, 0:1], lane[l].top[:, 0:1], lane[l].top[:, 1:2], None,
                                          ALU.subtract).then_inc(s.sub, 1)
                    else:
                        dve.tensor_scalar(lane[l].sub[:], lane[l].r[:], lane[l].top[:, 0:1], None, ALU.subtract
                                          ).then_inc(s.sub, 1)
                for l in range(LANES):
                    dve.wait_ge(s.idx, nth(t, l))
                    dve.tensor_copy(lane[l].idxf[:], lane[l].idx[:]).then_inc(s.oh2, 1)
                for l in range(LANES):
                    dve.wait_ge(s.oh2, nth(t, l))
                    dve.tensor_scalar(lane[l].oh[:], experts[:], lane[l].idxf[:, 0:1], None, ALU.is_equal
                                      ).then_inc(s.onehot, 1)
                if top2:
                    for l in range(LANES):
                        dve.wait_ge(s.exp, nth(t, l))
                        dve.tensor_scalar(lane[l].exp[:, 1:2], lane[l].exp[:, 0:1], -1.0, 1.0, ALU.mult, ALU.add
                                          ).then_inc(s.den, 1)
                    for l in range(LANES):
                        dve.wait_ge(s.den, nth(t, l))
                        dve.tensor_scalar(lane[l].oh2[:], experts[:], lane[l].idxf[:, 1:2], lane[l].exp[:, 1:2],
                                          ALU.is_equal, ALU.mult).then_inc(s.wt1, 1)
                    for l in range(LANES):
                        dve.wait_ge(s.onehot, nth(t, l))
                        dve.wait_ge(s.wt1, nth(t, l))
                        dve.scalar_tensor_tensor(lane[l].wt[:], lane[l].oh[:], lane[l].exp[:, 0:1], lane[l].oh2[:],
                                                 ALU.mult, ALU.add).then_inc(s.wt, 1)
                else:
                    for l in range(LANES):
                        dve.wait_ge(s.exp, nth(t, l))
                        dve.reciprocal(lane[l].rden[:], lane[l].den[:]).then_inc(s.rden, 1)
                    for l in range(LANES):
                        dve.wait_ge(s.cnt_ps, nth(t, l))
                        dve.wait_ge(s.onehot, nth(t, l))
                        dve.tensor_tensor(total[:], total[:], lane[l].oh[:], ALU.add).then_inc(s.total, 1)
                        dve.scalar_tensor_tensor(lane[l].oh2[:], misc[:, 1, 64 + E * l:64 + E * l + E], float(CAP),
                                                 lane[l].oh[:], ALU.is_le, ALU.mult).then_inc(s.kept, 1)
                    for l in range(LANES):
                        dve.wait_ge(s.rden, nth(t, l))
                        dve.wait_ge(s.kept, nth(t, l))
                        dve.tensor_scalar(lane[l].wt[:], lane[l].oh2[:], lane[l].rden[:], None, ALU.mult).then_inc(s.wt, 1)

                def product(n):
                    e, c = n // FC, n % FC
                    dve.wait_ge(s.up, nth_c(t, e, c))
                    if e >= 2:
                        dve.wait_ge(s.y_ps, nth_e(t, e - 2))
                    dve.tensor_tensor(hid[n % NH][:], act1[n % 2][:], up[:, 2 * (n % 2) + 1, :], ALU.mult).then_inc(s.h, 1)

                def add(e):
                    dve.wait_ge(s.y_ps, nth_e(t, e))
                    if e == 0:
                        dve.wait_ge(s.wt, nth(t, LANES - 1))
                    else:
                        dve.wait_ge(s.acc, nth_e(t, e - 1))
                    for l in range(LANES):
                        y = yps[:, e % 2, D * l:D * l + D]
                        if e == 0:
                            a = dve.tensor_scalar(acc[:, l, :], y, lane[l].wt[:, 0:1], None, ALU.mult)
                        else:
                            a = dve.scalar_tensor_tensor(acc[:, l, :], y, lane[l].wt[:, e:e + 1], acc[:, l, :],
                                                         ALU.mult, ALU.add)
                    a.then_inc(s.acc, 1)

                for e in range(E):
                    if top2:
                        for c in range(FC):
                            product(e * FC + c)
                    if e:
                        add(e - 1)
                add(E - 1)
                dve.wait_ge(s.acc, nth_e(t, E - 1))
                xg = m.x[:, bass.ds(t * (LANES * D), LANES * D)]
                dve.scalar_tensor_tensor(xg, acc[:].rearrange("p l d -> p (l d)"), m.tg[:, GATE:GATE + 1], xg,
                                         ALU.mult, ALU.add).then_inc(s.x, 1)
                dve.wait_ge(s.x, t + 1)


@sublayer
def l2_attention(nc, ctx, m, io):
    H, HD = 16, 8
    HH = H // 2
    SK = SC + S
    ROWS = HH * (HD + 1)
    LANES = 4
    TURNS = B // LANES
    PLACES = 24
    s = semaphores(nc, ctx, "a2", "stats mv var_eps rstd xn xt_ps xt v_ps k_ps v km at_ps at y_ps x c0 c1 c2 c3 zeros ones")
    c_in = [s.c0, s.c1, s.c2, s.c3]
    unit = [semaphores(nc, ctx, f"a2u{u}", "s_ps s_max s_sub p") for u in range(4)]
    half = [semaphores(nc, ctx, f"a2h{k}", "ptc_ps ptc ptx_ps ptx ot_ps ot o_ps o_r o") for k in range(2)]

    def nth(turn, lane):
        return turn * LANES + lane + 1

    def head_of(i):
        u, qq, jj = i // 4, i // 2 % 2, i % 2
        return 4 * (2 * (u // 2) + qq) + 2 * (u % 2) + jj

    with ExitStack() as mem:
        def sb(name, shape, dt=F32):
            return mem.enter_context(nc.sbuf_tensor("a2_" + name, shape, dt))

        lane = [Names(
            stats=sb(f"stats{l}", [S, 6]), mv=sb(f"mv{l}", [S, 2]), var_eps=sb(f"var{l}", [S, 1]),
            rstd=sb(f"rstd{l}", [S, 1]), xn=sb(f"xn{l}", [S, D]), xct=sb(f"xct{l}", [D, SK]),
            c=sb(f"c{l}", [SC, D]), qt=sb(f"qt{l}", [D, S]), km=sb(f"km{l}", [D, 4, SK]),
            vc=sb(f"vc{l}", [SC, 2, HH * (ROWS + HD + 1)]), vx=sb(f"vx{l}", [S, 2, HH * (ROWS + HD + 1)]),
            ou=sb(f"ou{l}", [ROWS, S]),
            mx=sb(f"mx{l}", [S, H]), p=sb(f"p{l}", [S, H, SK]),
            ptc=sb(f"ptc{l}", [SC, HH, S]), ptx=sb(f"ptx{l}", [S, HH, S]),
            rs=sb(f"rs{l}", [S, H]), o=sb(f"o{l}", [S, D]), ot=sb(f"ot{l}", [D, S])) for l in range(LANES)]
        ps = [mem.enter_context(nc.psum_tensor(f"a2_ps{l}", [128, 2, 512], F32)) for l in range(LANES)]
        block = mem.enter_context(nc.Block())

        def own_columns(v):
            return v[:].rearrange("p k (a m) -> p k a m", m=ROWS + HD + 1)[:, :, :, 0:HD + 1]

        @block.sync
        def _(sp):
            if m.prefetch_a2:
                m.prefetch_a2(sp)
            load_context(sp, io, s, lane, c_in, TURNS)

        @block.tensor
        def _(pe):
            def inputs(t, l):
                pe.wait_ge(s.xn, nth(t, l))
                pe.wait_ge(c_in[l], 16 * t + 16)
                pe.transpose(ps[l][:, 0, 0:SC], lane[l].c[:], m.ident[0:SC, 0:SC])
                pe.transpose(ps[l][:, 0, SC:SK], lane[l].xn[:], m.ident[:]).then_inc(s.xt_ps, 1)

            def project(t, l):
                pe.wait_ge(s.xt, nth(t, l))
                pe.matmul(ps[l][:, 1, 0:SK], m.wkv2[:, 0:D], lane[l].xct[:], start=True, stop=True).then_inc(s.k_ps, 1)
                pe.matmul(ps[l][:, 0, 0:S], m.wq2[:], lane[l].xct[:, SC:SK], start=True, stop=True)
                pe.matmul(ps[l][0:SC, 0, D:2 * D], lane[l].xct[:, 0:SC], m.wkv2[:, D:2 * D], start=True, stop=True)
                pe.matmul(ps[l][:, 0, 2 * D:3 * D], lane[l].xct[:, SC:SK], m.wkv2[:, D:2 * D], start=True, stop=True
                          ).then_inc(s.v_ps, 1)

            def scores(u):
                def step(t, l):
                    if u == 0:
                        pe.wait_ge(s.km, nth(t, l))
                        pe.wait_ge(s.v, nth(t, l))
                    else:
                        pe.wait_ge(unit[u - 1].s_sub, nth(t, l))
                    for qq in range(2):
                        pe.matmul(ps[l][:, qq, :].rearrange("p (j n) -> p j n", n=256)[:, :, 0:SK], m.identb[:],
                                  m.causal[:].unsqueeze(1).broadcast_to([S, 2, SK]), start=True, stop=False)
                    for qq in range(2):
                        quad = 2 * (u // 2) + qq
                        row = slice(32 * quad, 32 * quad + 32)
                        mm = pe.matmul(ps[l][:, qq, :].rearrange("p (j n) -> p j n", n=256)[:, :, 0:SK],
                                       lane[l].qt[row, :], lane[l].km[row, 2 * (u % 2):2 * (u % 2) + 2, :],
                                       start=False, stop=True)
                    mm.then_inc(unit[u].s_ps, 1)
                return step

            def transpose_pc(k):
                def step(t, l):
                    pe.wait_ge(unit[2 * k + 1].p, nth(t, l))
                    if k == 0:
                        pe.wait_ge(unit[3].s_sub, nth(t, l))
                    else:
                        pe.wait_ge(half[0].o, nth(t, l))
                    for i in range(HH):
                        mm = pe.transpose(ps[l][0:SC, i // 4, i % 4 * S:i % 4 * S + S], lane[l].p[:, HH * k + i, 0:SC],
                                          m.ident[:])
                    mm.then_inc(half[k].ptc_ps, 1)
                return step

            def transpose_px(k):
                def step(t, l):
                    pe.wait_ge(half[k].ptc, nth(t, l))
                    for i in range(HH):
                        mm = pe.transpose(ps[l][:, i // 4, i % 4 * S:i % 4 * S + S], lane[l].p[:, HH * k + i, SC:SK],
                                          m.ident[:])
                    mm.then_inc(half[k].ptx_ps, 1)
                return step

            def mix_v(k):
                def step(t, l):
                    pe.wait_ge(half[k].ptx, nth(t, l))
                    for i in range(HH):
                        a = head_of(HH * k + i) - HH * k
                        pe.matmul(ps[l][0:ROWS, 0, 0:S], lane[l].vc[:, k, ROWS * a:ROWS * a + ROWS], lane[l].ptc[:, i, :],
                                  start=(i == 0), stop=False)
                        mm = pe.matmul(ps[l][0:ROWS, 0, 0:S], lane[l].vx[:, k, ROWS * a:ROWS * a + ROWS],
                                       lane[l].ptx[:, i, :], start=False, stop=(i == HH - 1))
                    mm.then_inc(half[k].ot_ps, 1)
                return step

            def tokens_first(k):
                def step(t, l):
                    pe.wait_ge(half[k].ot, nth(t, l))
                    pe.transpose(ps[l][:, 1, 0:ROWS], lane[l].ou[:], m.ident[0:ROWS, 0:ROWS]).then_inc(half[k].o_ps, 1)
                return step

            def transpose_o(t, l):
                pe.wait_ge(half[1].o, nth(t, l))
                pe.transpose(ps[l][:, 0, 0:S], lane[l].o[:], m.ident[:]).then_inc(s.at_ps, 1)

            def project_o(t, l):
                pe.wait_ge(s.at, nth(t, l))
                pe.matmul(ps[l][:, 1, 0:D], lane[l].ot[:], m.wout2[:], start=True, stop=False)
                pe.matmul(ps[l][:, 1, 0:D], m.ones_row[:], m.rows[0:1, m.row_bout2, :], start=False, stop=True
                          ).then_inc(s.y_ps, 1)

            staggered(pe, TURNS, LANES, PLACES, {
                0: inputs, 1: project, 3: scores(0), 5: scores(1), 6: scores(2), 8: scores(3),
                10: transpose_pc(0), 11: transpose_px(0), 12: mix_v(0), 13: tokens_first(0),
                15: transpose_pc(1), 16: transpose_px(1), 17: mix_v(1), 18: tokens_first(1),
                20: transpose_o, 21: project_o})

        @block.scalar
        def _(act):
            def inputs(t, l):
                act.wait_ge(s.xt_ps, nth(t, l))
                act.copy(lane[l].xct[:], ps[l][:, 0, 0:SK]).then_inc(s.xt, 1)

            def copy_qv(t, l):
                act.wait_ge(s.v_ps, nth(t, l))
                act.copy(lane[l].qt[:], ps[l][:, 0, 0:S])
                act.copy(own_columns(lane[l].vc)[:, :, :, 0:HD],
                         ps[l][0:SC, 0, D:2 * D].rearrange("p (k a e) -> p k a e", k=2, e=HD))
                act.copy(own_columns(lane[l].vx)[:, :, :, 0:HD],
                         ps[l][:, 0, 2 * D:3 * D].rearrange("p (k a e) -> p k a e", k=2, e=HD)).then_inc(s.v, 1)

            def exponential(u):
                def step(t, l):
                    part = lane[l].p[:, 4 * u:4 * u + 4, :]
                    act.wait_ge(unit[u].s_sub, nth(t, l))
                    act.activation(part, part, ACT.Exp, scale=HD ** -0.5).then_inc(unit[u].p, 1)
                return step

            def copy_pc(k):
                def step(t, l):
                    act.wait_ge(half[k].ptc_ps, nth(t, l))
                    act.copy(lane[l].ptc[:], ps[l][0:SC, :, :].rearrange("p b (j q) -> p (b j) q", q=S)
                             ).then_inc(half[k].ptc, 1)
                return step

            def copy_px(k):
                def step(t, l):
                    act.wait_ge(half[k].ptx_ps, nth(t, l))
                    act.copy(lane[l].ptx[:], ps[l][:, :, :].rearrange("p b (j q) -> p (b j) q", q=S)
                             ).then_inc(half[k].ptx, 1)
                return step

            def copy_o(k):
                def step(t, l):
                    act.wait_ge(half[k].ot_ps, nth(t, l))
                    act.copy(lane[l].ou[:], ps[l][0:ROWS, 0, 0:S]).then_inc(half[k].ot, 1)
                return step

            def copy_ot(t, l):
                act.wait_ge(s.at_ps, nth(t, l))
                act.copy(lane[l].ot[:], ps[l][:, 0, 0:S]).then_inc(s.at, 1)

            staggered(act, TURNS, LANES, PLACES, {
                0: inputs, 1: copy_qv, 4: exponential(0), 6: exponential(1), 7: exponential(2), 9: exponential(3),
                10: copy_pc(0), 11: copy_px(0), 12: copy_o(0),
                15: copy_pc(1), 16: copy_px(1), 17: copy_o(1), 20: copy_ot})

        @block.gpsimd
        def _(pool):
            def root_ln(t, l):
                pool.wait_ge(s.var_eps, nth(t, l))
                inverse_root(pool, lane[l].rstd[:], lane[l].var_eps[:], m, s.rstd)

            staggered(pool, TURNS, LANES, PLACES, {
                -3: root_ln})

        @block.vector
        def _(dve):
            for l in range(LANES):
                dve.memset(lane[l].vc[:], 0.0).then_inc(s.zeros, 1)
                dve.memset(lane[l].vx[:], 0.0).then_inc(s.zeros, 1)
            dve.wait_ge(s.zeros, 2 * LANES)
            for l in range(LANES):
                dve.memset(own_columns(lane[l].vc)[:, :, :, HD:HD + 1], 1.0).then_inc(s.ones, 1)
                dve.memset(own_columns(lane[l].vx)[:, :, :, HD:HD + 1], 1.0).then_inc(s.ones, 1)
            dve.wait_ge(s.ones, 2 * LANES)

            def stats(t, l):
                token_stats(dve, m, s, lane[l], t * LANES + l, nth(t, l))

            def normalise(t, l):
                dve.wait_ge(s.rstd, nth(t, l))
                dve.tensor_scalar(lane[l].xn[:], m.x[:, bass.ds((t * LANES + l) * D, D)], lane[l].mv[:, 0:1],
                                  lane[l].rstd[:], ALU.subtract, ALU.mult).then_inc(s.xn, 1)

            def mask_k(t, l):
                dve.wait_ge(s.k_ps, nth(t, l))
                dve.tensor_tensor(lane[l].km[:], ps[l][:, 1, 0:SK].unsqueeze(1).broadcast_to([D, 4, SK]),
                                  bcast(m.headmask[:], SK), ALU.mult).then_inc(s.km, 1)

            def less_maximum(u):
                def step(t, l):
                    scores = ps[l][:, :, :].rearrange("p b (j n) -> p b j n", n=256)[:, :, :, 0:SK]
                    mx = lane[l].mx[:, 4 * u:4 * u + 4].rearrange("p (b j) -> p b j", j=2)
                    dve.wait_ge(unit[u].s_ps, nth(t, l))
                    dve.tensor_reduce(mx, scores, AX.X, ALU.max).then_inc(unit[u].s_max, 1)
                    dve.wait_ge(unit[u].s_max, nth(t, l))
                    dve.tensor_tensor(lane[l].p[:, 4 * u:4 * u + 4, :].rearrange("p (b j) n -> p b j n", j=2),
                                      scores, mx.unsqueeze(3).broadcast_to([S, 2, 2, SK]), ALU.subtract
                                      ).then_inc(unit[u].s_sub, 1)
                return step

            def divide(k):
                def step(t, l):
                    out = ps[l][:, 1, 0:ROWS].rearrange("p (h e) -> p h e", e=HD + 1)
                    rs = lane[l].rs[:, HH * k:HH * k + HH]
                    dve.wait_ge(half[k].o_ps, nth(t, l))
                    dve.reciprocal(rs, out[:, :, HD]).then_inc(half[k].o_r, 1)
                    dve.wait_ge(half[k].o_r, nth(t, l))
                    dve.tensor_tensor(lane[l].o[:, HH * HD * k:HH * HD * (k + 1)].rearrange("p (h e) -> p h e", e=HD),
                                      out[:, :, 0:HD], bcast(rs, HD), ALU.mult).then_inc(half[k].o, 1)
                return step

            def residual(t, l):
                xb = m.x[:, bass.ds((t * LANES + l) * D, D)]
                dve.wait_ge(s.y_ps, nth(t, l))
                dve.scalar_tensor_tensor(xb, ps[l][:, 1, 0:D], m.tg[:, 2:3], xb, ALU.mult, ALU.add).then_inc(s.x, 1)

            staggered(dve, TURNS, LANES, PLACES, {
                -3: stats, -1: normalise, 1: mask_k,
                3: less_maximum(0), 5: less_maximum(1), 6: less_maximum(2), 8: less_maximum(3),
                13: divide(0), 18: divide(1), 21: residual})


@sublayer
def l3_attention(nc, ctx, m, io):
    H, HD = 16, 8
    HH = H // 2
    ROWS = HH * (HD + 1)
    LANES = 4
    TURNS = B // LANES
    PLACES = 20
    s = semaphores(nc, ctx, "a3", "stats mv var_eps rstd xn xt_ps xt k_ps km qv_ps v at_ps at y_ps x "
                   "c0 c1 c2 c3 zeros ones")
    c_in = [s.c0, s.c1, s.c2, s.c3]
    half = [semaphores(nc, ctx, f"a3h{k}", "s_ps s_max s_sub p pt_ps pt ot_ps ot o_ps o_r o") for k in range(2)]

    def nth(turn, lane):
        return turn * LANES + lane + 1

    with ExitStack() as mem:
        def sb(name, shape, dt=F32):
            return mem.enter_context(nc.sbuf_tensor("a3_" + name, shape, dt))

        lane = [Names(
            stats=sb(f"stats{l}", [S, 6]), mv=sb(f"mv{l}", [S, 2]), var_eps=sb(f"var{l}", [S, 1]),
            rstd=sb(f"rstd{l}", [S, 1]), xn=sb(f"xn{l}", [S, D]), xt=sb(f"xt{l}", [D, S]), ct=sb(f"ct{l}", [D, SC]),
            c=sb(f"c{l}", [SC, D]), qt=sb(f"qt{l}", [D, S]), km=sb(f"km{l}", [D, 4, SC]), ou=sb(f"ou{l}", [ROWS, S]),
            v=sb(f"v{l}", [SC, 2, HH * (ROWS + HD + 1)]), mx=sb(f"mx{l}", [S, H]), p=sb(f"p{l}", [S, H, SC]),
            pt=sb(f"pt{l}", [SC, HH, S]), rs=sb(f"rs{l}", [S, H]), o=sb(f"o{l}", [S, D]), ot=sb(f"ot{l}", [D, S]))
            for l in range(LANES)]
        ps = [mem.enter_context(nc.psum_tensor(f"a3_ps{l}", [128, 2, 512], F32)) for l in range(LANES)]
        block = mem.enter_context(nc.Block())

        def own_columns(v):
            return v[:].rearrange("p k (a m) -> p k a m", m=ROWS + HD + 1)[:, :, :, 0:HD + 1]

        @block.sync
        def _(sp):
            load_context(sp, io, s, lane, c_in, TURNS)

        @block.tensor
        def _(pe):
            def inputs(t, l):
                pe.wait_ge(s.xn, nth(t, l))
                pe.wait_ge(c_in[l], 16 * t + 16)
                pe.transpose(ps[l][:, 0, 0:S], lane[l].xn[:], m.ident[:])
                pe.transpose(ps[l][:, 0, S:S + SC], lane[l].c[:], m.ident[0:SC, 0:SC]).then_inc(s.xt_ps, 1)

            def project(t, l):
                pe.wait_ge(s.xt, nth(t, l))
                pe.matmul(ps[l][:, 1, 0:SC], m.wk3[:], lane[l].ct[:], start=True, stop=True).then_inc(s.k_ps, 1)
                pe.matmul(ps[l][:, 0, 0:S], m.wq3[:], lane[l].xt[:], start=True, stop=True)
                pe.matmul(ps[l][0:SC, 0, S:S + D], lane[l].ct[:], m.wv3[:], start=True, stop=False)
                pe.matmul(ps[l][0:SC, 0, S:S + D], m.ones_row[:, 0:SC], m.rows[0:1, m.row_bv3, :],
                          start=False, stop=True).then_inc(s.qv_ps, 1)

            def scores(k):
                def step(t, l):
                    if k == 0:
                        pe.wait_ge(s.km, nth(t, l))
                        pe.wait_ge(s.v, nth(t, l))
                    else:
                        pe.wait_ge(half[0].s_sub, nth(t, l))
                    for qq in range(2):
                        pe.matmul(ps[l][:, qq, 0:4 * SC].rearrange("p (j n) -> p j n", n=SC), m.first_row[:],
                                  m.maskneg[:, bass.ds((t * LANES + l) * SC, SC)].unsqueeze(1).broadcast_to([D, 4, SC]),
                                  start=True, stop=False)
                    for qq in range(2):
                        row = slice(32 * (2 * k + qq), 32 * (2 * k + qq) + 32)
                        mm = pe.matmul(ps[l][:, qq, 0:4 * SC].rearrange("p (j n) -> p j n", n=SC), lane[l].qt[row, :],
                                       lane[l].km[row, :, :], start=False, stop=True)
                    mm.then_inc(half[k].s_ps, 1)
                return step

            def transpose_p(k):
                def step(t, l):
                    pe.wait_ge(half[k].p, nth(t, l))
                    if k == 0:
                        pe.wait_ge(half[1].s_sub, nth(t, l))
                    else:
                        pe.wait_ge(half[0].o, nth(t, l))
                    for i in range(HH):
                        mm = pe.transpose(ps[l][0:SC, i // 4, i % 4 * S:i % 4 * S + S], lane[l].p[:, HH * k + i, :],
                                          m.ident[:])
                    mm.then_inc(half[k].pt_ps, 1)
                return step

            def mix_v(k):
                def step(t, l):
                    pe.wait_ge(half[k].pt, nth(t, l))
                    for i in range(HH):
                        mm = pe.matmul(ps[l][0:ROWS, 0, 0:S], lane[l].v[:, k, ROWS * i:ROWS * i + ROWS],
                                       lane[l].pt[:, i, :], start=(i == 0), stop=(i == HH - 1))
                    mm.then_inc(half[k].ot_ps, 1)
                return step

            def tokens_first(k):
                def step(t, l):
                    pe.wait_ge(half[k].ot, nth(t, l))
                    pe.transpose(ps[l][:, 1, 0:ROWS], lane[l].ou[:], m.ident[0:ROWS, 0:ROWS]).then_inc(half[k].o_ps, 1)
                return step

            def transpose_o(t, l):
                pe.wait_ge(half[1].o, nth(t, l))
                pe.transpose(ps[l][:, 0, 0:S], lane[l].o[:], m.ident[:]).then_inc(s.at_ps, 1)

            def project_o(t, l):
                pe.wait_ge(s.at, nth(t, l))
                pe.matmul(ps[l][:, 1, 0:D], lane[l].ot[:], m.wo3[:], start=True, stop=False)
                pe.matmul(ps[l][:, 1, 0:D], m.ones_row[:], m.rows[0:1, m.row_bo3, :], start=False, stop=True
                          ).then_inc(s.y_ps, 1)

            staggered(pe, TURNS, LANES, PLACES, {
                0: inputs, 1: project, 4: scores(0), 7: scores(1),
                9: transpose_p(0), 10: mix_v(0), 11: tokens_first(0),
                13: transpose_p(1), 14: mix_v(1), 15: tokens_first(1), 16: transpose_o, 17: project_o})

        @block.scalar
        def _(act):
            def inputs(t, l):
                act.wait_ge(s.xt_ps, nth(t, l))
                act.copy(lane[l].xt[:], ps[l][:, 0, 0:S])
                act.copy(lane[l].ct[:], ps[l][:, 0, S:S + SC]).then_inc(s.xt, 1)

            def copy_qv(t, l):
                act.wait_ge(s.qv_ps, nth(t, l))
                act.activation(lane[l].qt[:], ps[l][:, 0, 0:S], ACT.Identity, bias=m.bqk3[:, 0:1])
                act.copy(own_columns(lane[l].v)[:, :, :, 0:HD],
                         ps[l][0:SC, 0, S:S + D].rearrange("p (k a e) -> p k a e", k=2, e=HD)).then_inc(s.v, 1)

            def exponential(k):
                def step(t, l):
                    part = lane[l].p[:, HH * k:HH * k + HH, :]
                    act.wait_ge(half[k].s_sub, nth(t, l))
                    act.activation(part, part, ACT.Exp, scale=HD ** -0.5).then_inc(half[k].p, 1)
                return step

            def copy_pt(k):
                def step(t, l):
                    act.wait_ge(half[k].pt_ps, nth(t, l))
                    act.copy(lane[l].pt[:], ps[l][0:SC, :, :].rearrange("p b (j q) -> p (b j) q", q=S)
                             ).then_inc(half[k].pt, 1)
                return step

            def copy_o(k):
                def step(t, l):
                    act.wait_ge(half[k].ot_ps, nth(t, l))
                    act.copy(lane[l].ou[:], ps[l][0:ROWS, 0, 0:S]).then_inc(half[k].ot, 1)
                return step

            def copy_ot(t, l):
                act.wait_ge(s.at_ps, nth(t, l))
                act.copy(lane[l].ot[:], ps[l][:, 0, 0:S]).then_inc(s.at, 1)

            staggered(act, TURNS, LANES, PLACES, {
                0: inputs, 1: copy_qv, 5: exponential(0), 8: exponential(1),
                9: copy_pt(0), 10: copy_o(0), 13: copy_pt(1), 14: copy_o(1), 16: copy_ot})

        @block.gpsimd
        def _(pool):
            def root_ln(t, l):
                pool.wait_ge(s.var_eps, nth(t, l))
                inverse_root(pool, lane[l].rstd[:], lane[l].var_eps[:], m, s.rstd)

            staggered(pool, TURNS, LANES, PLACES, {
                -3: root_ln})

        @block.vector
        def _(dve):
            for l in range(LANES):
                dve.memset(lane[l].v[:], 0.0).then_inc(s.zeros, 1)
            dve.wait_ge(s.zeros, LANES)
            for l in range(LANES):
                dve.memset(own_columns(lane[l].v)[:, :, :, HD:HD + 1], 1.0).then_inc(s.ones, 1)
            dve.wait_ge(s.ones, LANES)

            def stats(t, l):
                token_stats(dve, m, s, lane[l], t * LANES + l, nth(t, l))

            def normalise(t, l):
                dve.wait_ge(s.rstd, nth(t, l))
                dve.tensor_scalar(lane[l].xn[:], m.x[:, bass.ds((t * LANES + l) * D, D)], lane[l].mv[:, 0:1],
                                  lane[l].rstd[:], ALU.subtract, ALU.mult).then_inc(s.xn, 1)

            def mask_k(t, l):
                dve.wait_ge(s.k_ps, nth(t, l))
                dve.scalar_tensor_tensor(lane[l].km[:], ps[l][:, 1, 0:SC].unsqueeze(1).broadcast_to([D, 4, SC]),
                                         m.bqk3[:, 1:2], bcast(m.headmask[:], SC), ALU.add, ALU.mult).then_inc(s.km, 1)

            def less_maximum(k):
                def step(t, l):
                    scores = ps[l][:, :, 0:4 * SC].rearrange("p b (j n) -> p b j n", n=SC)
                    mx = lane[l].mx[:, HH * k:HH * k + HH].rearrange("p (b j) -> p b j", j=4)
                    dve.wait_ge(half[k].s_ps, nth(t, l))
                    dve.tensor_reduce(mx, scores, AX.X, ALU.max).then_inc(half[k].s_max, 1)
                    dve.wait_ge(half[k].s_max, nth(t, l))
                    dve.tensor_tensor(lane[l].p[:, HH * k:HH * k + HH, :].rearrange("p (b j) n -> p b j n", j=4), scores,
                                      mx.unsqueeze(3).broadcast_to([S, 2, 4, SC]), ALU.subtract
                                      ).then_inc(half[k].s_sub, 1)
                return step

            def divide(k):
                def step(t, l):
                    out = ps[l][:, 1, 0:ROWS].rearrange("p (h e) -> p h e", e=HD + 1)
                    rs = lane[l].rs[:, HH * k:HH * k + HH]
                    dve.wait_ge(half[k].o_ps, nth(t, l))
                    dve.reciprocal(rs, out[:, :, HD]).then_inc(half[k].o_r, 1)
                    dve.wait_ge(half[k].o_r, nth(t, l))
                    dve.tensor_tensor(lane[l].o[:, HH * HD * k:HH * HD * (k + 1)].rearrange("p (h e) -> p h e", e=HD),
                                      out[:, :, 0:HD], bcast(rs, HD), ALU.mult).then_inc(half[k].o, 1)
                return step

            def residual(t, l):
                xb = m.x[:, bass.ds((t * LANES + l) * D, D)]
                dve.wait_ge(s.y_ps, nth(t, l))
                dve.scalar_tensor_tensor(xb, ps[l][:, 1, 0:D], m.tg[:, 3:4], xb, ALU.mult, ALU.add).then_inc(s.x, 1)

            staggered(dve, TURNS, LANES, PLACES, {
                -3: stats, -1: normalise, 1: mask_k, 4: less_maximum(0), 7: less_maximum(1),
                11: divide(0), 15: divide(1), 17: residual})


@sublayer
def l2_ffn(nc, ctx, m, io):
    F = 512
    FC = F // 128
    LANES = 4
    TURNS = B // LANES
    ROUND = 1.5 * 2 ** 23
    NW = 3 * D * F // D
    s = semaphores(nc, ctx, "f2", "w wsum wsum_ps wmean wclip wscale wr1 wr2 wq wg stats mv var_eps rstd xn mx clip rcp qs dq xa "
                   "xb xq xt_ps xt gu_ps sg h hmx hclip hrcp hqs hdq ha hb hq ht_ps ht y_ps x")

    def nth(turn, lane):
        return turn * LANES + lane + 1

    with ExitStack() as mem:
        def sb(name, shape, dt=F32):
            return mem.enter_context(nc.sbuf_tensor("f2_" + name, shape, dt))

        w = sb("w", [128, 3, F])
        wr = sb("wr", [128, 3, F])
        wq = sb("wq", [128, 3, F], BF16)
        wsum, wmean, wscale = sb("wsum", [128, 3]), sb("wmean", [128, 3]), sb("wscale", [128, 3])
        wdg = sb("wdg", [128, 1])
        ones = sb("ones", [128, 128])
        lane = [Names(
            stats=sb(f"stats{l}", [S, 6]), mv=sb(f"mv{l}", [S, 2]), var_eps=sb(f"var{l}", [S, 1]),
            rstd=sb(f"rstd{l}", [S, 1]), xn=sb(f"xn{l}", [S, D]), mx=sb(f"mx{l}", [S, 2]), clip=sb(f"clip{l}", [S, 2]),
            rcp=sb(f"rcp{l}", [S, 2]), qs=sb(f"qs{l}", [S, 2]), dq=sb(f"dq{l}", [S, 3]), xa=sb(f"xa{l}", [S, D]),
            xq=sb(f"xq{l}", [S, D], BF16), xt=sb(f"xt{l}", [D, S], BF16), sg=sb(f"sg{l}", [S, F]), h=sb(f"h{l}", [S, F]),
            hq=sb(f"hq{l}", [S, F], BF16), ht=sb(f"ht{l}", [128, FC, S], BF16)) for l in range(LANES)]
        ps = [mem.enter_context(nc.psum_tensor(f"f2_ps{l}", [128, 2, 512], F32)) for l in range(LANES)]
        ps_b = [p[:, 0, :].bitcast(BF16) for p in ps]
        block = mem.enter_context(nc.Block())

        @block.sync
        def _(sp):
            sp.dma_start(w[:, 0, :], io.w_gate).then_inc(s.w, 16)
            sp.dma_start(w[:, 1, :], io.w_up).then_inc(s.w, 16)
            sp.dma_start(w[:, 2, :].rearrange("p (c n) -> p c n", c=FC), io.w_down).then_inc(s.w, 16)

        @block.tensor
        def _(pe):
            pe.wait_ge(s.wsum, 2)
            pe.matmul(ps[0][:, 0, 0:3], ones[:], wsum[:], start=True, stop=True).then_inc(s.wsum_ps, 1)
            pe.wait_ge(s.wq, 1)
            with pe.Fori(0, TURNS) as t:
                for l in range(LANES):
                    pe.wait_ge(s.xq, nth(t, l))
                    pe.transpose(ps_b[l][:, 0:S], lane[l].xq[:], m.identb[:]).then_inc(s.xt_ps, 1)
                for l in range(LANES):
                    pe.wait_ge(s.xt, nth(t, l))
                    for n in range(2):
                        mm = pe.matmul(ps[l][:, n, :], lane[l].xt[:], wq[:, n, :], start=True, stop=True)
                    mm.then_inc(s.gu_ps, 1)
                for l in range(LANES):
                    pe.wait_ge(s.hq, nth(t, l))
                    for c in range(FC):
                        mm = pe.transpose(ps_b[l][:, S * c:S * c + S], lane[l].hq[:, 128 * c:128 * c + 128], m.identb[:])
                    mm.then_inc(s.ht_ps, 1)
                for l in range(LANES):
                    pe.wait_ge(s.ht, nth(t, l))
                    for c in range(FC):
                        mm = pe.matmul(ps[l][:, 1, 0:D], lane[l].ht[:, c, :], wq[:, 2, D * c:D * c + D],
                                       start=(c == 0), stop=(c == FC - 1))
                    mm.then_inc(s.y_ps, 1)

        @block.scalar
        def _(act):
            with act.Fori(0, TURNS) as t:
                for l in range(LANES):
                    act.wait_ge(s.xt_ps, nth(t, l))
                    act.copy(lane[l].xt[:], ps_b[l][:, 0:S]).then_inc(s.xt, 1)
                for l in range(LANES):
                    act.wait_ge(s.dq, nth(t, l))
                    act.wait_ge(s.gu_ps, nth(t, l))
                    act.activation(lane[l].sg[:], ps[l][:, 0, :], ACT.Silu, scale=lane[l].dq[:, 0:1]).then_inc(s.sg, 1)
                for l in range(LANES):
                    act.wait_ge(s.ht_ps, nth(t, l))
                    act.copy(lane[l].ht[:], ps_b[l][:, 0:FC * S].rearrange("p (c n) -> p c n", c=FC)).then_inc(s.ht, 1)

        @block.gpsimd
        def _(pool):
            pool.memset(ones[:], 1.0).then_inc(s.wsum, 1)
            with pool.Fori(0, TURNS) as t:
                for l in range(LANES):
                    pool.wait_ge(s.var_eps, nth(t, l))
                    inverse_root(pool, lane[l].rstd[:], lane[l].var_eps[:], m, s.rstd)

        @block.vector
        def _(dve):
            dve.wait_ge(s.w, 48)
            dve.tensor_reduce(wsum[:], w[:], AX.X, ALU.add, apply_absolute_value=True).then_inc(s.wsum, 1)
            dve.wait_ge(s.wsum_ps, 1)
            dve.tensor_scalar(wmean[:], ps[0][:, 0, 0:3], 1.0 / (D * F), 1e-5, ALU.mult, ALU.max).then_inc(s.wmean, 1)
            dve.wait_ge(s.wmean, 1)
            dve.reciprocal(wscale[:], wmean[:]).then_inc(s.wscale, 1)
            dve.tensor_tensor(wdg[:], wmean[:, 2:3], m.tg[:, 6:7], ALU.mult).then_inc(s.wg, 1)
            dve.wait_ge(s.wscale, 1)
            for n in range(3):
                dve.tensor_scalar(wr[:, n, :], w[:, n, :], wscale[:, n:n + 1], ROUND, ALU.mult, ALU.add).then_inc(s.wr1, 1)
            dve.wait_ge(s.wr1, 3)
            dve.tensor_scalar(w[:], wr[:], ROUND, -1.0, ALU.subtract, ALU.max).then_inc(s.wr2, 1)
            dve.wait_ge(s.wr2, 1)
            dve.tensor_scalar(wq[:], w[:], 1.0, None, ALU.min).then_inc(s.wq, 1)
            dve.wait_ge(s.wg, 1)
            with dve.Fori(0, TURNS) as t:
                layer_norm_stats(dve, m, s, t, lane)
                for l in range(LANES):
                    dve.wait_ge(s.rstd, nth(t, l))
                    dve.tensor_scalar(lane[l].xn[:], m.x[:, bass.ds((t * LANES + l) * D, D)], lane[l].mv[:, 0:1],
                                      lane[l].rstd[:], ALU.subtract, ALU.mult).then_inc(s.xn, 1)

                def scales(k, source, waited, sems):
                    mx, clip, rcp, qs = sems
                    for l in range(LANES):
                        dve.wait_ge(waited, nth(t, l))
                        dve.tensor_reduce(lane[l].mx[:, k:k + 1], source(l), AX.X, ALU.max, apply_absolute_value=True
                                          ).then_inc(mx, 1)
                    for l in range(LANES):
                        dve.wait_ge(mx, nth(t, l))
                        dve.tensor_scalar(lane[l].clip[:, k:k + 1], lane[l].mx[:, k:k + 1], 1e-5, None, ALU.max
                                          ).then_inc(clip, 1)
                    for l in range(LANES):
                        dve.wait_ge(clip, nth(t, l))
                        dve.reciprocal(lane[l].rcp[:, k:k + 1], lane[l].clip[:, k:k + 1]).then_inc(rcp, 1)
                    for l in range(LANES):
                        dve.wait_ge(rcp, nth(t, l))
                        dve.tensor_scalar(lane[l].qs[:, k:k + 1], lane[l].rcp[:, k:k + 1], 127.0, None, ALU.mult
                                          ).then_inc(qs, 1)

                scales(0, lambda l: lane[l].xn[:], s.xn, (s.mx, s.clip, s.rcp, s.qs))
                for l in range(LANES):
                    dve.tensor_scalar(lane[l].dq[:, 0:2], wmean[:, 0:2], lane[l].clip[:, 0:1], 1.0 / 127, ALU.mult, ALU.mult
                                      ).then_inc(s.dq, 1)
                for l in range(LANES):
                    dve.wait_ge(s.qs, nth(t, l))
                    dve.tensor_scalar(lane[l].xa[:], lane[l].xn[:], lane[l].qs[:, 0:1], ROUND, ALU.mult, ALU.add
                                      ).then_inc(s.xa, 1)
                for l in range(LANES):
                    dve.wait_ge(s.xa, nth(t, l))
                    dve.tensor_scalar(lane[l].xn[:], lane[l].xa[:], ROUND, -128.0, ALU.subtract, ALU.max).then_inc(s.xb, 1)
                for l in range(LANES):
                    dve.wait_ge(s.xb, nth(t, l))
                    dve.tensor_scalar(lane[l].xq[:], lane[l].xn[:], 127.0, None, ALU.min).then_inc(s.xq, 1)
                for l in range(LANES):
                    dve.wait_ge(s.dq, nth(t, l))
                    dve.wait_ge(s.sg, nth(t, l))
                    dve.scalar_tensor_tensor(lane[l].h[:], ps[l][:, 1, :], lane[l].dq[:, 1:2], lane[l].sg[:],
                                             ALU.mult, ALU.mult).then_inc(s.h, 1)
                scales(1, lambda l: lane[l].h[:], s.h, (s.hmx, s.hclip, s.hrcp, s.hqs))
                for l in range(LANES):
                    dve.tensor_scalar(lane[l].dq[:, 2:3], wdg[:], lane[l].clip[:, 1:2], 1.0 / 127, ALU.mult, ALU.mult
                                      ).then_inc(s.hdq, 1)
                for l in range(LANES):
                    dve.wait_ge(s.hqs, nth(t, l))
                    dve.tensor_scalar(lane[l].sg[:], lane[l].h[:], lane[l].qs[:, 1:2], ROUND, ALU.mult, ALU.add
                                      ).then_inc(s.ha, 1)
                for l in range(LANES):
                    dve.wait_ge(s.ha, nth(t, l))
                    dve.tensor_scalar(lane[l].h[:], lane[l].sg[:], ROUND, -128.0, ALU.subtract, ALU.max).then_inc(s.hb, 1)
                for l in range(LANES):
                    dve.wait_ge(s.hb, nth(t, l))
                    dve.tensor_scalar(lane[l].hq[:], lane[l].h[:], 127.0, None, ALU.min).then_inc(s.hq, 1)
                for l in range(LANES):
                    xb = m.x[:, bass.ds((t * LANES + l) * D, D)]
                    dve.wait_ge(s.hdq, nth(t, l))
                    dve.wait_ge(s.y_ps, nth(t, l))
                    dve.scalar_tensor_tensor(xb, ps[l][:, 1, 0:D], lane[l].dq[:, 2:3], xb, ALU.mult, ALU.add).then_inc(s.x, 1)
                dve.wait_ge(s.x, nth(t, LANES - 1))


@sublayer
def switch_ffn(nc, ctx, m, io):
    E, F = 8, 512
    FC = F // 128
    CAP = B * S // E
    TILES = CAP // 128
    GROUP = 4
    NORM = 8
    s = semaphores(nc, ctx, "f3", "w zero init stats mv var_eps rstd sub0 xn xt_ps xt r_ps r mx sub exp den gate eq key kmax idx "
                   "oh cnt_ps pre excl pos sel place base over tok alt1 alt dest gidx wt wtg iota tri one in0 in1 in2 in3 in4 "
                   "in5 in6 in7 xet_ps xet up_ps h y_ps y out sc0 sc1 sc2 sc3 g0 g1 g2 g3 x")
    expert_in = [s.in0, s.in1, s.in2, s.in3, s.in4, s.in5, s.in6, s.in7]
    scattered = [s.sc0, s.sc1, s.sc2, s.sc3]
    gathered = [s.g0, s.g1, s.g2, s.g3]
    rows_in = nc.dram_tensor("f3_rows_in", (E * CAP + B * S, D), F32, kind="Internal").ap()
    rows_out = nc.dram_tensor("f3_rows_out", (E * CAP, D), F32, kind="Internal").ap()

    with ExitStack() as mem:
        def sb(name, shape, dt=F32):
            return mem.enter_context(nc.sbuf_tensor("f3_" + name, shape, dt))

        wr, w1, w3 = sb("wr", [D, E]), sb("w1", [D, E, FC, 128]), sb("w3", [128, E, FC, D])
        b1, b2 = sb("b1", [128, E, FC]), sb("b2", [128, E * D])
        zeros = sb("zeros", [128, 8 * D])
        tri = sb("tri", [S, S])
        ones = sb("ones", [S, S])
        experts = sb("experts", [S, E])
        token = sb("token", [S, B])
        stats, mv = sb("stats", [S, B, 6]), sb("mv", [S, B, 2])
        var_eps, rstd = sb("var", [S, B]), sb("rstd", [S, B])
        xn = sb("xn", [S, B, D])
        xt = [sb(f"xt{k}", [D, GROUP, S]) for k in range(2)]
        r, sub, eq, key, oh = (sb(n, [S, B, E]) for n in ("r", "sub", "eq", "key", "oh"))
        cum = [sb(f"cum{k}", [S, B, E]) for k in range(2)]
        pos, sel = sb("pos", [S, B, E]), sb("sel", [S, B, E])
        mx, den, gate, kmax, idx, place, base, over, alt1, alt, dest_f, gidx_f, keep, wt, wtg = (
            sb(n, [S, B]) for n in ("mx", "den", "gate", "kmax", "idx", "place", "base", "over", "alt1", "alt", "destf",
                                    "gidxf", "keep", "wt", "wtg"))
        dest, gidx = sb("dest", [S, B], U32), sb("gidx", [S, B], U32)
        rows = sb("rows", [128, E, TILES * D])
        xet = [sb(f"xet{k}", [D, CAP]) for k in range(2)]
        hid = [sb(f"hid{k}", [128, CAP]) for k in range(2 * FC)]
        tp = mem.enter_context(nc.psum_tensor("f3_tp", [128, 2, 512], F32))
        up = mem.enter_context(nc.psum_tensor("f3_up", [128, 4, 512], F32))
        yps = mem.enter_context(nc.psum_tensor("f3_y", [128, 2, 512], F32))
        scores_ps = yps[:, 0, 0:B * E].rearrange("p (b e) -> p b e", e=E)
        before_ps = yps[:, 1, 0:B * E].rearrange("p (b e) -> p b e", e=E)
        count_ps = yps[:, 1, 256:256 + B * E].rearrange("p (b e) -> p b e", e=E)
        block = mem.enter_context(nc.Block())

        @block.sync
        def _(sp):
            for dst, src in ((wr[:], io.router), (w1[:], io.w1), (w3[:], io.w3), (b1[:], io.b1),
                             (b2[:], io.b2.rearrange("e d -> (e d)").partition_broadcast(128))):
                sp.dma_start(dst, src).then_inc(s.w, 16)
            sp.wait_ge(s.zero, 1)
            empty = rows_in[0:E * CAP, :].rearrange("(p r) d -> p (r d)", p=128)
            for i in range(4):
                sp.dma_start(empty[:, 8 * D * i:8 * D * (i + 1)], zeros[:]).then_inc(s.init, 16)
            for l in range(4):
                sp.wait_ge(scattered[l], 16 * (B // 4))
            for e in range(E):
                sp.dma_start(rows[:, e, :].rearrange("p (k d) -> p k d", d=D),
                             rows_in[CAP * e:CAP * (e + 1), :].rearrange("(k p) d -> p k d", p=128)
                             ).then_inc(expert_in[e], 16)
            for e in range(E):
                sp.wait_ge(s.y, e + 1)
                sp.dma_start(rows_out[CAP * e:CAP * (e + 1), :].rearrange("(k p) d -> p k d", p=128),
                             rows[:, e, :].rearrange("p (k d) -> p k d", d=D)).then_inc(s.out, 16)
            sp.wait_ge(s.out, 16 * E)

        def router(pe, g):
            pe.wait_ge(s.xt, g + 1)
            for l in range(GROUP):
                b = GROUP * g + l
                mm = pe.matmul(scores_ps[:, b, :], xt[g % 2][:, l, :], wr[:], start=True, stop=True)
            mm.then_inc(s.r_ps, 1)

        def inputs(pe, e):
            pe.wait_ge(expert_in[e], 16)
            if e >= 2:
                pe.wait_ge(s.xet, e - 1)
            for k in range(TILES):
                mm = pe.transpose(tp[:, e % 2, 128 * k:128 * k + 128], rows[:, e, D * k:D * k + D], m.ident[:])
            mm.then_inc(s.xet_ps, 1)

        def first(pe, e):
            pe.wait_ge(s.xet, e + 1)
            for c in range(FC):
                if e:
                    pe.wait_ge(s.h, FC * (e - 1) + c + 1)
                pe.matmul(up[:, c, :], w1[:, e, c, :], xet[e % 2][:], start=True, stop=True).then_inc(s.up_ps, 1)

        def second(pe, e):
            pe.wait_ge(s.h, FC * (e + 1))
            if e >= 2:
                pe.wait_ge(s.y, e - 1)
            for k in range(TILES):
                for c in range(FC):
                    mm = pe.matmul(yps[:, e % 2, D * k:D * k + D], hid[e % 2 * FC + c][:, 128 * k:128 * k + 128],
                                   w3[:, e, c, :], start=(c == 0), stop=(c == FC - 1))
            mm.then_inc(s.y_ps, 1)

        @block.tensor
        def _(pe):
            for g in range(B // GROUP):
                pe.wait_ge(s.xn, GROUP * g // NORM + 1)
                if g >= 2:
                    pe.wait_ge(s.xt, g - 1)
                for l in range(GROUP):
                    mm = pe.transpose(tp[:, g % 2, S * l:S * l + S], xn[:, GROUP * g + l, :], m.ident[:])
                mm.then_inc(s.xt_ps, 1)
                if g == 0:
                    pe.wait_ge(s.w, 80)
                else:
                    router(pe, g - 1)
            router(pe, B // GROUP - 1)
            pe.wait_ge(s.oh, 1)
            pe.wait_ge(s.tri, 1)
            flat_oh = oh[:].rearrange("p b e -> p (b e)")
            pe.matmul(yps[:, 1, 0:B * E], tri[:], flat_oh, start=True, stop=True)
            pe.matmul(yps[:, 1, 256:256 + B * E], ones[:], flat_oh, start=True, stop=True).then_inc(s.cnt_ps, 1)
            for e in range(E + 1):
                if e == 0:
                    inputs(pe, 0)
                if e + 1 < E:
                    inputs(pe, e + 1)
                if e < E:
                    first(pe, e)
                if e:
                    second(pe, e - 1)

        @block.scalar
        def _(act):
            for g in range(B // GROUP):
                act.wait_ge(s.xt_ps, g + 1)
                if g >= 2:
                    act.wait_ge(s.r_ps, g - 1)
                act.copy(xt[g % 2][:], tp[:, g % 2, :].rearrange("p (l n) -> p l n", n=S)).then_inc(s.xt, 1)
            act.wait_ge(s.sub, 1)
            act.activation(sub[:], sub[:], ACT.Exp).then_inc(s.exp, 1)
            for e in range(E + 1):
                for i in ((0, 1) if e == 0 else (e + 1,)):
                    if i < E:
                        act.wait_ge(s.xet_ps, i + 1)
                        if i >= 2:
                            act.wait_ge(s.up_ps, FC * (i - 1))
                        act.copy(xet[i % 2][:], tp[:, i % 2, :]).then_inc(s.xet, 1)
                if e < E:
                    for c in range(FC):
                        act.wait_ge(s.up_ps, FC * e + c + 1)
                        if e >= 2:
                            act.wait_ge(s.y_ps, e - 1)
                        act.activation(hid[e % 2 * FC + c][:], up[:, c, :], ACT.Relu, bias=b1[:, e, c:c + 1]
                                       ).then_inc(s.h, 1)

        @block.gpsimd
        def _(pool):
            pool.memset(zeros[:], 0.0).then_inc(s.zero, 1)
            pool.iota(experts[:], [[1, E]], base=0, channel_multiplier=0, allow_small_or_imprecise_dtypes=True
                      ).then_inc(s.iota, 1)
            pool.iota(token[:], [[S, B]], base=0, channel_multiplier=1, allow_small_or_imprecise_dtypes=True
                      ).then_inc(s.iota, 1)
            pool.memset(ones[:], 1.0).then_inc(s.one, 1)
            pool.wait_ge(s.one, 1)
            pool.affine_select(tri[:], ones[:], [[1, S]], ALU.is_ge, 0.0, 0, -1).then_inc(s.tri, 1)
            pool.wait_ge(s.var_eps, 1)
            for i in range(2):
                inverse_root(pool, rstd[:, 16 * i:16 * i + 16], var_eps[:, 16 * i:16 * i + 16], m, s.rstd)
            pool.wait_ge(s.init, 64)
            pool.wait_ge(s.dest, 1)
            for b in range(B):
                if b >= 4:
                    pool.wait_ge(scattered[b % 4], 16 * (b // 4))
                pool.indirect_dma_start(rows_in, bass.IndirectOffsetOnAxis(ap=dest[:, b:b + 1], axis=0), xn[:, b, :], None
                                        ).then_inc(scattered[b % 4], 16)
            pool.wait_ge(s.out, 16 * E)
            for l in range(4):
                pool.wait_ge(scattered[l], 16 * (B // 4))
            for b in range(B):
                if b >= 4:
                    pool.wait_ge(gathered[b % 4], 16 * (b // 4))
                pool.indirect_dma_start(xn[:, b, :], None, rows_out, bass.IndirectOffsetOnAxis(ap=gidx[:, b:b + 1], axis=0)
                                        ).then_inc(gathered[b % 4], 16)

        @block.vector
        def _(dve):
            with dve.Fori(0, B // 4) as t:
                for l in range(4):
                    dve.bn_stats(stats[:, bass.ds(t * 4 + l, 1), :].rearrange("p a s -> p (a s)"),
                                 m.x[:, bass.ds((t * 4 + l) * D, D)]).then_inc(s.stats, 1)
            dve.wait_ge(s.stats, B)
            for b in range(B):
                dve.bn_aggr(mv[:, b, :], stats[:, b, :]).then_inc(s.mv, 1)
            dve.wait_ge(s.mv, B)
            dve.tensor_scalar(var_eps[:], mv[:, :, 1], LN_EPS, None, ALU.add).then_inc(s.var_eps, 1)
            xb = m.x[:].rearrange("p (b d) -> p b d", d=D)
            for i in range(B // NORM):
                part = slice(NORM * i, NORM * i + NORM)
                dve.tensor_tensor(xn[:, part, :], xb[:, part, :], bcast(mv[:, part, 0], D), ALU.subtract).then_inc(s.sub0, 1)
            for i in range(B // NORM):
                part = slice(NORM * i, NORM * i + NORM)
                dve.wait_ge(s.sub0, i + 1)
                dve.wait_ge(s.rstd, 2)
                dve.tensor_tensor(xn[:, part, :], xn[:, part, :], bcast(rstd[:, part], D), ALU.mult).then_inc(s.xn, 1)
            dve.wait_ge(s.r_ps, B // GROUP)
            dve.tensor_copy(r[:], scores_ps).then_inc(s.r, 1)
            dve.wait_ge(s.r, 1)
            dve.tensor_reduce(mx[:], r[:], AX.X, ALU.max).then_inc(s.mx, 1)
            dve.wait_ge(s.mx, 1)
            dve.tensor_tensor(eq[:], r[:], bcast(mx[:], E), ALU.is_equal).then_inc(s.eq, 1)
            dve.tensor_tensor(sub[:], r[:], bcast(mx[:], E), ALU.subtract).then_inc(s.sub, 1)
            dve.wait_ge(s.iota, 2)
            dve.wait_ge(s.eq, 1)
            each = experts[:].unsqueeze(1).broadcast_to([S, B, E])
            dve.scalar_tensor_tensor(key[:], eq[:], float(E), each, ALU.mult, ALU.subtract).then_inc(s.key, 1)
            dve.wait_ge(s.key, 1)
            dve.tensor_reduce(kmax[:], key[:], AX.X, ALU.max).then_inc(s.kmax, 1)
            dve.wait_ge(s.kmax, 1)
            dve.tensor_scalar(idx[:], kmax[:], -1.0, float(E), ALU.mult, ALU.add).then_inc(s.idx, 1)
            dve.wait_ge(s.idx, 1)
            dve.tensor_tensor(oh[:], each, bcast(idx[:], E), ALU.is_equal).then_inc(s.oh, 1)
            dve.wait_ge(s.exp, 1)
            dve.tensor_reduce(den[:], sub[:], AX.X, ALU.add).then_inc(s.den, 1)
            dve.wait_ge(s.den, 1)
            dve.reciprocal(gate[:], den[:]).then_inc(s.gate, 1)
            dve.wait_ge(s.cnt_ps, 1)
            dve.tensor_copy(cum[0][:], count_ps).then_inc(s.pre, 1)
            step, k = 1, 0
            while step < B:
                dve.wait_ge(s.pre, 2 * k + 1)
                a, c = cum[k % 2], cum[1 - k % 2]
                dve.tensor_copy(c[:, 0:step, :], a[:, 0:step, :]).then_inc(s.pre, 1)
                dve.tensor_tensor(c[:, step:B, :], a[:, step:B, :], a[:, 0:B - step, :], ALU.add).then_inc(s.pre, 1)
                step, k = 2 * step, k + 1
            dve.wait_ge(s.pre, 2 * k + 1)
            total = cum[k % 2]
            dve.tensor_copy(pos[:, 0:1, :], before_ps[:, 0:1, :]).then_inc(s.pos, 1)
            dve.tensor_tensor(pos[:, 1:B, :], before_ps[:, 1:B, :], total[:, 0:B - 1, :], ALU.add).then_inc(s.pos, 1)
            dve.wait_ge(s.pos, 2)
            dve.wait_ge(s.oh, 1)
            dve.tensor_tensor(sel[:], pos[:], oh[:], ALU.mult).then_inc(s.sel, 1)
            dve.wait_ge(s.sel, 1)
            dve.tensor_reduce(place[:], sel[:], AX.X, ALU.add).then_inc(s.place, 1)
            dve.wait_ge(s.place, 1)
            dve.scalar_tensor_tensor(base[:], idx[:], float(CAP), place[:], ALU.mult, ALU.add).then_inc(s.base, 1)
            dve.tensor_scalar(over[:], place[:], float(CAP), None, ALU.is_gt).then_inc(s.over, 1)
            dve.tensor_scalar(keep[:], place[:], float(CAP), None, ALU.is_le).then_inc(s.tok, 1)
            dve.wait_ge(s.base, 1)
            dve.scalar_tensor_tensor(alt1[:], token[:], float(E * CAP + 1), base[:], ALU.add, ALU.subtract
                                     ).then_inc(s.alt1, 1)
            dve.tensor_scalar(gidx_f[:], base[:], -1.0, float(E * CAP - 1), ALU.add, ALU.min).then_inc(s.gidx, 1)
            dve.wait_ge(s.alt1, 1)
            dve.wait_ge(s.over, 1)
            dve.tensor_tensor(alt[:], alt1[:], over[:], ALU.mult).then_inc(s.alt, 1)
            dve.wait_ge(s.alt, 1)
            dve.scalar_tensor_tensor(dest_f[:], base[:], -1.0, alt[:], ALU.add, ALU.add).then_inc(s.alt, 1)
            dve.wait_ge(s.alt, 2)
            dve.wait_ge(s.gidx, 1)
            dve.tensor_copy(gidx[:], gidx_f[:])
            dve.tensor_copy(dest[:], dest_f[:]).then_inc(s.dest, 1)
            dve.wait_ge(s.gate, 1)
            dve.wait_ge(s.tok, 1)
            dve.tensor_tensor(wt[:], gate[:], keep[:], ALU.mult).then_inc(s.wt, 1)
            dve.wait_ge(s.wt, 1)
            dve.tensor_scalar(wtg[:], wt[:], m.tg[:, 7:8], None, ALU.mult).then_inc(s.wtg, 1)
            for e in range(E):
                dve.wait_ge(s.y_ps, e + 1)
                dve.tensor_tensor(rows[:, e, :].rearrange("p (k d) -> p k d", d=D),
                                  yps[:, e % 2, :].rearrange("p (k d) -> p k d", d=D),
                                  b2[:, D * e:D * e + D].unsqueeze(1).broadcast_to([128, TILES, D]), ALU.add
                                  ).then_inc(s.y, 1)
            dve.wait_ge(s.wtg, 1)
            for b in range(B):
                dve.wait_ge(gathered[b % 4], 16 * (b // 4 + 1))
                dve.scalar_tensor_tensor(xb[:, b, :], xn[:, b, :], wtg[:, b:b + 1], xb[:, b, :], ALU.mult, ALU.add
                                         ).then_inc(s.x, 1)
            dve.wait_ge(s.x, B)


HOST_LAYOUT = {
    "L0_ffn_Wg": (1, 0, 2), "L0_ffn_Wu": (1, 0, 2),
    "L1_ffn_Wg": (1, 0), "L1_ffn_W1": (2, 0, 1), "L1_ffn_W2": (2, 0, 1), "L1_ffn_W3": (2, 0, 1),
    "L2_ffn_w_gate": (1, 0), "L2_ffn_w_up": (1, 0), "L2_ffn_w_down": (1, 0),
    "L3_ffn_w1": (1, 0, 2), "L0_ffn_bd": (1, 0),
    "L0_ffn_bg": (2, 0, 1), "L0_ffn_bu": (2, 0, 1), "L3_ffn_b1": (2, 0, 1),
}
HOST_SHAPE = {"L0_ffn_bg": (16, 2, 128), "L0_ffn_bu": (16, 2, 128), "L3_ffn_b1": (8, 4, 128)}


def run_phases(nc, ctx, m, io):
    ios = Names(ctx=io["ctx_1024"])
    m.prefetch_a1 = m.prefetch_a2 = None
    if 1 in PHASES:
        f = {n: io["L0_ffn_" + n] for n in ("norm_g", "norm_b", "slot_g", "slot_b", "scale", "slot_embeds", "Wg", "Wu")}
        l0_ffn(nc, m, Names(
            Wd=io["L0_ffn_Wd"].rearrange("e (c p) n -> p e c n", p=128),
            bg=io["L0_ffn_bg"], bu=io["L0_ffn_bu"], bd=io["L0_ffn_bd"], **f))
    if 2 in PHASES:
        l1_attention(nc, m, ios)
    if 3 in PHASES:
        routed_ffn(nc, m, Names(
            router=io["L1_ffn_Wg"], w1=io["L1_ffn_W1"].rearrange("d e (c p) -> d e c p", p=128),
            w2=io["L1_ffn_W2"].rearrange("d e (c p) -> d e c p", p=128),
            w3=io["L1_ffn_W3"].rearrange("(c p) e n -> p e c n", p=128)), "top2")
    if 4 in PHASES:
        l2_attention(nc, m, ios)
    if 5 in PHASES:
        l2_ffn(nc, m, Names(
            w_gate=io["L2_ffn_w_gate"], w_up=io["L2_ffn_w_up"],
            w_down=io["L2_ffn_w_down"].rearrange("(c p) n -> p c n", p=128)))
    if 6 in PHASES:
        l3_attention(nc, m, ios)
    if 7 in PHASES:
        switch_ffn(nc, m, Names(
            router=io["L3_ffn_router_w"], w1=io["L3_ffn_w1"].rearrange("d e (c p) -> d e c p", p=128),
            b1=io["L3_ffn_b1"],
            w3=io["L3_ffn_w2"].rearrange("e (c p) n -> p e c n", p=128), b2=io["L3_ffn_b2"]))


def bass_flamingo_gated_stack(nc, io, out):
    with ExitStack() as ctx:
        def sb(name, shape, dt=F32):
            return ctx.enter_context(nc.sbuf_tensor(name, shape, dt))

        m = Shared()
        m.x = sb("x_res", [S, B * D])
        m.ident = sb("ident", [128, 128])
        m.identb = sb("identb", [128, 128], BF16)
        m.causal = sb("causal", [S, SC + S], BF16)
        m.first_row = sb("first_row", [128, 128], BF16)
        m.minus_half = sb("minus_half", [128, 16])
        m.ones_row = sb("ones_row", [1, 128])
        m.wait_pad = sb("wait_pad", [128, 1])
        m.zero = sb("zero", [128, 1])
        m.g_raw = sb("g_raw", [128, 8])
        m.tg = sb("tg", [128, 8])
        m.mask = sb("mask", [128, B * SC], U8)
        m.maskneg = sb("maskneg", [128, B * SC], BF16)
        ROWS = "bo0 bv1 bout2 bv3 bo3".split()
        m.rows = sb("rows", [1, len(ROWS), D])
        m.row_bo0, m.row_bv1, m.row_bout2, m.row_bv3, m.row_bo3 = range(5)
        m.gq = sb("gq", [128, 1])
        m.gk = sb("gk", [128, 1])
        m.gqk = sb("gqk", [128, 1])
        m.bqk1 = sb("bqk1", [128, 2])
        m.bqk3 = sb("bqk3", [128, 2])
        m.headmask = sb("headmask", [128, 4])
        m.wq1, m.wk1, m.wv1 = (sb(n, [D, D]) for n in ("wq1", "wk1", "wv1"))
        m.wq2, m.wkv2, m.wout2 = sb("wq2", [D, D]), sb("wkv2", [D, 2 * D]), sb("wout2", [D, D])
        m.wq3, m.wk3, m.wv3, m.wo3 = (sb(n, [D, D]) for n in ("wq3", "wk3", "wv3", "wo3"))

        m.s_small = ctx.enter_context(nc.semaphore("small_in"))
        m.s_x = ctx.enter_context(nc.semaphore("x_in"))
        m.s_w0 = ctx.enter_context(nc.semaphore("w0_in"))
        m.s_out = ctx.enter_context(nc.semaphore("out_done"))
        m.s_ready = ctx.enter_context(nc.semaphore("ready"))
        setup = semaphores(nc, [], "setup", "zero ident identb causal misc tanh vec hm")
        small = []
        for i, n in enumerate(("L0_xattn_bo", "L1_xattn_bv", "L2_xattn_bout", "L3_xattn_bv", "L3_xattn_bo")):
            small.append((m.rows[0:1, i, :], io[n].unsqueeze(0)))
        small += [(m.g_raw[:, 0:4], io["g_xattn"].partition_broadcast(128)),
                  (m.g_raw[:, 4:8], io["g_ffn"].partition_broadcast(128)),
                  (m.mask[:], io["mask_BxS2_bk0"].rearrange("b s -> (b s)").partition_broadcast(128)),
                  (m.bqk1[:, 0:1], io["L1_xattn_bq"].unsqueeze(1)), (m.bqk1[:, 1:2], io["L1_xattn_bk"].unsqueeze(1)),
                  (m.bqk3[:, 0:1], io["L3_xattn_bq"].unsqueeze(1)), (m.bqk3[:, 1:2], io["L3_xattn_bk"].unsqueeze(1)),
                  (m.wq1[:], io["L1_xattn_Wq"]), (m.wk1[:], io["L1_xattn_Wk"]), (m.wv1[:], io["L1_xattn_Wv"]),
                  (m.wq2[:], io["L2_xattn_Wq"]), (m.wkv2[:], io["L2_xattn_Wkv"]), (m.wout2[:], io["L2_xattn_Wout"]),
                  (m.wq3[:], io["L3_xattn_Wq"]), (m.wk3[:], io["L3_xattn_Wk"]), (m.wv3[:], io["L3_xattn_Wv"]),
                  (m.wo3[:], io["L3_xattn_Wo"])]
        for half in range(2):
            row = slice(64 * half, 64 * half + 64)
            small += [(m.gq[row], io["L0_xattn_gq"].unsqueeze(1)), (m.gk[row], io["L0_xattn_gk"].unsqueeze(1))]

        with ExitStack() as mem0:
            if 0 in PHASES:
                m.wq0, m.wk0, m.wv0 = (mem0.enter_context(nc.sbuf_tensor(n, [D, 1024], F32)) for n in ("wq0", "wk0", "wv0"))
                m.wo0 = mem0.enter_context(nc.sbuf_tensor("wo0", [128, 8, D], F32))
            m.n_w0 = 64
            m.prefetch_a0 = None
            with nc.Block() as block:
                @block.sync
                def _(sp):
                    for dst, src in small:
                        sp.dma_start(dst, src).then_inc(m.s_small, 16)
                    xv = io["x"].rearrange("b s d -> s b d")
                    sp.dma_start(m.x[:].rearrange("p (b d) -> p b d", d=D), xv).then_inc(m.s_x, 16)
                    if 0 in PHASES:
                        sp.dma_start(m.wq0[:], io["L0_xattn_Wq"].rearrange("d h e -> d (h e)")).then_inc(m.s_w0, 16)
                        sp.dma_start(m.wk0[:], io["L0_xattn_Wk"].rearrange("d h e -> d (h e)")).then_inc(m.s_w0, 16)
                        sp.dma_start(m.wv0[:], io["L0_xattn_Wv"].rearrange("d h e -> d (h e)")).then_inc(m.s_w0, 16)
                        sp.dma_start(m.wo0[:], io["L0_xattn_Wo"].rearrange("(j a) e n -> (a e) j n", a=2)).then_inc(m.s_w0, 16)

                @block.gpsimd
                def _(pool):
                    pool.memset(m.ident[:], 0.0).then_inc(setup.zero, 1)
                    pool.memset(m.causal[:], 0.0).then_inc(setup.zero, 1)
                    pool.memset(m.minus_half[:], -0.5)
                    pool.memset(m.ones_row[:], 1.0)
                    pool.memset(m.first_row[:], 0.0).then_inc(setup.zero, 1)
                    pool.memset(m.headmask[:], 1.0).then_inc(setup.zero, 1)
                    pool.wait_ge(setup.zero, 4)
                    pool.memset(m.first_row[0:1, :], 1.0).then_inc(setup.misc, 1)
                    pool.wait_ge(setup.misc, 1)
                    pool.affine_select(m.ident[:], m.ident[:], [[-1, 128]], ALU.not_equal, 1.0, 0, 1).then_inc(setup.ident, 1)
                    pool.affine_select(m.causal[:, SC:SC + S], m.causal[:, SC:SC + S], [[-1, S]], ALU.is_ge, NEG, 0, 1).then_inc(setup.causal, 1)
                    for quad in range(4):
                        if quad:
                            pool.wait_ge(setup.hm, 2 * quad)
                        part = m.headmask[32 * quad:32 * quad + 32, :]
                        pool.affine_select(part, part, [[-8, 4]], ALU.is_ge, 0.0, 0, 1).then_inc(setup.hm, 1)
                        pool.wait_ge(setup.hm, 2 * quad + 1)
                        pool.affine_select(part, part, [[8, 4]], ALU.is_ge, 0.0, 7, -1).then_inc(setup.hm, 1)
                    pool.wait_ge(setup.hm, 8)
                    pool.wait_ge(setup.ident, 1)
                    pool.tensor_copy(m.identb[:], m.ident[:]).then_inc(setup.identb, 1)

                @block.scalar
                def _(act):
                    act.wait_ge(m.s_small, 16 * len(small))
                    act.activation(m.tg[:], m.g_raw[:], ACT.Tanh).then_inc(setup.tanh, 1)

                @block.vector
                def _(dve):
                    dve.wait_ge(m.s_small, 16 * len(small))
                    dve.tensor_tensor(m.gqk[:], m.gq[:], m.gk[:], ALU.mult).then_inc(setup.vec, 1)
                    dve.tensor_scalar(m.maskneg[:], m.mask[:], NEG, None, ALU.mult).then_inc(setup.vec, 1)
                    dve.memset(m.zero[:], 0.0).then_inc(m.s_ready, 1)
                    dve.wait_ge(m.s_x, 16)
            ios = Names(ctx=io["ctx_1024"])
            if 0 in PHASES:
                l0_attention(nc, m, ios)
        run_phases(nc, ctx, m, io)

        with nc.Block() as block:
            @block.sync
            def _(sp):
                sp.dma_start(out.rearrange("b s d -> s b d"), m.x[:].rearrange("p (b d) -> p b d", d=D)
                             ).then_inc(m.s_out, 16)
                sp.wait_ge(m.s_out, 16)


def kernel(**inputs):
    import numpy as np
    import concourse.bacc as bacc
    from concourse.bass_utils import run_bass_kernel_spmd

    nc = bacc.Bacc("TRN2", target_bir_lowering=False, num_devices=1)
    arrays, io = {}, {}
    for name, value in inputs.items():
        a = np.ascontiguousarray(value)
        if name in HOST_SHAPE:
            a = a.reshape(HOST_SHAPE[name])
        if name in HOST_LAYOUT:
            a = np.ascontiguousarray(np.transpose(a, HOST_LAYOUT[name]))
        arrays[f"in_{name}"] = a
        io[name] = nc.dram_tensor(f"in_{name}", a.shape, mybir.dt.from_np(a.dtype), kind="ExternalInput").ap()
    out = nc.dram_tensor("out_x", (B, S, D), F32, kind="ExternalOutput").ap()
    bass_flamingo_gated_stack(nc, io, out)
    result = run_bass_kernel_spmd(nc, [arrays], core_ids=[0])
    return result.results[0]["out_x"]
```

```python
from collections import namedtuple
from contextlib import ExitStack

import concourse.bass as bass
from concourse import mybir

F32 = mybir.dt.float32
BF16 = mybir.dt.bfloat16
U8 = mybir.dt.uint8
U32 = mybir.dt.uint32
ALU = mybir.AluOpType
ACT = mybir.ActivationFunctionType
AX = mybir.AxisListType

B, S, D = 32, 128, 128
SC = 77
LN_EPS = 1e-5
NEG = -1e30


class Shared:
    pass


def Names(**named):
    return namedtuple("Names", sorted(named))(**named)


def semaphores(nc, own, phase, names):
    found = {n: nc.alloc_semaphore(name=f"{phase}_{n}") for n in names.split()}
    own += found.values()
    return Names(**found)


def bcast(ap, n):
    return ap.unsqueeze(2).broadcast_to([ap.shape[0], ap.shape[1], n])


def sublayer(build):
    def scoped(nc, m, *args):
        own = []
        build(nc, own, m, *args)
        nc.clear_and_free_semaphores(own)
        nc.all_engine_barrier()
    return scoped


def staggered(eng, turns, lanes, places, steps):
    lag = places // lanes

    def part(i, turn, every):
        for l in sorted(range(lanes), key=lambda l: (i - lag * l) % places):
            place = (i - lag * l) % places
            own_turn = turn if i >= lag * l else turn - 1
            if place in steps and (every or 0 <= own_turn < turns):
                steps[place](own_turn, l)
            if place - places in steps and (every or 0 <= own_turn + 1 < turns):
                steps[place - places](own_turn + 1, l)

    for i in range(places + min(steps), places):
        part(i, -1, False)
    for i in range(places):
        part(i, 0, False)
    with eng.Fori(0, turns - 2) as t:
        for i in range(places):
            part(i, t + 1, True)
    for i in range(places):
        part(i, turns - 1, False)
    for i in range(lag * (lanes - 1)):
        part(i, turns, False)


PHASES = range(8)


def token_stats(dve, m, s, l, batch, n):
    dve.bn_stats(l.stats[:], m.x[:, bass.ds(batch * D, D)]).then_inc(s.stats, 1)
    dve.wait_ge(s.stats, n)
    dve.memset(m.wait_pad[:], 0.0)
    dve.bn_aggr(l.mv[:], l.stats[:]).then_inc(s.mv, 1)
    dve.wait_ge(s.mv, n)
    dve.tensor_scalar(l.var_eps[:], l.mv[:, 1:2], LN_EPS, None, ALU.add).then_inc(s.var_eps, 1)


def layer_norm_stats(dve, m, s, turn, lanes, lane_offset=0):
    L = len(lanes)
    for i, l in enumerate(lanes):
        dve.bn_stats(l.stats[:], m.x[:, bass.ds((turn * L + i) * D, D)]).then_inc(s.stats, 1)
    dve.wait_ge(s.stats, turn * L + L)
    dve.memset(m.wait_pad[:], 0.0)
    for i, l in enumerate(lanes):
        dve.bn_aggr(l.mv[:], l.stats[:]).then_inc(s.mv, 1)
    for i, l in enumerate(lanes):
        dve.wait_ge(s.mv, turn * L + i + 1)
        dve.tensor_scalar(l.var_eps[:], l.mv[:, 1:2], LN_EPS, None, ALU.add).then_inc(s.var_eps, 1)


def load_context(sp, io, s, lane, c_in, turns):
    L = len(lane)
    for l in range(L):
        sp.dma_start(lane[l].c[:], io.ctx[l]).then_inc(c_in[l], 16)
    with sp.Fori(0, turns - 1) as t:
        for l in range(L):
            sp.wait_ge(s.xt_ps, t * L + l + 1)
            sp.dma_start(lane[l].c[:], io.ctx[bass.ds((t + 1) * L + l, 1)].rearrange("a s d -> (a s) d")
                         ).then_inc(c_in[l], 16)


def inverse_root(pool, out, in_, m, done):
    n = in_.shape[1]
    pool.tensor_tensor(out, in_, m.minus_half[0:in_.shape[0], 0:n], ALU.pow).then_inc(done, 1)


@sublayer
def l0_attention(nc, ctx, m, io):
    H, HD = 16, 64
    HH = H // 2
    LANES = 4
    TURNS = B // LANES
    PLACES = 24
    CH = H // 2
    s = semaphores(nc, ctx, "a0", "stats mv var_eps rstd xn xt_ps xt q_ps q q_sq q_ss q_ms q_r v_ps v k_ps k k_sq k_ss "
                   "k_ms k_r k_n qt_ps qt kt_ps km y_ps x "
                   "c0 c1 c2 c3 gzero gain")
    c_in = [s.c0, s.c1, s.c2, s.c3]

    def nth(turn, lane):
        return turn * LANES + lane + 1

    half = [semaphores(nc, ctx, f"a0h{k}", "s_ps s_max s_sub s_q e sum rs p pt_ps pt ot_ps ot") for k in range(2)]

    with ExitStack() as mem:
        def sb(name, shape, dt=F32):
            return mem.enter_context(nc.sbuf_tensor("a0_" + name, shape, dt))

        def lane_buffers(l):
            return Names(
                stats=sb(f"stats{l}", [S, 6]), mv=sb(f"mv{l}", [S, 2]), var_eps=sb(f"var{l}", [S, 1]),
                rstd=sb(f"rstd{l}", [S, 1]), xn=sb(f"xn{l}", [S, D]), xt=sb(f"xt{l}", [D, S]),
                c=sb(f"c{l}", [SC, D]), ct=sb(f"ct{l}", [D, SC]),
                sq=sb(f"sq{l}", [128, H * HD]),
                ss=sb(f"ss{l}", [S, H]), ms=sb(f"ms{l}", [S, H]), r=sb(f"r{l}", [S, H]),
                kss=sb(f"kss{l}", [SC, H]), kms=sb(f"kms{l}", [SC, H]), kr=sb(f"kr{l}", [SC, H]),
                q=sb(f"q{l}", [S, H * HD]),
                kn=sb(f"kn{l}", [128, H * HD]),
                v=sb(f"v{l}", [SC, H, HD]),
                qt=sb(f"qt{l}", [128, CH, S]), km=sb(f"km{l}", [128, CH, 2, SC]),
                mx=sb(f"mx{l}", [S, 2, HH]), p=sb(f"p{l}", [S, 2, HH, SC]), sm=sb(f"sm{l}", [S, 2, HH]),
                rs=sb(f"rs{l}", [S, 2, HH]))

        lane = [lane_buffers(l) for l in range(LANES)]
        pt = [b.sq[0:SC, :].rearrange("p (i q) -> p i q", q=S) for b in lane]
        gain = sb("gain", [128, 2])
        out_t = [b.kn[:].rearrange("p (i q) -> p i q", q=S) for b in lane]
        ps = [mem.enter_context(nc.psum_tensor(f"a0_ps{l}", [128, 2, 512], F32)) for l in range(LANES)]
        block = mem.enter_context(nc.Block())

        def by_chunk(l, n):
            return ps[l][:, :, 0:4 * n].rearrange("p b (j n) -> p b j n", n=n)

        @block.sync
        def _(sp):
            load_context(sp, io, s, lane, c_in, TURNS)

        @block.tensor
        def _(pe):
            def first(t, l):
                return isinstance(t, int) and t == 0 and l == 0

            def inputs(t, l):
                pe.wait_ge(s.xn, nth(t, l))
                pe.wait_ge(c_in[l], 16 * t + 16)
                pe.transpose(ps[l][:, 0, 0:S], lane[l].xn[:], m.ident[:])
                pe.transpose(ps[l][:, 0, S:S + SC], lane[l].c[:], m.ident[0:SC, 0:SC]).then_inc(s.xt_ps, 1)

            def project(l, out, lhs, w, done):
                for n in range(2):
                    mm = pe.matmul(out[:, n, :], lhs, w[:, 512 * n:512 * n + 512], start=True, stop=True)
                mm.then_inc(done, 1)

            def project_k(t, l):
                if first(t, l):
                    pe.wait_ge(m.s_wk0, 16)
                pe.wait_ge(s.xt, nth(t, l))
                project(l, ps[l][0:SC], lane[l].ct[:], m.wk0, s.k_ps)

            def project_v(t, l):
                if first(t, l):
                    pe.wait_ge(m.s_wv0, 16)
                pe.wait_ge(s.k, nth(t, l))
                project(l, ps[l][0:SC], lane[l].ct[:], m.wv0, s.v_ps)

            def project_q(t, l):
                if first(t, l):
                    pe.wait_ge(m.s_wq0, 16)
                pe.wait_ge(s.v, nth(t, l))
                project(l, ps[l], lane[l].xt[:], m.wq0, s.q_ps)

            def transpose_q(t, l):
                pe.wait_ge(s.q, nth(t, l))
                for j in range(HH):
                    mm = pe.transpose(ps[l][:, j // 4, j % 4 * S:j % 4 * S + S],
                                      lane[l].q[:, 128 * j:128 * j + 128], m.ident[:])
                mm.then_inc(s.qt_ps, 1)

            def transpose_k(t, l):
                pe.wait_ge(s.k_n, nth(t, l))
                pe.wait_ge(s.qt, nth(t, l))
                for j in range(CH):
                    mm = pe.transpose(ps[l][:, j // 4, j % 4 * 128:j % 4 * 128 + SC],
                                      lane[l].kn[0:SC, 128 * j:128 * j + 128], m.ident[0:SC, 0:SC])
                mm.then_inc(s.kt_ps, 1)

            def scores(k):
                def step(t, l):
                    if k:
                        pe.wait_ge(half[0].s_q, nth(t, l))
                    else:
                        pe.wait_ge(s.km, nth(t, l))
                    for c in range(CH // 2):
                        mm = pe.matmul(ps[l][:, c // 2, c % 2 * 2 * SC:(c % 2 + 1) * 2 * SC],
                                       lane[l].qt[:, CH // 2 * k + c, :], lane[l].km[:, CH // 2 * k + c],
                                       start=True, stop=True)
                    mm.then_inc(half[k].s_ps, 1)
                return step

            def transpose_p(k):
                def step(t, l):
                    pe.wait_ge(half[k].p, nth(t, l))
                    if k:
                        pe.wait_ge(half[0].ot, nth(t, l))
                    else:
                        pe.wait_ge(half[1].s_q, nth(t, l))
                    for i in range(HH):
                        mm = pe.transpose(ps[l][0:SC, i // 4, i % 4 * S:i % 4 * S + S], lane[l].p[:, k, i, :],
                                          m.ident[:])
                    mm.then_inc(half[k].pt_ps, 1)
                return step

            def mix_v(k):
                def step(t, l):
                    pe.wait_ge(half[k].pt, nth(t, l))
                    for i in range(HH):
                        mm = pe.matmul(ps[l][HD * (i % 2):HD * (i % 2) + HD, k, i // 2 * S:i // 2 * S + S],
                                       lane[l].v[:, HH * k + i, :], pt[l][:, i, :], start=True, stop=True)
                    mm.then_inc(half[k].ot_ps, 1)
                return step

            def project_o(t, l):
                if first(t, l):
                    pe.wait_ge(m.s_wo0, 16)
                pe.wait_ge(half[1].ot, nth(t, l))
                for j in range(HH):
                    pe.matmul(ps[l][:, 0, 0:D], out_t[l][:, j, :], m.wo0[:, j, :], start=(j == 0), stop=False)
                pe.matmul(ps[l][:, 0, 0:D], m.ones_row[:], m.rows[0:1, m.row_bo0, :], start=False, stop=True
                          ).then_inc(s.y_ps, 1)

            staggered(pe, TURNS, LANES, PLACES, {
                0: inputs, 1: project_k, 2: project_v, 4: project_q, 6: transpose_q, 7: transpose_k,
                9: scores(0), 12: scores(1), 15: transpose_p(0), 16: mix_v(0), 18: transpose_p(1), 19: mix_v(1),
                20: project_o})

        @block.scalar
        def _(act):
            def inputs(t, l):
                act.wait_ge(s.xt_ps, nth(t, l))
                act.copy(lane[l].xt[:], ps[l][:, 0, 0:S])
                act.copy(lane[l].ct[:], ps[l][:, 0, S:S + SC]).then_inc(s.xt, 1)

            def copy_k(t, l):
                act.wait_ge(s.k_ps, nth(t, l))
                act.copy(lane[l].kn[0:SC, :], ps[l][0:SC].rearrange("p b n -> p (b n)")).then_inc(s.k, 1)

            def square_k(t, l):
                act.wait_ge(s.k, nth(t, l))
                act.activation(lane[l].sq[0:SC, :], lane[l].kn[0:SC, :], ACT.Square).then_inc(s.k_sq, 1)

            def copy_v(t, l):
                act.wait_ge(s.v_ps, nth(t, l))
                act.copy(lane[l].v[:, :, 0:HD],
                         ps[l][0:SC].rearrange("p b (h e) -> p (b h) e", e=HD)).then_inc(s.v, 1)

            def copy_q(t, l):
                act.wait_ge(s.q_ps, nth(t, l))
                act.copy(lane[l].q[:], ps[l][:].rearrange("p b n -> p (b n)")).then_inc(s.q, 1)

            def square_q(t, l):
                act.wait_ge(s.q, nth(t, l))
                act.wait_ge(s.k_ss, nth(t, l))
                act.activation(lane[l].sq[:], lane[l].q[:], ACT.Square).then_inc(s.q_sq, 1)

            def copy_qt(t, l):
                act.wait_ge(s.qt_ps, nth(t, l))
                act.copy(lane[l].qt[:].rearrange("p (b j) q -> p b j q", b=2), by_chunk(l, S)).then_inc(s.qt, 1)

            def exponential(k):
                def step(t, l):
                    act.wait_ge(half[k].s_sub, nth(t, l))
                    act.activation(lane[l].p[:, k], lane[l].p[:, k], ACT.Exp, scale=HD ** -0.5
                                   ).then_inc(half[k].e, 1)
                return step

            def copy_pt(k):
                def step(t, l):
                    act.wait_ge(half[k].pt_ps, nth(t, l))
                    act.copy(pt[l].rearrange("p (b j) q -> p b j q", b=2), by_chunk(l, S)[0:SC]).then_inc(half[k].pt, 1)
                return step

            def copy_ot(k):
                def step(t, l):
                    act.wait_ge(half[k].ot_ps, nth(t, l))
                    act.copy(out_t[l][:, CH // 2 * k:CH // 2 * (k + 1), :],
                             ps[l][:, k, :].rearrange("p (c q) -> p c q", q=S)).then_inc(half[k].ot, 1)
                return step

            staggered(act, TURNS, LANES, PLACES, {
                -1: inputs, 1: copy_k, 2: copy_v, 3: square_k, 4: copy_q, 5: square_q, 6: copy_qt,
                12: exponential(0), 14: exponential(1), 15: copy_pt(0), 16: copy_ot(0), 18: copy_pt(1),
                19: copy_ot(1)})

        @block.gpsimd
        def _(pool):
            def root_ln(t, l):
                pool.wait_ge(s.var_eps, nth(t, l))
                inverse_root(pool, lane[l].rstd[:], lane[l].var_eps[:], m, s.rstd)

            def root_k(t, l):
                pool.wait_ge(s.k_ms, nth(t, l))
                inverse_root(pool, lane[l].kr[:], lane[l].kms[:], m, s.k_r)

            def root_q(t, l):
                pool.wait_ge(s.q_ms, nth(t, l))
                inverse_root(pool, lane[l].r[:], lane[l].ms[:], m, s.q_r)

            staggered(pool, TURNS, LANES, PLACES, {
                -6: root_ln, 4: root_k, 7: root_q})

        @block.vector
        def _(dve):
            dve.memset(gain[:], 0.0).then_inc(s.gzero, 1)
            dve.wait_ge(s.gzero, 1)
            for odd in range(2):
                row = slice(HD * odd, HD * odd + HD)
                dve.tensor_copy(gain[row, odd:odd + 1], m.gqk[row, :]).then_inc(s.gain, 1)
            dve.wait_ge(s.gain, 2)

            def stats(t, l):
                if isinstance(t, int) and t == 1 and l == 0:
                    dve.wait_ge(m.s_x_rest, 16)
                token_stats(dve, m, s, lane[l], t * LANES + l, nth(t, l))

            def normalise(t, l):
                dve.wait_ge(s.rstd, nth(t, l))
                dve.tensor_scalar(lane[l].xn[:], m.x[:, bass.ds((t * LANES + l) * D, D)], lane[l].mv[:, 0:1],
                                  lane[l].rstd[:], ALU.subtract, ALU.mult).then_inc(s.xn, 1)

            def mean_square_k(t, l):
                dve.wait_ge(s.k_sq, nth(t, l))
                dve.tensor_reduce(lane[l].kss[:], lane[l].sq[0:SC].rearrange("p (h e) -> p h e", e=HD), AX.X,
                                  ALU.add).then_inc(s.k_ss, 1)
                dve.wait_ge(s.k_ss, nth(t, l))
                dve.tensor_scalar(lane[l].kms[:], lane[l].kss[:], 1.0 / HD, 1e-6, ALU.mult, ALU.add).then_inc(s.k_ms, 1)

            def scale_k(t, l):
                dve.wait_ge(s.k_r, nth(t, l))
                kn = lane[l].kn[0:SC].rearrange("p (h e) -> p h e", e=HD)
                dve.tensor_tensor(kn, kn, bcast(lane[l].kr[:], HD), ALU.mult).then_inc(s.k_n, 1)

            def mean_square_q(t, l):
                dve.wait_ge(s.q_sq, nth(t, l))
                dve.tensor_reduce(lane[l].ss[:], lane[l].sq[:].rearrange("p (h e) -> p h e", e=HD), AX.X, ALU.add
                                  ).then_inc(s.q_ss, 1)
                dve.wait_ge(s.q_ss, nth(t, l))
                dve.tensor_scalar(lane[l].ms[:], lane[l].ss[:], 1.0 / HD, 1e-6, ALU.mult, ALU.add).then_inc(s.q_ms, 1)

            def mask_k(t, l):
                dve.wait_ge(s.kt_ps, nth(t, l))
                dve.tensor_tensor(lane[l].km[:], ps[l][:].rearrange("p b (j n) -> p (b j) n", n=128)[:, :, 0:SC]
                                  .unsqueeze(2).broadcast_to([128, CH, 2, SC]),
                                  gain[:].unsqueeze(1).unsqueeze(3).broadcast_to([128, CH, 2, SC]), ALU.mult
                                  ).then_inc(s.km, 1)

            def scale_scores(k):
                def step(t, l):
                    r = lane[l].r[:, HH * k:HH * k + HH].rearrange("p (b j) -> p b j", b=2)
                    dve.wait_ge(s.q_r, nth(t, l))
                    dve.wait_ge(half[k].s_ps, nth(t, l))
                    dve.tensor_tensor(lane[l].p[:, k].rearrange("p (b j) n -> p b j n", b=2), by_chunk(l, SC),
                                      r.unsqueeze(3).broadcast_to([S, 2, 4, SC]), ALU.mult).then_inc(half[k].s_q, 1)
                return step

            def less_maximum(k):
                def step(t, l):
                    dve.wait_ge(half[k].s_q, nth(t, l))
                    dve.tensor_reduce(lane[l].mx[:, k], lane[l].p[:, k], AX.X, ALU.max).then_inc(half[k].s_max, 1)
                    dve.wait_ge(half[k].s_max, nth(t, l))
                    dve.tensor_tensor(lane[l].p[:, k], lane[l].p[:, k], bcast(lane[l].mx[:, k], SC), ALU.subtract
                                      ).then_inc(half[k].s_sub, 1)
                return step

            def normalise_p(k):
                def step(t, l):
                    dve.wait_ge(half[k].e, nth(t, l))
                    dve.tensor_reduce(lane[l].sm[:, k], lane[l].p[:, k], AX.X, ALU.add).then_inc(half[k].sum, 1)
                    dve.wait_ge(half[k].sum, nth(t, l))
                    dve.reciprocal(lane[l].rs[:, k], lane[l].sm[:, k]).then_inc(half[k].rs, 1)
                    dve.wait_ge(half[k].rs, nth(t, l))
                    dve.tensor_tensor(lane[l].p[:, k], lane[l].p[:, k], bcast(lane[l].rs[:, k], SC), ALU.mult
                                      ).then_inc(half[k].p, 1)
                return step

            def residual(t, l):
                xb = m.x[:, bass.ds((t * LANES + l) * D, D)]
                dve.wait_ge(s.y_ps, nth(t, l))
                dve.scalar_tensor_tensor(xb, ps[l][:, 0, 0:D], m.tg[:, 0:1], xb, ALU.mult, ALU.add).then_inc(s.x, 1)

            staggered(dve, TURNS, LANES, PLACES, {
                -5: stats, -3: normalise, 3: mean_square_k, 5: scale_k, 6: mean_square_q, 7: mask_k,
                10: scale_scores(0), 11: less_maximum(0), 12: scale_scores(1), 13: less_maximum(1),
                14: normalise_p(0), 16: normalise_p(1), 21: residual})


@sublayer
def l0_ffn(nc, ctx, m, io):
    E, SE, F = 16, 64, 256
    NS = E * SE
    NC = NS // 128
    LANES = 4
    TURNS = B // LANES
    s = semaphores(nc, ctx, "f0", "w vecs se se_stats se_mv se_ve se_r se_n se_ps gs bs set stats mv var_eps rstd x1 "
                   "stats2 mv2 var_eps2 rstd2 x2 xg xs xst_ps xst lt_ps lt_max lt_neg lt_exp lt_r dt d_ps d "
                   "sl_ps sl l_ps l_max l_neg c ct_ps ct gu_ps gelu h eo_ps eot eoe_ps eo y_ps yr yg free")

    def nth(turn, lane):
        return turn * LANES + lane + 1

    def nth_e(turn, e):
        return turn * E + e + 1

    with ExitStack() as mem:
        def sb(name, shape, dt=F32):
            return mem.enter_context(nc.sbuf_tensor("f0_" + name, shape, dt))

        wg, wu, wd = sb("wg", [D, E, F]), sb("wu", [D, E, F]), sb("wd", [128, E, 2, D])
        bg, bu, bd = sb("bg", [128, E, 2]), sb("bu", [128, E, 2]), sb("bd", [D, E])
        g_row, b_row = sb("g_row", [128, D]), sb("b_row", [128, D])
        slot_g, slot_b, scale = sb("slot_g", [D, 1]), sb("slot_b", [D, 1]), sb("scale", [D, 1])
        gs, bs = sb("gs", [D, 1]), sb("bs", [D, 1])
        set_ = sb("set", [D, NC, 128])
        se_stats, se_mv, se_ve, se_r = (sb("se_stats", [128, NC, 6]), sb("se_mv", [128, NC, 2]), sb("se_ve", [128, NC]),
                                        sb("se_r", [128, NC]))
        d_all = sb("d_all", [128, LANES, NS])
        t_all = sb("t_all", [128, LANES, NC, S])
        sl_all = sb("sl_all", [D, LANES, NS])
        hg = [sb(f"hg{k}", [128, 2, LANES * SE]) for k in range(2)]
        hh = [sb(f"hh{k}", [128, 2, LANES * SE]) for k in range(2)]
        se = d_all[:, 0, :].rearrange("p (c d) -> p c d", d=D)
        lane = [Names(
            stats=sb(f"stats{l}", [S, 6]), mv=sb(f"mv{l}", [S, 2]), var_eps=sb(f"var{l}", [S, 1]),
            rstd=sb(f"rstd{l}", [S, 1]), stats2=sb(f"stats2{l}", [S, 6]), mv2=sb(f"mv2{l}", [S, 2]),
            var_eps2=sb(f"var2{l}", [S, 1]), rstd2=sb(f"rstd2{l}", [S, 1]),
            x1=sb(f"x1{l}", [S, D]), xs=sb(f"xs{l}", [S, D]), xst=sb(f"xst{l}", [D, S]),
            mx=sb(f"mx{l}", [128, NC]), tneg=sb(f"tneg{l}", [128, NC]), sum=sb(f"sum{l}", [128, NC]), r=sb(f"r{l}", [128, NC]),
            cmx=sb(f"cmx{l}", [S, 1]), neg=sb(f"neg{l}", [S, 1]), csum=sb(f"csum{l}", [S, 1]),
            cr=sb(f"cr{l}", [S, 1]), cg=sb(f"cg{l}", [S, 1]),
            t=t_all[:, l], d=d_all[:, l, :], sl=sl_all[:, l, :]) for l in range(LANES)]
        ps = [mem.enter_context(nc.psum_tensor(f"f0_ps{l}", [128, 2, 512], F32)) for l in range(LANES)]
        gate_ps = [ps[2 * k][:, 0, :].rearrange("p (c n) -> p c n", c=2) for k in range(2)]
        up_ps = [ps[2 * k][:, 1, :].rearrange("p (c n) -> p c n", c=2) for k in range(2)]
        eo_ps = [ps[2 * k + 1][:, 0, 0:LANES * SE] for k in range(2)]
        block = mem.enter_context(nc.Block())

        def flat(p):
            return p.rearrange("p b n -> p (b n)")

        @block.sync
        def _(sp):
            sp.dma_start(se, io.slot_embeds.rearrange("e s d -> (e s) d").rearrange("(c p) d -> p c d", p=128)
                         ).then_inc(s.se, 16)
            for dst, src in ((g_row[:], io.norm_g.partition_broadcast(128)), (b_row[:], io.norm_b.partition_broadcast(128)),
                             (slot_g[:], io.slot_g.unsqueeze(1)), (slot_b[:], io.slot_b.unsqueeze(1)),
                             (scale[:], io.scale.partition_broadcast(128))):
                sp.dma_start(dst, src).then_inc(s.vecs, 16)
            for dst, src in ((wg[:], io.Wg), (wu[:], io.Wu), (wd[:], io.Wd), (bg[:], io.bg), (bu[:], io.bu), (bd[:], io.bd)):
                sp.dma_start(dst, src).then_inc(s.w, 16)

        @block.tensor
        def _(pe):
            pe.wait_ge(s.se_n, NC)
            for c in range(NC):
                mm = pe.transpose(ps[0][:, c // 4, c % 4 * 128:c % 4 * 128 + 128], se[:, c, :], m.ident[:])
            mm.then_inc(s.se_ps, 1)
            pe.wait_ge(s.set, 1)
            pe.wait_ge(s.w, 96)
            with pe.Fori(0, TURNS) as t:
                for l in range(LANES):
                    pe.wait_ge(s.xs, nth(t, l))
                    pe.wait_ge(s.free, nth(t, l))
                    pe.transpose(ps[l][:, 0, 0:S], lane[l].xs[:], m.ident[:]).then_inc(s.xst_ps, 1)
                for l in range(LANES):
                    pe.wait_ge(s.xst, nth(t, l))
                    for c in range(NC):
                        mm = pe.matmul(ps[l][:, c // 4, c % 4 * S:c % 4 * S + S], set_[:, c, :], lane[l].xst[:],
                                       start=True, stop=True)
                    mm.then_inc(s.lt_ps, 1)
                for l in range(LANES):
                    pe.wait_ge(s.dt, nth(t, l))
                    for c in range(NC):
                        mm = pe.transpose(ps[l][:, c // 4, c % 4 * 128:c % 4 * 128 + 128], lane[l].t[:, c, :], m.ident[:])
                    mm.then_inc(s.d_ps, 1)
                for l in range(LANES):
                    pe.wait_ge(s.d, nth(t, l))
                    for n in range(2):
                        mm = pe.matmul(ps[l][:, n, :], lane[l].xs[:], lane[l].d[:, 512 * n:512 * n + 512],
                                       start=True, stop=True)
                    mm.then_inc(s.sl_ps, 1)
                for l in range(LANES):
                    pe.wait_ge(s.sl, nth(t, l))
                    for n in range(2):
                        mm = pe.matmul(ps[l][:, n, :], lane[l].xst[:], set_[:, 4 * n:4 * n + 4, :], start=True, stop=True)
                    mm.then_inc(s.l_ps, 1)
                for l in range(LANES):
                    pe.wait_ge(s.c, nth(t, l))
                    for c in range(NC):
                        mm = pe.transpose(ps[l][:, c // 4, c % 4 * S:c % 4 * S + S], lane[l].d[:, 128 * c:128 * c + 128],
                                          m.ident[:])
                    mm.then_inc(s.ct_ps, 1)

                def gate_up(e):
                    k = e % 2
                    if e < 2:
                        pe.wait_ge(s.ct, nth(t, 2 * k + 1))
                    else:
                        pe.wait_ge(s.h, nth_e(t, e - 2))
                    rhs = sl_all[:, :, SE * e:SE * e + SE]
                    for w, out in ((wg, gate_ps[k]), (wu, up_ps[k])):
                        for c in range(2):
                            mm = pe.matmul(out[:, c, :], w[:, e, 128 * c:128 * c + 128], rhs, start=True, stop=True)
                    mm.then_inc(s.gu_ps, 1)

                def down(e):
                    k = e % 2
                    pe.wait_ge(s.h, nth_e(t, e))
                    if e >= 2:
                        pe.wait_ge(s.eot, nth_e(t, e - 2))
                    for c in range(2):
                        mm = pe.matmul(eo_ps[k], wd[:, e, c, :], hh[k][:, c, :], start=(c == 0), stop=(c == 1))
                    mm.then_inc(s.eo_ps, 1)

                gate_up(0)
                for e in range(E):
                    if e + 1 < E:
                        gate_up(e + 1)
                    down(e)
                pe.wait_ge(s.eot, nth_e(t, E - 1))
                for l in range(LANES):
                    for c in range(NC):
                        mm = pe.transpose(ps[l][:, c // 4, c % 4 * 128:c % 4 * 128 + 128],
                                          lane[l].sl[:, 128 * c:128 * c + 128], m.ident[:])
                    mm.then_inc(s.eoe_ps, 1)
                for l in range(LANES):
                    pe.wait_ge(s.eo, nth(t, l))
                    for c in range(NC):
                        mm = pe.matmul(ps[l][:, 0, 0:D], lane[l].t[:, c, :], lane[l].d[:, 128 * c:128 * c + 128],
                                       start=(c == 0), stop=(c == NC - 1))
                    mm.then_inc(s.y_ps, 1)

        @block.scalar
        def _(act):
            with act.Fori(0, TURNS) as t:
                for l in range(LANES):
                    act.wait_ge(s.xst_ps, nth(t, l))
                    act.copy(lane[l].xst[:], ps[l][:, 0, 0:S]).then_inc(s.xst, 1)
                for l in range(LANES):
                    act.wait_ge(s.lt_neg, nth(t, l))
                    for c in range(NC):
                        ex = act.activation(lane[l].t[:, c, :], ps[l][:, c // 4, c % 4 * S:c % 4 * S + S], ACT.Exp,
                                            bias=lane[l].tneg[:, c:c + 1], accum_out=lane[l].sum[:, c:c + 1])
                    ex.then_inc(s.lt_exp, 1)
                for l in range(LANES):
                    act.wait_ge(s.d_ps, nth(t, l))
                    act.copy(lane[l].d, flat(ps[l])).then_inc(s.d, 1)
                for l in range(LANES):
                    act.wait_ge(s.sl_ps, nth(t, l))
                    act.copy(lane[l].sl, flat(ps[l])).then_inc(s.sl, 1)
                for l in range(LANES):
                    act.wait_ge(s.l_neg, nth(t, l))
                    act.activation(lane[l].d, flat(ps[l]), ACT.Exp, bias=lane[l].neg[:], accum_out=lane[l].csum[:]
                                   ).then_inc(s.c, 1)
                for l in range(LANES):
                    act.wait_ge(s.ct_ps, nth(t, l))
                    act.copy(lane[l].t, ps[l][:].rearrange("p b (c n) -> p (b c) n", c=4)).then_inc(s.ct, 1)
                for e in range(E):
                    act.wait_ge(s.gu_ps, nth_e(t, e))
                    for c in range(2):
                        ge = act.activation(hg[e % 2][:, c, :], gate_ps[e % 2][:, c, :], ACT.Gelu, bias=bg[:, e, c:c + 1])
                    ge.then_inc(s.gelu, 1)
                for l in range(LANES):
                    act.wait_ge(s.eoe_ps, nth(t, l))
                    act.copy(lane[l].d, flat(ps[l])).then_inc(s.eo, 1)

        @block.gpsimd
        def _(pool):
            def roots(t):
                for l in range(LANES):
                    pool.wait_ge(s.var_eps, nth(t, l))
                    inverse_root(pool, lane[l].rstd[:], lane[l].var_eps[:], m, s.rstd)
                for l in range(LANES):
                    pool.wait_ge(s.var_eps2, nth(t, l))
                    inverse_root(pool, lane[l].rstd2[:], lane[l].var_eps2[:], m, s.rstd2)

            roots(0)
            pool.wait_ge(s.se_ve, NC)
            inverse_root(pool, se_r[:], se_ve[:], m, s.se_r)
            with pool.Fori(0, TURNS - 1) as t:
                roots(t + 1)

        @block.vector
        def _(dve):
            def first_stats(t):
                layer_norm_stats(dve, m, s, t, lane)

            def first_norm(t):
                for l in range(LANES):
                    dve.wait_ge(s.rstd, nth(t, l))
                    dve.tensor_scalar(lane[l].x1[:], m.x[:, bass.ds((t * LANES + l) * D, D)], lane[l].mv[:, 0:1],
                                      lane[l].rstd[:], ALU.subtract, ALU.mult).then_inc(s.x1, 1)

            def second_stats(t):
                for l in range(LANES):
                    dve.wait_ge(s.x1, nth(t, l))
                    dve.bn_stats(lane[l].stats2[:], lane[l].x1[:]).then_inc(s.stats2, 1)

            def second_variance(t):
                dve.wait_ge(s.stats2, nth(t, LANES - 1))
                dve.memset(m.wait_pad[:], 0.0)
                for l in range(LANES):
                    dve.bn_aggr(lane[l].mv2[:], lane[l].stats2[:]).then_inc(s.mv2, 1)
                for l in range(LANES):
                    dve.wait_ge(s.mv2, nth(t, l))
                    dve.tensor_scalar(lane[l].var_eps2[:], lane[l].mv2[:, 1:2], LN_EPS, None, ALU.add).then_inc(s.var_eps2, 1)

            def second_norm(t):
                for l in range(LANES):
                    dve.wait_ge(s.rstd2, nth(t, l))
                    dve.tensor_scalar(lane[l].x1[:], lane[l].x1[:], lane[l].mv2[:, 0:1], lane[l].rstd2[:],
                                      ALU.subtract, ALU.mult).then_inc(s.x2, 1)

            def times_g(t):
                for l in range(LANES):
                    dve.wait_ge(s.x2, nth(t, l))
                    dve.tensor_tensor(lane[l].x1[:], lane[l].x1[:], g_row[:], ALU.mult).then_inc(s.xg, 1)

            def plus_b(t):
                for l in range(LANES):
                    dve.wait_ge(s.xg, nth(t, l))
                    dve.tensor_tensor(lane[l].xs[:], lane[l].x1[:], b_row[:], ALU.add).then_inc(s.xs, 1)

            norms = (first_stats, first_norm, second_stats, second_variance, second_norm, times_g, plus_b)
            for norm in norms:
                if norm is times_g:
                    dve.wait_ge(s.vecs, 80)
                norm(0)

            dve.wait_ge(s.se, 16)
            for c in range(NC):
                dve.bn_stats(se_stats[:, c, :], se[:, c, :]).then_inc(s.se_stats, 1)
            for c in range(NC):
                dve.wait_ge(s.se_stats, c + 1)
                dve.bn_aggr(se_mv[:, c, :], se_stats[:, c, :]).then_inc(s.se_mv, 1)
            for c in range(NC):
                dve.wait_ge(s.se_mv, c + 1)
                dve.tensor_scalar(se_ve[:, c:c + 1], se_mv[:, c, 1:2], LN_EPS, None, ALU.add).then_inc(s.se_ve, 1)
            dve.tensor_tensor(gs[:], slot_g[:], scale[:], ALU.mult).then_inc(s.gs, 1)
            dve.tensor_tensor(bs[:], slot_b[:], scale[:], ALU.mult).then_inc(s.bs, 1)
            dve.wait_ge(s.se_r, 1)
            for c in range(NC):
                dve.tensor_scalar(se[:, c, :], se[:, c, :], se_mv[:, c, 0:1], se_r[:, c:c + 1], ALU.subtract, ALU.mult
                                  ).then_inc(s.se_n, 1)
            dve.wait_ge(s.se_ps, 1)
            dve.wait_ge(s.gs, 1)
            dve.wait_ge(s.bs, 1)
            dve.tensor_scalar(set_[:].rearrange("p c n -> p (c n)"), flat(ps[0]), gs[:], bs[:], ALU.mult, ALU.add
                              ).then_inc(s.set, 1)

            def turn(t, ahead):
                for l in range(LANES):
                    logits = ps[l][:].rearrange("p b (c n) -> p (b c) n", c=4)
                    dve.wait_ge(s.lt_ps, nth(t, l))
                    dve.tensor_reduce(lane[l].mx[:], logits, AX.X, ALU.max).then_inc(s.lt_max, 1)
                    dve.wait_ge(s.lt_max, nth(t, l))
                    dve.tensor_scalar(lane[l].tneg[:], lane[l].mx[:], -1.0, None, ALU.mult).then_inc(s.lt_neg, 1)
                for l in range(LANES):
                    dve.wait_ge(s.lt_exp, nth(t, l))
                    dve.reciprocal(lane[l].r[:], lane[l].sum[:]).then_inc(s.lt_r, 1)
                    dve.wait_ge(s.lt_r, nth(t, l))
                    dve.tensor_tensor(lane[l].t, lane[l].t, bcast(lane[l].r[:], S), ALU.mult).then_inc(s.dt, 1)
                for l in range(LANES):
                    dve.wait_ge(s.l_ps, nth(t, l))
                    dve.tensor_reduce(lane[l].cmx[:], ps[l][:], AX.XY, ALU.max).then_inc(s.l_max, 1)
                    dve.wait_ge(s.l_max, nth(t, l))
                    dve.tensor_scalar(lane[l].neg[:], lane[l].cmx[:], -1.0, None, ALU.mult).then_inc(s.l_neg, 1)

                def hidden(e):
                    k = e % 2
                    dve.wait_ge(s.gelu, nth_e(t, e))
                    if e >= 2:
                        dve.wait_ge(s.eo_ps, nth_e(t, e - 2))
                    for c in range(2):
                        mul = dve.scalar_tensor_tensor(hh[k][:, c, :], up_ps[k][:, c, :], bu[:, e, c:c + 1],
                                                       hg[k][:, c, :], ALU.add, ALU.mult)
                    mul.then_inc(s.h, 1)

                def outputs(e):
                    k = e % 2
                    dve.wait_ge(s.eo_ps, nth_e(t, e))
                    dve.tensor_scalar(sl_all[:, :, SE * e:SE * e + SE], eo_ps[k].rearrange("p (b n) -> p b n", n=SE),
                                      bd[:, e:e + 1], None, ALU.add).then_inc(s.eot, 1)

                hidden(0)
                for e in range(E):
                    if e + 1 < E:
                        hidden(e + 1)
                    outputs(e)
                    if ahead and e % 2 and e // 2 < len(norms):
                        norms[e // 2](t + 1)
                for l in range(LANES):
                    dve.wait_ge(s.c, nth(t, l))
                    dve.reciprocal(lane[l].cr[:], lane[l].csum[:]).then_inc(s.yr, 1)
                for l in range(LANES):
                    dve.wait_ge(s.yr, nth(t, l))
                    dve.tensor_tensor(lane[l].cg[:], lane[l].cr[:], m.tg[:, 4:5], ALU.mult).then_inc(s.yg, 1)
                for l in range(LANES):
                    xb = m.x[:, bass.ds((t * LANES + l) * D, D)]
                    dve.wait_ge(s.yg, nth(t, l))
                    dve.wait_ge(s.y_ps, nth(t, l))
                    dve.scalar_tensor_tensor(xb, ps[l][:, 0, 0:D], lane[l].cg[:], xb, ALU.mult, ALU.add).then_inc(s.free, 1)

            for l in range(LANES):
                dve.memset(lane[l].cg[:], 0.0).then_inc(s.free, 1)
            with dve.Fori(0, TURNS - 1) as t:
                turn(t, ahead=True)
            turn(TURNS - 1, ahead=False)


@sublayer
def l1_attention(nc, ctx, m, io):
    LANES = 4
    TURNS = B // LANES
    PLACES = 12
    SCALE = D ** -0.5
    s = semaphores(nc, ctx, "a1", "stats mv var_eps rstd xn xt_ps xt qkv_ps qkv s_ps s_max neg p pt_ps pt "
                   "o_ps r g x c0 c1 c2 c3")
    c_in = [s.c0, s.c1, s.c2, s.c3]

    def nth(turn, lane):
        return turn * LANES + lane + 1

    with ExitStack() as mem:
        def sb(name, shape, dt=F32):
            return mem.enter_context(nc.sbuf_tensor("a1_" + name, shape, dt))

        lane = [Names(
            stats=sb(f"stats{l}", [S, 6]), mv=sb(f"mv{l}", [S, 2]), var_eps=sb(f"var{l}", [S, 1]),
            rstd=sb(f"rstd{l}", [S, 1]), xn=sb(f"xn{l}", [S, D]), xt=sb(f"xt{l}", [D, S]),
            c=sb(f"c{l}", [SC, D]), ct=sb(f"ct{l}", [D, SC]), qt=sb(f"qt{l}", [D, S]), kt=sb(f"kt{l}", [D, SC]),
            v=sb(f"v{l}", [SC, D]), mx=sb(f"mx{l}", [S, 1]), neg=sb(f"neg{l}", [S, 1]), p=sb(f"p{l}", [S, SC]),
            sum=sb(f"sum{l}", [S, 1]), r=sb(f"r{l}", [S, 1]), g=sb(f"g{l}", [S, 1]), pt=sb(f"pt{l}", [SC, S]))
            for l in range(LANES)]
        ps = [mem.enter_context(nc.psum_tensor(f"a1_ps{l}", [128, 2, 512], F32)) for l in range(LANES)]
        block = mem.enter_context(nc.Block())

        @block.sync
        def _(sp):
            load_context(sp, io, s, lane, c_in, TURNS)

        @block.tensor
        def _(pe):
            def inputs(t, l):
                pe.wait_ge(s.xn, nth(t, l))
                pe.wait_ge(c_in[l], 16 * t + 16)
                pe.transpose(ps[l][:, 0, 0:S], lane[l].xn[:], m.ident[:])
                pe.transpose(ps[l][:, 0, S:S + SC], lane[l].c[:], m.ident[0:SC, 0:SC]).then_inc(s.xt_ps, 1)

            def project(t, l):
                pe.wait_ge(s.xt, nth(t, l))
                pe.matmul(ps[l][:, 1, 0:S], m.wq1[:], lane[l].xt[:], start=True, stop=True)
                pe.matmul(ps[l][:, 1, S:S + SC], m.wk1[:], lane[l].ct[:], start=True, stop=True)
                pe.matmul(ps[l][0:SC, 1, 256:256 + D], lane[l].ct[:], m.wv1[:], start=True, stop=False)
                pe.matmul(ps[l][0:SC, 1, 256:256 + D], m.ones_row[:, 0:SC], m.rows[0:1, m.row_bv1, :],
                          start=False, stop=True).then_inc(s.qkv_ps, 1)

            def scores(t, l):
                pe.wait_ge(s.qkv, nth(t, l))
                pe.matmul(ps[l][:, 0, 0:SC], lane[l].qt[:], lane[l].kt[:], start=True, stop=True).then_inc(s.s_ps, 1)

            def transpose_p(t, l):
                pe.wait_ge(s.p, nth(t, l))
                pe.transpose(ps[l][0:SC, 1, 0:S], lane[l].p[:], m.ident[:]).then_inc(s.pt_ps, 1)

            def mix_v(t, l):
                pe.wait_ge(s.pt, nth(t, l))
                pe.matmul(ps[l][:, 0, 0:D], lane[l].pt[:], lane[l].v[:], start=True, stop=True).then_inc(s.o_ps, 1)

            staggered(pe, TURNS, LANES, PLACES, {0: inputs, 2: project, 5: scores, 8: transpose_p, 10: mix_v})

        @block.scalar
        def _(act):
            if m.load_next:
                m.load_next(act)

            def inputs(t, l):
                act.wait_ge(s.xt_ps, nth(t, l))
                act.copy(lane[l].xt[:], ps[l][:, 0, 0:S])
                act.copy(lane[l].ct[:], ps[l][:, 0, S:S + SC]).then_inc(s.xt, 1)

            def copy_qkv(t, l):
                act.wait_ge(s.qkv_ps, nth(t, l))
                act.activation(lane[l].qt[:], ps[l][:, 1, 0:S], ACT.Identity, bias=m.bqk1[:, 0:1])
                act.activation(lane[l].kt[:], ps[l][:, 1, S:S + SC], ACT.Identity, bias=m.bqk1[:, 1:2])
                act.copy(lane[l].v[:], ps[l][0:SC, 1, 256:256 + D]).then_inc(s.qkv, 1)

            def exponential(t, l):
                act.wait_ge(s.neg, nth(t, l))
                act.activation(lane[l].p[:], ps[l][:, 0, 0:SC], ACT.Exp, bias=lane[l].neg[:], scale=SCALE,
                               accum_out=lane[l].sum[:]).then_inc(s.p, 1)

            def copy_pt(t, l):
                act.wait_ge(s.pt_ps, nth(t, l))
                act.copy(lane[l].pt[:], ps[l][0:SC, 1, 0:S]).then_inc(s.pt, 1)

            staggered(act, TURNS, LANES, PLACES, {0: inputs, 2: copy_qkv, 6: exponential, 8: copy_pt})

        @block.gpsimd
        def _(pool):
            def root_ln(t, l):
                pool.wait_ge(s.var_eps, nth(t, l))
                inverse_root(pool, lane[l].rstd[:], lane[l].var_eps[:], m, s.rstd)

            staggered(pool, TURNS, LANES, PLACES, {-3: root_ln})

        @block.vector
        def _(dve):
            def stats(t, l):
                token_stats(dve, m, s, lane[l], t * LANES + l, nth(t, l))

            def normalise(t, l):
                dve.wait_ge(s.rstd, nth(t, l))
                dve.tensor_scalar(lane[l].xn[:], m.x[:, bass.ds((t * LANES + l) * D, D)], lane[l].mv[:, 0:1],
                                  lane[l].rstd[:], ALU.subtract, ALU.mult).then_inc(s.xn, 1)

            def maximum(t, l):
                dve.wait_ge(s.s_ps, nth(t, l))
                dve.reduce_max(lane[l].mx[:], ps[l][:, 0, 0:SC], AX.X).then_inc(s.s_max, 1)
                dve.wait_ge(s.s_max, nth(t, l))
                dve.tensor_scalar(lane[l].neg[:], lane[l].mx[:], -SCALE, None, ALU.mult).then_inc(s.neg, 1)

            def gate(t, l):
                dve.wait_ge(s.p, nth(t, l))
                dve.reciprocal(lane[l].r[:], lane[l].sum[:]).then_inc(s.r, 1)
                dve.wait_ge(s.r, nth(t, l))
                dve.tensor_tensor(lane[l].g[:], lane[l].r[:], m.tg[:, 1:2], ALU.mult).then_inc(s.g, 1)

            def residual(t, l):
                xb = m.x[:, bass.ds((t * LANES + l) * D, D)]
                dve.wait_ge(s.g, nth(t, l))
                dve.wait_ge(s.o_ps, nth(t, l))
                dve.scalar_tensor_tensor(xb, ps[l][:, 0, 0:D], lane[l].g[:], xb, ALU.mult, ALU.add).then_inc(s.x, 1)

            staggered(dve, TURNS, LANES, PLACES, {
                -3: stats, -2: normalise, 5: maximum, 8: gate, 10: residual})


@sublayer
def top2_ffn(nc, ctx, m, weights):
    E, FC = 8, 2
    LANES = 4
    TURNS = B // LANES
    s = semaphores(nc, ctx, "f1", "stats mv var_eps rstd xn xt_ps xt r_ps r top idx sub share share2 onehot idxf "
                   "wt wt1 up_ps up h y_ps acc x iota")

    def nth(turn, lane):
        return turn * LANES + lane + 1

    def nth_c(turn, e, c):
        return turn * (E * FC) + e * FC + c + 1

    def nth_e(turn, e):
        return turn * E + e + 1

    def turns(eng, turn):
        with eng.Fori(0, TURNS // 2 - 1) as pair:
            for parity in range(2):
                turn(pair * 2 + parity, parity, True)
        turn(TURNS - 2, 0, True)
        turn(TURNS - 1, 1, False)

    with ExitStack() as mem:
        def sb(name, shape, dt=F32):
            return mem.enter_context(nc.sbuf_tensor("f1_" + name, shape, dt))

        wr, w1, w2, w3 = weights.wr, weights.w1, weights.w2, weights.w3
        experts = sb("experts", [S, E])
        xt = [sb(f"xt{k}", [D, LANES, S]) for k in range(2)]
        wt = [[sb(f"wt{k}{l}", [S, E]) for l in range(LANES)] for k in range(2)]
        NH = 2 * FC
        silu = [sb(f"silu{k}", [128, LANES * S]) for k in range(2)]
        hid = [sb(f"hid{k}", [128, LANES * S]) for k in range(NH)]
        acc = sb("acc", [S, LANES, D])
        lane = [Names(
            stats=sb(f"stats{l}", [S, 6]), mv=sb(f"mv{l}", [S, 2]), var_eps=sb(f"var{l}", [S, 1]),
            rstd=sb(f"rstd{l}", [S, 1]), xn=sb(f"xn{l}", [S, D]), r=sb(f"r{l}", [S, E]), top=sb(f"top{l}", [S, 8]),
            idx=sb(f"idx{l}", [S, 8], U32), idxf=sb(f"idxf{l}", [S, 8]), sub=sb(f"sub{l}", [S, 1]),
            share=sb(f"share{l}", [S, 2]), oh=sb(f"oh{l}", [S, E]), oh2=sb(f"oh2{l}", [S, E])) for l in range(LANES)]
        misc = mem.enter_context(nc.psum_tensor("f1_misc", [128, 2, 512], F32))
        up = mem.enter_context(nc.psum_tensor("f1_up", [128, 4, 512], F32))
        yps = mem.enter_context(nc.psum_tensor("f1_y", [128, 2, 512], F32))
        block = mem.enter_context(nc.Block())

        if 2 not in PHASES:
            @block.sync
            def _(sp):
                weights.load(sp)

        @block.tensor
        def _(pe):
            def transposes(t):
                for l in range(LANES):
                    pe.wait_ge(s.xn, nth(t, l))
                    pe.transpose(misc[:, 0, S * l:S * l + S], lane[l].xn[:], m.ident[:]).then_inc(s.xt_ps, 1)

            def router(t, parity):
                pe.wait_ge(s.xt, t + 1)
                for l in range(LANES):
                    pe.matmul(misc[:, 1, E * l:E * l + E], xt[parity][:, l, :], wr[:], start=True, stop=True
                              ).then_inc(s.r_ps, 1)

            def turn(t, parity, ahead):
                def first(e, c):
                    k = c
                    if e:
                        pe.wait_ge(s.h, nth_c(t, e, c) - FC)
                    pe.matmul(up[:, 2 * k, :], w1[:, e, c, :], xt[parity][:], start=True, stop=True)
                    pe.matmul(up[:, 2 * k + 1, :], w2[:, e, c, :], xt[parity][:], start=True, stop=True
                              ).then_inc(s.up_ps, 1)

                def second(e):
                    pe.wait_ge(s.h, nth_c(t, e, FC - 1))
                    if e >= 2:
                        pe.wait_ge(s.acc, nth_e(t, e - 2))
                    for l in range(LANES):
                        for c in range(FC):
                            mm = pe.matmul(yps[:, e % 2, D * l:D * l + D], hid[(e * FC + c) % NH][:, S * l:S * l + S],
                                           w3[:, e, c, :], start=(c == 0), stop=(c == FC - 1))
                    mm.then_inc(s.y_ps, 1)

                for c in range(FC):
                    first(0, c)
                for e in range(E):
                    if e + 1 < E:
                        for c in range(FC):
                            first(e + 1, c)
                    second(e)
                    if ahead and e == 1:
                        transposes(t + 1)
                    if ahead and e == 3:
                        router(t + 1, 1 - parity)

            transposes(0)
            pe.wait_ge(weights.first, 16)
            router(0, 0)
            pe.wait_ge(weights.rest, 48)
            turns(pe, turn)

        @block.scalar
        def _(act):
            def copy_xt(t, parity):
                act.wait_ge(s.xt_ps, nth(t, LANES - 1))
                act.copy(xt[parity][:], misc[:, 0, :].rearrange("p (l n) -> p l n", n=S)).then_inc(s.xt, 1)

            def best_share(t):
                for l in range(LANES):
                    act.wait_ge(s.sub, nth(t, l))
                    act.activation(lane[l].share[:, 0:1], lane[l].sub[:], ACT.Sigmoid).then_inc(s.share, 1)

            def turn(t, parity, ahead):
                for e in range(E):
                    if ahead and e == 3:
                        copy_xt(t + 1, 1 - parity)
                    if ahead and e == 7:
                        best_share(t + 1)
                    for c in range(FC):
                        act.wait_ge(s.up_ps, nth_c(t, e, c))
                        if e:
                            act.wait_ge(s.h, nth_c(t, e, c) - FC)
                        act.activation(silu[c][:], up[:, 2 * c, :], ACT.Silu).then_inc(s.up, 1)

            copy_xt(0, 0)
            best_share(0)
            turns(act, turn)

        @block.gpsimd
        def _(pool):
            pool.iota(experts[:], [[1, E]], base=0, channel_multiplier=0, allow_small_or_imprecise_dtypes=True
                      ).then_inc(s.iota, 1)
            with pool.Fori(0, TURNS) as t:
                for l in range(LANES):
                    pool.wait_ge(s.var_eps, nth(t, l))
                    inverse_root(pool, lane[l].rstd[:], lane[l].var_eps[:], m, s.rstd)

        @block.vector
        def _(dve):
            def norm_stats(t, parity):
                layer_norm_stats(dve, m, s, t, lane)

            def normalise(t, parity):
                for l in range(LANES):
                    dve.wait_ge(s.rstd, nth(t, l))
                    dve.tensor_scalar(lane[l].xn[:], m.x[:, bass.ds((t * LANES + l) * D, D)], lane[l].mv[:, 0:1],
                                      lane[l].rstd[:], ALU.subtract, ALU.mult).then_inc(s.xn, 1)

            def best_scores(t, parity):
                for l in range(LANES):
                    dve.wait_ge(s.r_ps, nth(t, LANES - 1))
                    dve.tensor_copy(lane[l].r[:], misc[:, 1, E * l:E * l + E]).then_inc(s.r, 1)
                dve.wait_ge(s.r, nth(t, LANES - 1))
                dve.memset(m.wait_pad[:], 0.0)
                for l in range(LANES):
                    dve.max(lane[l].top[:], lane[l].r[:]).then_inc(s.top, 1)

            def best_experts(t, parity):
                dve.wait_ge(s.top, nth(t, LANES - 1))
                dve.memset(m.wait_pad[:], 0.0)
                for l in range(LANES):
                    dve.max_index(lane[l].idx[:], lane[l].top[:], lane[l].r[:]).then_inc(s.idx, 1)
                for l in range(LANES):
                    dve.tensor_scalar(lane[l].sub[:], lane[l].top[:, 0:1], lane[l].top[:, 1:2], None,
                                      ALU.subtract).then_inc(s.sub, 1)

            def one_hot(t, parity):
                for l in range(LANES):
                    dve.wait_ge(s.idx, nth(t, l))
                    dve.tensor_copy(lane[l].idxf[:], lane[l].idx[:]).then_inc(s.idxf, 1)
                for l in range(LANES):
                    dve.wait_ge(s.idxf, nth(t, l))
                    dve.tensor_scalar(lane[l].oh[:], experts[:], lane[l].idxf[:, 0:1], None, ALU.is_equal
                                      ).then_inc(s.onehot, 1)

            def shares(t, parity):
                for l in range(LANES):
                    dve.wait_ge(s.share, nth(t, l))
                    dve.tensor_scalar(lane[l].share[:, 1:2], lane[l].share[:, 0:1], -1.0, 1.0, ALU.mult, ALU.add
                                      ).then_inc(s.share2, 1)
                for l in range(LANES):
                    dve.wait_ge(s.share2, nth(t, l))
                    dve.tensor_scalar(lane[l].oh2[:], experts[:], lane[l].idxf[:, 1:2], lane[l].share[:, 1:2],
                                      ALU.is_equal, ALU.mult).then_inc(s.wt1, 1)
                for l in range(LANES):
                    dve.wait_ge(s.onehot, nth(t, l))
                    dve.wait_ge(s.wt1, nth(t, l))
                    dve.scalar_tensor_tensor(wt[parity][l][:], lane[l].oh[:], lane[l].share[:, 0:1], lane[l].oh2[:],
                                             ALU.mult, ALU.add).then_inc(s.wt, 1)

            route = {0: norm_stats, 1: normalise, 4: best_scores, 5: best_experts, 6: one_hot, 7: shares}

            def turn(t, parity, ahead):
                def product(e, c):
                    dve.wait_ge(s.up, nth_c(t, e, c))
                    if e >= 2:
                        dve.wait_ge(s.y_ps, nth_e(t, e - 2))
                    dve.tensor_tensor(hid[(e * FC + c) % NH][:], silu[c][:], up[:, 2 * c + 1, :], ALU.mult
                                      ).then_inc(s.h, 1)

                def add(e):
                    dve.wait_ge(s.y_ps, nth_e(t, e))
                    if e == 0:
                        dve.wait_ge(s.wt, nth(t, LANES - 1))
                    else:
                        dve.wait_ge(s.acc, nth_e(t, e - 1))
                    for l in range(LANES):
                        y = yps[:, e % 2, D * l:D * l + D]
                        share = wt[parity][l][:, e:e + 1]
                        if e == 0:
                            a = dve.tensor_scalar(acc[:, l, :], y, share, None, ALU.mult)
                        else:
                            a = dve.scalar_tensor_tensor(acc[:, l, :], y, share, acc[:, l, :], ALU.mult, ALU.add)
                    a.then_inc(s.acc, 1)

                for e in range(E):
                    for c in range(FC):
                        product(e, c)
                    if e:
                        add(e - 1)
                    if ahead and e in route:
                        route[e](t + 1, 1 - parity)
                add(E - 1)
                dve.wait_ge(s.acc, nth_e(t, E - 1))
                xg = m.x[:, bass.ds(t * (LANES * D), LANES * D)]
                dve.scalar_tensor_tensor(xg, acc[:].rearrange("p l d -> p (l d)"), m.tg[:, 5:6], xg,
                                         ALU.mult, ALU.add).then_inc(s.x, 1)
                dve.wait_ge(s.x, t + 1)

            dve.wait_ge(s.iota, 1)
            for e in sorted(route):
                route[e](0, 0)
            turns(dve, turn)


@sublayer
def l2_attention(nc, ctx, m, io):
    H, HD = 16, 8
    HH = H // 2
    SK = SC + S
    ROWS = HH * (HD + 1)
    LANES = 4
    TURNS = B // LANES
    PLACES = 24
    s = semaphores(nc, ctx, "a2", "stats mv var_eps rstd xn xt_ps xt v_ps k_ps v km at_ps at y_ps x c0 c1 c2 c3 zeros ones")
    c_in = [s.c0, s.c1, s.c2, s.c3]
    unit = [semaphores(nc, ctx, f"a2u{u}", "s_ps s_max s_sub p") for u in range(4)]
    half = [semaphores(nc, ctx, f"a2h{k}", "ptc_ps ptc ptx_ps ptx ot_ps ot o_ps o_r o") for k in range(2)]

    def nth(turn, lane):
        return turn * LANES + lane + 1

    def head_of(i):
        u, qq, jj = i // 4, i // 2 % 2, i % 2
        return 4 * (2 * (u // 2) + qq) + 2 * (u % 2) + jj

    with ExitStack() as mem:
        def sb(name, shape, dt=F32):
            return mem.enter_context(nc.sbuf_tensor("a2_" + name, shape, dt))

        lane = [Names(
            stats=sb(f"stats{l}", [S, 6]), mv=sb(f"mv{l}", [S, 2]), var_eps=sb(f"var{l}", [S, 1]),
            rstd=sb(f"rstd{l}", [S, 1]), xn=sb(f"xn{l}", [S, D]), xct=sb(f"xct{l}", [D, SK]),
            c=sb(f"c{l}", [SC, D]), qt=sb(f"qt{l}", [D, S]), km=sb(f"km{l}", [D, 4, SK]),
            vc=sb(f"vc{l}", [SC, 2, HH * (ROWS + HD + 1)]), vx=sb(f"vx{l}", [S, 2, HH * (ROWS + HD + 1)]),
            ou=sb(f"ou{l}", [ROWS, S]),
            mx=sb(f"mx{l}", [S, H]), p=sb(f"p{l}", [S, H, SK]),
            ptc=sb(f"ptc{l}", [SC, HH, S]), ptx=sb(f"ptx{l}", [S, HH, S]),
            rs=sb(f"rs{l}", [S, H]), o=sb(f"o{l}", [S, D]), ot=sb(f"ot{l}", [D, S])) for l in range(LANES)]
        ps = [mem.enter_context(nc.psum_tensor(f"a2_ps{l}", [128, 2, 512], F32)) for l in range(LANES)]
        block = mem.enter_context(nc.Block())

        def own_columns(v):
            return v[:].rearrange("p k (a m) -> p k a m", m=ROWS + HD + 1)[:, :, :, 0:HD + 1]

        @block.sync
        def _(sp):
            load_context(sp, io, s, lane, c_in, TURNS)

        @block.tensor
        def _(pe):
            def inputs(t, l):
                pe.wait_ge(s.xn, nth(t, l))
                pe.wait_ge(c_in[l], 16 * t + 16)
                pe.transpose(ps[l][:, 0, 0:SC], lane[l].c[:], m.ident[0:SC, 0:SC])
                pe.transpose(ps[l][:, 0, SC:SK], lane[l].xn[:], m.ident[:]).then_inc(s.xt_ps, 1)

            def project(t, l):
                pe.wait_ge(s.xt, nth(t, l))
                pe.matmul(ps[l][:, 1, 0:SK], m.wkv2[:, 0:D], lane[l].xct[:], start=True, stop=True).then_inc(s.k_ps, 1)
                pe.matmul(ps[l][:, 0, 0:S], m.wq2[:], lane[l].xct[:, SC:SK], start=True, stop=True)
                pe.matmul(ps[l][0:SC, 0, D:2 * D], lane[l].xct[:, 0:SC], m.wkv2[:, D:2 * D], start=True, stop=True)
                pe.matmul(ps[l][:, 0, 2 * D:3 * D], lane[l].xct[:, SC:SK], m.wkv2[:, D:2 * D], start=True, stop=True
                          ).then_inc(s.v_ps, 1)

            def scores(u):
                def step(t, l):
                    if u == 0:
                        pe.wait_ge(s.km, nth(t, l))
                        pe.wait_ge(s.v, nth(t, l))
                    else:
                        pe.wait_ge(unit[u - 1].s_sub, nth(t, l))
                    for qq in range(2):
                        row = slice(32 * (2 * (u // 2) + qq), 32 * (2 * (u // 2) + qq) + 32)
                        q, k = lane[l].qt[row, :], lane[l].km[row, 2 * (u % 2):2 * (u % 2) + 2, :]
                        out = ps[l][:, qq, :].rearrange("p (j n) -> p j n", n=256)
                        pe.matmul(out[:, :, 0:SC], q, k[:, :, 0:SC], start=True, stop=True)
                        pe.matmul(out[:, :, SC:SK], m.identb[:], m.causal[:, SC:SK].unsqueeze(1).broadcast_to([S, 2, S]),
                                  start=True, stop=False)
                        mm = pe.matmul(out[:, :, SC:SK], q, k[:, :, SC:SK], start=False, stop=True)
                    mm.then_inc(unit[u].s_ps, 1)
                return step

            def transpose_pc(k):
                def step(t, l):
                    pe.wait_ge(unit[2 * k + 1].p, nth(t, l))
                    if k == 0:
                        pe.wait_ge(unit[3].s_sub, nth(t, l))
                    else:
                        pe.wait_ge(half[0].o, nth(t, l))
                    for i in range(HH):
                        mm = pe.transpose(ps[l][0:SC, i // 4, i % 4 * S:i % 4 * S + S], lane[l].p[:, HH * k + i, 0:SC],
                                          m.ident[:])
                    mm.then_inc(half[k].ptc_ps, 1)
                return step

            def transpose_px(k):
                def step(t, l):
                    pe.wait_ge(half[k].ptc, nth(t, l))
                    for i in range(HH):
                        mm = pe.transpose(ps[l][:, i // 4, i % 4 * S:i % 4 * S + S], lane[l].p[:, HH * k + i, SC:SK],
                                          m.ident[:])
                    mm.then_inc(half[k].ptx_ps, 1)
                return step

            def mix_v(k):
                def step(t, l):
                    pe.wait_ge(half[k].ptx, nth(t, l))
                    for i in range(HH):
                        a = head_of(HH * k + i) - HH * k
                        pe.matmul(ps[l][0:ROWS, 0, 0:S], lane[l].vc[:, k, ROWS * a:ROWS * a + ROWS], lane[l].ptc[:, i, :],
                                  start=(i == 0), stop=False)
                        mm = pe.matmul(ps[l][0:ROWS, 0, 0:S], lane[l].vx[:, k, ROWS * a:ROWS * a + ROWS],
                                       lane[l].ptx[:, i, :], start=False, stop=(i == HH - 1))
                    mm.then_inc(half[k].ot_ps, 1)
                return step

            def tokens_first(k):
                def step(t, l):
                    pe.wait_ge(half[k].ot, nth(t, l))
                    pe.transpose(ps[l][:, 1, 0:ROWS], lane[l].ou[:], m.ident[0:ROWS, 0:ROWS]).then_inc(half[k].o_ps, 1)
                return step

            def transpose_o(t, l):
                pe.wait_ge(half[1].o, nth(t, l))
                pe.transpose(ps[l][:, 0, 0:S], lane[l].o[:], m.ident[:]).then_inc(s.at_ps, 1)

            def project_o(t, l):
                pe.wait_ge(s.at, nth(t, l))
                pe.matmul(ps[l][:, 1, 0:D], lane[l].ot[:], m.wout2[:], start=True, stop=False)
                pe.matmul(ps[l][:, 1, 0:D], m.ones_row[:], m.rows[0:1, m.row_bout2, :], start=False, stop=True
                          ).then_inc(s.y_ps, 1)

            staggered(pe, TURNS, LANES, PLACES, {
                0: inputs, 1: project, 3: scores(0), 5: scores(1), 6: scores(2), 8: scores(3),
                10: transpose_pc(0), 11: transpose_px(0), 12: mix_v(0), 13: tokens_first(0),
                15: transpose_pc(1), 16: transpose_px(1), 17: mix_v(1), 18: tokens_first(1),
                20: transpose_o, 21: project_o})

        @block.scalar
        def _(act):
            if m.load_next:
                m.load_next(act)

            def inputs(t, l):
                act.wait_ge(s.xt_ps, nth(t, l))
                act.copy(lane[l].xct[:], ps[l][:, 0, 0:SK]).then_inc(s.xt, 1)

            def copy_qv(t, l):
                act.wait_ge(s.v_ps, nth(t, l))
                act.copy(lane[l].qt[:], ps[l][:, 0, 0:S])
                act.copy(own_columns(lane[l].vc)[:, :, :, 0:HD],
                         ps[l][0:SC, 0, D:2 * D].rearrange("p (k a e) -> p k a e", k=2, e=HD))
                act.copy(own_columns(lane[l].vx)[:, :, :, 0:HD],
                         ps[l][:, 0, 2 * D:3 * D].rearrange("p (k a e) -> p k a e", k=2, e=HD)).then_inc(s.v, 1)

            def exponential(u):
                def step(t, l):
                    part = lane[l].p[:, 4 * u:4 * u + 4, :]
                    act.wait_ge(unit[u].s_sub, nth(t, l))
                    act.activation(part, part, ACT.Exp, scale=HD ** -0.5).then_inc(unit[u].p, 1)
                return step

            def copy_pc(k):
                def step(t, l):
                    act.wait_ge(half[k].ptc_ps, nth(t, l))
                    act.copy(lane[l].ptc[:], ps[l][0:SC, :, :].rearrange("p b (j q) -> p (b j) q", q=S)
                             ).then_inc(half[k].ptc, 1)
                return step

            def copy_px(k):
                def step(t, l):
                    act.wait_ge(half[k].ptx_ps, nth(t, l))
                    act.copy(lane[l].ptx[:], ps[l][:, :, :].rearrange("p b (j q) -> p (b j) q", q=S)
                             ).then_inc(half[k].ptx, 1)
                return step

            def copy_o(k):
                def step(t, l):
                    act.wait_ge(half[k].ot_ps, nth(t, l))
                    act.copy(lane[l].ou[:], ps[l][0:ROWS, 0, 0:S]).then_inc(half[k].ot, 1)
                return step

            def copy_ot(t, l):
                act.wait_ge(s.at_ps, nth(t, l))
                act.copy(lane[l].ot[:], ps[l][:, 0, 0:S]).then_inc(s.at, 1)

            act.wait_ge(s.ones, 2 * LANES)
            staggered(act, TURNS, LANES, PLACES, {
                0: inputs, 1: copy_qv, 4: exponential(0), 6: exponential(1), 7: exponential(2), 9: exponential(3),
                10: copy_pc(0), 11: copy_px(0), 12: copy_o(0),
                15: copy_pc(1), 16: copy_px(1), 17: copy_o(1), 20: copy_ot})

        @block.gpsimd
        def _(pool):
            for l in range(LANES):
                pool.memset(lane[l].vc[:], 0.0).then_inc(s.zeros, 1)
                pool.memset(lane[l].vx[:], 0.0).then_inc(s.zeros, 1)
            pool.wait_ge(s.zeros, 2 * LANES)
            for l in range(LANES):
                pool.memset(own_columns(lane[l].vc)[:, :, :, HD:HD + 1], 1.0).then_inc(s.ones, 1)
                pool.memset(own_columns(lane[l].vx)[:, :, :, HD:HD + 1], 1.0).then_inc(s.ones, 1)

            def root_ln(t, l):
                pool.wait_ge(s.var_eps, nth(t, l))
                inverse_root(pool, lane[l].rstd[:], lane[l].var_eps[:], m, s.rstd)

            staggered(pool, TURNS, LANES, PLACES, {
                -3: root_ln})

        @block.vector
        def _(dve):

            def stats(t, l):
                token_stats(dve, m, s, lane[l], t * LANES + l, nth(t, l))

            def normalise(t, l):
                dve.wait_ge(s.rstd, nth(t, l))
                dve.tensor_scalar(lane[l].xn[:], m.x[:, bass.ds((t * LANES + l) * D, D)], lane[l].mv[:, 0:1],
                                  lane[l].rstd[:], ALU.subtract, ALU.mult).then_inc(s.xn, 1)

            def mask_k(t, l):
                dve.wait_ge(s.k_ps, nth(t, l))
                dve.tensor_tensor(lane[l].km[:], ps[l][:, 1, 0:SK].unsqueeze(1).broadcast_to([D, 4, SK]),
                                  bcast(m.headmask[:], SK), ALU.mult).then_inc(s.km, 1)

            def less_maximum(u):
                def step(t, l):
                    scores = ps[l][:, :, :].rearrange("p b (j n) -> p b j n", n=256)[:, :, :, 0:SK]
                    mx = lane[l].mx[:, 4 * u:4 * u + 4].rearrange("p (b j) -> p b j", j=2)
                    dve.wait_ge(unit[u].s_ps, nth(t, l))
                    dve.tensor_reduce(mx, scores, AX.X, ALU.max).then_inc(unit[u].s_max, 1)
                    dve.wait_ge(unit[u].s_max, nth(t, l))
                    dve.tensor_tensor(lane[l].p[:, 4 * u:4 * u + 4, :].rearrange("p (b j) n -> p b j n", j=2),
                                      scores, mx.unsqueeze(3).broadcast_to([S, 2, 2, SK]), ALU.subtract
                                      ).then_inc(unit[u].s_sub, 1)
                return step

            def divide(k):
                def step(t, l):
                    out = ps[l][:, 1, 0:ROWS].rearrange("p (h e) -> p h e", e=HD + 1)
                    rs = lane[l].rs[:, HH * k:HH * k + HH]
                    dve.wait_ge(half[k].o_ps, nth(t, l))
                    dve.reciprocal(rs, out[:, :, HD]).then_inc(half[k].o_r, 1)
                    dve.wait_ge(half[k].o_r, nth(t, l))
                    dve.tensor_tensor(lane[l].o[:, HH * HD * k:HH * HD * (k + 1)].rearrange("p (h e) -> p h e", e=HD),
                                      out[:, :, 0:HD], bcast(rs, HD), ALU.mult).then_inc(half[k].o, 1)
                return step

            def residual(t, l):
                xb = m.x[:, bass.ds((t * LANES + l) * D, D)]
                dve.wait_ge(s.y_ps, nth(t, l))
                dve.scalar_tensor_tensor(xb, ps[l][:, 1, 0:D], m.tg[:, 2:3], xb, ALU.mult, ALU.add).then_inc(s.x, 1)

            staggered(dve, TURNS, LANES, PLACES, {
                -3: stats, -1: normalise, 1: mask_k,
                3: less_maximum(0), 5: less_maximum(1), 6: less_maximum(2), 8: less_maximum(3),
                13: divide(0), 18: divide(1), 21: residual})


@sublayer
def l3_attention(nc, ctx, m, io):
    H, HD = 16, 8
    HH = H // 2
    ROWS = HH * (HD + 1)
    LANES = 4
    TURNS = B // LANES
    PLACES = 20
    s = semaphores(nc, ctx, "a3", "stats mv var_eps rstd xn xt_ps xt k_ps km qv_ps v at_ps at y_ps x "
                   "c0 c1 c2 c3 zeros ones")
    c_in = [s.c0, s.c1, s.c2, s.c3]
    half = [semaphores(nc, ctx, f"a3h{k}", "s_ps s_max s_sub p pt_ps pt ot_ps ot o_ps o_r o") for k in range(2)]

    def nth(turn, lane):
        return turn * LANES + lane + 1

    with ExitStack() as mem:
        def sb(name, shape, dt=F32):
            return mem.enter_context(nc.sbuf_tensor("a3_" + name, shape, dt))

        lane = [Names(
            stats=sb(f"stats{l}", [S, 6]), mv=sb(f"mv{l}", [S, 2]), var_eps=sb(f"var{l}", [S, 1]),
            rstd=sb(f"rstd{l}", [S, 1]), xn=sb(f"xn{l}", [S, D]), xt=sb(f"xt{l}", [D, S]), ct=sb(f"ct{l}", [D, SC]),
            c=sb(f"c{l}", [SC, D]), qt=sb(f"qt{l}", [D, S]), km=sb(f"km{l}", [D, 4, SC]), ou=sb(f"ou{l}", [ROWS, S]),
            v=sb(f"v{l}", [SC, 2, HH * (ROWS + HD + 1)]), mx=sb(f"mx{l}", [S, H]), p=sb(f"p{l}", [S, H, SC]),
            pt=sb(f"pt{l}", [SC, HH, S]), rs=sb(f"rs{l}", [S, H]), o=sb(f"o{l}", [S, D]), ot=sb(f"ot{l}", [D, S]))
            for l in range(LANES)]
        ps = [mem.enter_context(nc.psum_tensor(f"a3_ps{l}", [128, 2, 512], F32)) for l in range(LANES)]
        block = mem.enter_context(nc.Block())

        def own_columns(v):
            return v[:].rearrange("p k (a m) -> p k a m", m=ROWS + HD + 1)[:, :, :, 0:HD + 1]

        @block.sync
        def _(sp):
            load_context(sp, io, s, lane, c_in, TURNS)

        @block.tensor
        def _(pe):
            def inputs(t, l):
                pe.wait_ge(s.xn, nth(t, l))
                pe.wait_ge(c_in[l], 16 * t + 16)
                pe.transpose(ps[l][:, 0, 0:S], lane[l].xn[:], m.ident[:])
                pe.transpose(ps[l][:, 0, S:S + SC], lane[l].c[:], m.ident[0:SC, 0:SC]).then_inc(s.xt_ps, 1)

            def project(t, l):
                pe.wait_ge(s.xt, nth(t, l))
                pe.matmul(ps[l][:, 1, 0:SC], m.wk3[:], lane[l].ct[:], start=True, stop=True).then_inc(s.k_ps, 1)
                pe.matmul(ps[l][:, 0, 0:S], m.wq3[:], lane[l].xt[:], start=True, stop=True)
                pe.matmul(ps[l][0:SC, 0, S:S + D], lane[l].ct[:], m.wv3[:], start=True, stop=False)
                pe.matmul(ps[l][0:SC, 0, S:S + D], m.ones_row[:, 0:SC], m.rows[0:1, m.row_bv3, :],
                          start=False, stop=True).then_inc(s.qv_ps, 1)

            def scores(k):
                def step(t, l):
                    if k == 0:
                        pe.wait_ge(s.km, nth(t, l))
                        pe.wait_ge(s.v, nth(t, l))
                    else:
                        pe.wait_ge(half[0].s_sub, nth(t, l))
                    for qq in range(2):
                        pe.matmul(ps[l][:, qq, 0:4 * SC].rearrange("p (j n) -> p j n", n=SC), m.first_row[:],
                                  m.maskneg[:, bass.ds((t * LANES + l) * SC, SC)].unsqueeze(1).broadcast_to([D, 4, SC]),
                                  start=True, stop=False)
                    for qq in range(2):
                        row = slice(32 * (2 * k + qq), 32 * (2 * k + qq) + 32)
                        mm = pe.matmul(ps[l][:, qq, 0:4 * SC].rearrange("p (j n) -> p j n", n=SC), lane[l].qt[row, :],
                                       lane[l].km[row, :, :], start=False, stop=True)
                    mm.then_inc(half[k].s_ps, 1)
                return step

            def transpose_p(k):
                def step(t, l):
                    pe.wait_ge(half[k].p, nth(t, l))
                    if k == 0:
                        pe.wait_ge(half[1].s_sub, nth(t, l))
                    else:
                        pe.wait_ge(half[0].o, nth(t, l))
                    for i in range(HH):
                        mm = pe.transpose(ps[l][0:SC, i // 4, i % 4 * S:i % 4 * S + S], lane[l].p[:, HH * k + i, :],
                                          m.ident[:])
                    mm.then_inc(half[k].pt_ps, 1)
                return step

            def mix_v(k):
                def step(t, l):
                    pe.wait_ge(half[k].pt, nth(t, l))
                    for i in range(HH):
                        mm = pe.matmul(ps[l][0:ROWS, 0, 0:S], lane[l].v[:, k, ROWS * i:ROWS * i + ROWS],
                                       lane[l].pt[:, i, :], start=(i == 0), stop=(i == HH - 1))
                    mm.then_inc(half[k].ot_ps, 1)
                return step

            def tokens_first(k):
                def step(t, l):
                    pe.wait_ge(half[k].ot, nth(t, l))
                    pe.transpose(ps[l][:, 1, 0:ROWS], lane[l].ou[:], m.ident[0:ROWS, 0:ROWS]).then_inc(half[k].o_ps, 1)
                return step

            def transpose_o(t, l):
                pe.wait_ge(half[1].o, nth(t, l))
                pe.transpose(ps[l][:, 0, 0:S], lane[l].o[:], m.ident[:]).then_inc(s.at_ps, 1)

            def project_o(t, l):
                pe.wait_ge(s.at, nth(t, l))
                pe.matmul(ps[l][:, 1, 0:D], lane[l].ot[:], m.wo3[:], start=True, stop=False)
                pe.matmul(ps[l][:, 1, 0:D], m.ones_row[:], m.rows[0:1, m.row_bo3, :], start=False, stop=True
                          ).then_inc(s.y_ps, 1)

            staggered(pe, TURNS, LANES, PLACES, {
                0: inputs, 1: project, 4: scores(0), 7: scores(1),
                9: transpose_p(0), 10: mix_v(0), 11: tokens_first(0),
                13: transpose_p(1), 14: mix_v(1), 15: tokens_first(1), 16: transpose_o, 17: project_o})

        @block.scalar
        def _(act):
            if m.load_next:
                m.load_next(act)

            def inputs(t, l):
                act.wait_ge(s.xt_ps, nth(t, l))
                act.copy(lane[l].xt[:], ps[l][:, 0, 0:S])
                act.copy(lane[l].ct[:], ps[l][:, 0, S:S + SC]).then_inc(s.xt, 1)

            def copy_qv(t, l):
                act.wait_ge(s.qv_ps, nth(t, l))
                act.activation(lane[l].qt[:], ps[l][:, 0, 0:S], ACT.Identity, bias=m.bqk3[:, 0:1])
                act.copy(own_columns(lane[l].v)[:, :, :, 0:HD],
                         ps[l][0:SC, 0, S:S + D].rearrange("p (k a e) -> p k a e", k=2, e=HD)).then_inc(s.v, 1)

            def exponential(k):
                def step(t, l):
                    part = lane[l].p[:, HH * k:HH * k + HH, :]
                    act.wait_ge(half[k].s_sub, nth(t, l))
                    act.activation(part, part, ACT.Exp, scale=HD ** -0.5).then_inc(half[k].p, 1)
                return step

            def copy_pt(k):
                def step(t, l):
                    act.wait_ge(half[k].pt_ps, nth(t, l))
                    act.copy(lane[l].pt[:], ps[l][0:SC, :, :].rearrange("p b (j q) -> p (b j) q", q=S)
                             ).then_inc(half[k].pt, 1)
                return step

            def copy_o(k):
                def step(t, l):
                    act.wait_ge(half[k].ot_ps, nth(t, l))
                    act.copy(lane[l].ou[:], ps[l][0:ROWS, 0, 0:S]).then_inc(half[k].ot, 1)
                return step

            def copy_ot(t, l):
                act.wait_ge(s.at_ps, nth(t, l))
                act.copy(lane[l].ot[:], ps[l][:, 0, 0:S]).then_inc(s.at, 1)

            act.wait_ge(s.ones, LANES)
            staggered(act, TURNS, LANES, PLACES, {
                0: inputs, 1: copy_qv, 5: exponential(0), 8: exponential(1),
                9: copy_pt(0), 10: copy_o(0), 13: copy_pt(1), 14: copy_o(1), 16: copy_ot})

        @block.gpsimd
        def _(pool):
            for l in range(LANES):
                pool.memset(lane[l].v[:], 0.0).then_inc(s.zeros, 1)
            pool.wait_ge(s.zeros, LANES)
            for l in range(LANES):
                pool.memset(own_columns(lane[l].v)[:, :, :, HD:HD + 1], 1.0).then_inc(s.ones, 1)

            def root_ln(t, l):
                pool.wait_ge(s.var_eps, nth(t, l))
                inverse_root(pool, lane[l].rstd[:], lane[l].var_eps[:], m, s.rstd)

            staggered(pool, TURNS, LANES, PLACES, {
                -3: root_ln})

        @block.vector
        def _(dve):

            def stats(t, l):
                token_stats(dve, m, s, lane[l], t * LANES + l, nth(t, l))

            def normalise(t, l):
                dve.wait_ge(s.rstd, nth(t, l))
                dve.tensor_scalar(lane[l].xn[:], m.x[:, bass.ds((t * LANES + l) * D, D)], lane[l].mv[:, 0:1],
                                  lane[l].rstd[:], ALU.subtract, ALU.mult).then_inc(s.xn, 1)

            def mask_k(t, l):
                dve.wait_ge(s.k_ps, nth(t, l))
                dve.scalar_tensor_tensor(lane[l].km[:], ps[l][:, 1, 0:SC].unsqueeze(1).broadcast_to([D, 4, SC]),
                                         m.bqk3[:, 1:2], bcast(m.headmask[:], SC), ALU.add, ALU.mult).then_inc(s.km, 1)

            def less_maximum(k):
                def step(t, l):
                    scores = ps[l][:, :, 0:4 * SC].rearrange("p b (j n) -> p b j n", n=SC)
                    mx = lane[l].mx[:, HH * k:HH * k + HH].rearrange("p (b j) -> p b j", j=4)
                    dve.wait_ge(half[k].s_ps, nth(t, l))
                    dve.tensor_reduce(mx, scores, AX.X, ALU.max).then_inc(half[k].s_max, 1)
                    dve.wait_ge(half[k].s_max, nth(t, l))
                    dve.tensor_tensor(lane[l].p[:, HH * k:HH * k + HH, :].rearrange("p (b j) n -> p b j n", j=4), scores,
                                      mx.unsqueeze(3).broadcast_to([S, 2, 4, SC]), ALU.subtract
                                      ).then_inc(half[k].s_sub, 1)
                return step

            def divide(k):
                def step(t, l):
                    out = ps[l][:, 1, 0:ROWS].rearrange("p (h e) -> p h e", e=HD + 1)
                    rs = lane[l].rs[:, HH * k:HH * k + HH]
                    dve.wait_ge(half[k].o_ps, nth(t, l))
                    dve.reciprocal(rs, out[:, :, HD]).then_inc(half[k].o_r, 1)
                    dve.wait_ge(half[k].o_r, nth(t, l))
                    dve.tensor_tensor(lane[l].o[:, HH * HD * k:HH * HD * (k + 1)].rearrange("p (h e) -> p h e", e=HD),
                                      out[:, :, 0:HD], bcast(rs, HD), ALU.mult).then_inc(half[k].o, 1)
                return step

            def residual(t, l):
                xb = m.x[:, bass.ds((t * LANES + l) * D, D)]
                dve.wait_ge(s.y_ps, nth(t, l))
                dve.scalar_tensor_tensor(xb, ps[l][:, 1, 0:D], m.tg[:, 3:4], xb, ALU.mult, ALU.add).then_inc(s.x, 1)

            staggered(dve, TURNS, LANES, PLACES, {
                -3: stats, -1: normalise, 1: mask_k, 4: less_maximum(0), 7: less_maximum(1),
                11: divide(0), 15: divide(1), 17: residual})


@sublayer
def l2_ffn(nc, ctx, m, weights):
    F = 512
    FC = F // 128
    LANES = 4
    TURNS = B // LANES
    PLACES = 16
    ROUND = 1.5 * 2 ** 23
    s = semaphores(nc, ctx, "f2", "lr wsum wsum_ps wmean wclip wscale wr1 wr2 wq wg stats mv var_eps rstd xn mx clip rcp qs dq xa "
                   "xb xq xt_ps xt gu_ps sg h hmx hclip hrcp hqs hdq ha hb hq ht_ps ht y_ps x")

    def nth(turn, lane):
        return turn * LANES + lane + 1

    with ExitStack() as mem:
        def sb(name, shape, dt=F32):
            return mem.enter_context(nc.sbuf_tensor("f2_" + name, shape, dt))

        w = [weights.gate[:], weights.up[:], weights.down[:].rearrange("p c n -> p (c n)")]
        wr, wl = sb("wr", [128, 3, F]), sb("wl", [128, 3, F])
        wq = sb("wq", [128, 3, F], BF16)
        wsum, wmean, wscale = sb("wsum", [128, 3]), sb("wmean", [128, 3]), sb("wscale", [128, 3])
        wdg = sb("wdg", [128, 1])
        ones = sb("ones", [128, 128])
        less_round = sb("less_round", [128, 1])
        lane = [Names(
            stats=sb(f"stats{l}", [S, 6]), mv=sb(f"mv{l}", [S, 2]), var_eps=sb(f"var{l}", [S, 1]),
            rstd=sb(f"rstd{l}", [S, 1]), xn=sb(f"xn{l}", [S, D]), mx=sb(f"mx{l}", [S, 2]), clip=sb(f"clip{l}", [S, 2]),
            rcp=sb(f"rcp{l}", [S, 2]), qs=sb(f"qs{l}", [S, 2]), dq=sb(f"dq{l}", [S, 3]), xa=sb(f"xa{l}", [S, D]),
            xq=sb(f"xq{l}", [S, D], BF16), xt=sb(f"xt{l}", [D, S], BF16), sg=sb(f"sg{l}", [S, F]), h=sb(f"h{l}", [S, F]),
            hq=sb(f"hq{l}", [S, F], BF16), ht=sb(f"ht{l}", [128, FC, S], BF16)) for l in range(LANES)]
        ps = [mem.enter_context(nc.psum_tensor(f"f2_ps{l}", [128, 2, 512], F32)) for l in range(LANES)]
        ps_b = [p[:, 0, :].bitcast(BF16) for p in ps]
        block = mem.enter_context(nc.Block())

        if 4 not in PHASES:
            @block.sync
            def _(sp):
                weights.load(sp)

        @block.tensor
        def _(pe):
            pe.wait_ge(s.wsum, 4)
            pe.matmul(ps[0][:, 0, 0:3], ones[:], wsum[:], start=True, stop=True).then_inc(s.wsum_ps, 1)
            pe.wait_ge(s.wq, 1)

            def transpose_x(t, l):
                pe.wait_ge(s.xq, nth(t, l))
                pe.transpose(ps_b[l][:, 0:S], lane[l].xq[:], m.identb[:]).then_inc(s.xt_ps, 1)

            def gate_up(t, l):
                pe.wait_ge(s.xt, nth(t, l))
                for n in range(2):
                    mm = pe.matmul(ps[l][:, n, :], lane[l].xt[:], wq[:, n, :], start=True, stop=True)
                mm.then_inc(s.gu_ps, 1)

            def transpose_h(t, l):
                pe.wait_ge(s.hq, nth(t, l))
                for c in range(FC):
                    mm = pe.transpose(ps_b[l][:, S * c:S * c + S], lane[l].hq[:, 128 * c:128 * c + 128], m.identb[:])
                mm.then_inc(s.ht_ps, 1)

            def down(t, l):
                pe.wait_ge(s.ht, nth(t, l))
                for c in range(FC):
                    mm = pe.matmul(ps[l][:, 1, 0:D], lane[l].ht[:, c, :], wq[:, 2, D * c:D * c + D],
                                   start=(c == 0), stop=(c == FC - 1))
                mm.then_inc(s.y_ps, 1)

            staggered(pe, TURNS, LANES, PLACES, {0: transpose_x, 1: gate_up, 9: transpose_h, 10: down})

        @block.scalar
        def _(act):
            def integers_x(t, l):
                act.wait_ge(s.xb, nth(t, l))
                act.activation(lane[l].xq[:], lane[l].xn[:], ACT.Identity, bias=less_round[:]).then_inc(s.xq, 1)

            def integers_h(t, l):
                act.wait_ge(s.hb, nth(t, l))
                act.activation(lane[l].hq[:], lane[l].h[:], ACT.Identity, bias=less_round[:]).then_inc(s.hq, 1)

            def copy_xt(t, l):
                act.wait_ge(s.xt_ps, nth(t, l))
                act.copy(lane[l].xt[:], ps_b[l][:, 0:S]).then_inc(s.xt, 1)

            def silu(t, l):
                act.wait_ge(s.dq, nth(t, l))
                act.wait_ge(s.gu_ps, nth(t, l))
                act.activation(lane[l].sg[:], ps[l][:, 0, :], ACT.Silu, scale=lane[l].dq[:, 0:1]).then_inc(s.sg, 1)

            def copy_ht(t, l):
                act.wait_ge(s.ht_ps, nth(t, l))
                act.copy(lane[l].ht[:], ps_b[l][:, 0:FC * S].rearrange("p (c n) -> p c n", c=FC)).then_inc(s.ht, 1)

            act.wait_ge(s.lr, 1)
            staggered(act, TURNS, LANES, PLACES, {
                -1: integers_x, 0: copy_xt, 1: silu, 8: integers_h, 9: copy_ht})

        @block.gpsimd
        def _(pool):
            pool.memset(less_round[:], -ROUND).then_inc(s.lr, 1)
            pool.memset(ones[:], 1.0).then_inc(s.wsum, 1)

            def root_ln(t, l):
                pool.wait_ge(s.var_eps, nth(t, l))
                inverse_root(pool, lane[l].rstd[:], lane[l].var_eps[:], m, s.rstd)

            staggered(pool, TURNS, LANES, PLACES, {-7: root_ln})

        @block.vector
        def _(dve):
            dve.wait_ge(weights.first, 16)
            dve.wait_ge(weights.rest, 32)
            for n in range(3):
                dve.tensor_reduce(wsum[:, n:n + 1], w[n], AX.X, ALU.add, apply_absolute_value=True).then_inc(s.wsum, 1)
            dve.wait_ge(s.wsum_ps, 1)
            dve.tensor_scalar(wmean[:], ps[0][:, 0, 0:3], 1.0 / (D * F), 1e-5, ALU.mult, ALU.max).then_inc(s.wmean, 1)
            dve.wait_ge(s.wmean, 1)
            dve.reciprocal(wscale[:], wmean[:]).then_inc(s.wscale, 1)
            dve.tensor_tensor(wdg[:], wmean[:, 2:3], m.tg[:, 6:7], ALU.mult).then_inc(s.wg, 1)
            dve.wait_ge(s.wscale, 1)
            for n in range(3):
                dve.tensor_scalar(wr[:, n, :], w[n], wscale[:, n:n + 1], ROUND, ALU.mult, ALU.add).then_inc(s.wr1, 1)
            dve.wait_ge(s.wr1, 3)
            dve.tensor_scalar(wl[:], wr[:], ROUND, -1.0, ALU.subtract, ALU.max).then_inc(s.wr2, 1)
            dve.wait_ge(s.wr2, 1)
            dve.tensor_scalar(wq[:], wl[:], 1.0, None, ALU.min).then_inc(s.wq, 1)
            dve.wait_ge(s.wg, 1)

            def stats(t, l):
                token_stats(dve, m, s, lane[l], t * LANES + l, nth(t, l))

            def normalise(t, l):
                dve.wait_ge(s.rstd, nth(t, l))
                dve.tensor_scalar(lane[l].xn[:], m.x[:, bass.ds((t * LANES + l) * D, D)], lane[l].mv[:, 0:1],
                                  lane[l].rstd[:], ALU.subtract, ALU.mult).then_inc(s.xn, 1)

            def maximum(t, l):
                dve.wait_ge(s.xn, nth(t, l))
                dve.tensor_reduce(lane[l].mx[:, 0:1], lane[l].xn[:], AX.X, ALU.max, apply_absolute_value=True
                                  ).then_inc(s.mx, 1)

            def clip(t, l):
                dve.wait_ge(s.mx, nth(t, l))
                dve.tensor_scalar(lane[l].clip[:, 0:1], lane[l].mx[:, 0:1], 1e-5, None, ALU.max).then_inc(s.clip, 1)

            def scale(t, l):
                dve.wait_ge(s.clip, nth(t, l))
                dve.reciprocal(lane[l].rcp[:, 0:1], lane[l].clip[:, 0:1]).then_inc(s.rcp, 1)
                dve.tensor_scalar(lane[l].dq[:, 0:2], wmean[:, 0:2], lane[l].clip[:, 0:1], 1.0 / 127, ALU.mult, ALU.mult
                                  ).then_inc(s.dq, 1)
                dve.wait_ge(s.rcp, nth(t, l))
                dve.tensor_scalar(lane[l].qs[:, 0:1], lane[l].rcp[:, 0:1], 127.0, None, ALU.mult).then_inc(s.qs, 1)

            def round_x(t, l):
                dve.wait_ge(s.qs, nth(t, l))
                dve.tensor_scalar(lane[l].xa[:], lane[l].xn[:], lane[l].qs[:, 0:1], ROUND, ALU.mult, ALU.add
                                  ).then_inc(s.xa, 1)

            def clip_x(t, l):
                dve.wait_ge(s.xa, nth(t, l))
                dve.tensor_scalar(lane[l].xn[:], lane[l].xa[:], ROUND - 128, ROUND + 127, ALU.max, ALU.min
                                  ).then_inc(s.xb, 1)

            def hidden(t, l):
                dve.wait_ge(s.dq, nth(t, l))
                dve.wait_ge(s.sg, nth(t, l))
                dve.scalar_tensor_tensor(lane[l].h[:], ps[l][:, 1, :], lane[l].dq[:, 1:2], lane[l].sg[:],
                                         ALU.mult, ALU.mult).then_inc(s.h, 1)

            def maximum_h(t, l):
                dve.wait_ge(s.h, nth(t, l))
                dve.tensor_reduce(lane[l].mx[:, 1:2], lane[l].h[:], AX.X, ALU.max, apply_absolute_value=True
                                  ).then_inc(s.hmx, 1)

            def clip_h(t, l):
                dve.wait_ge(s.hmx, nth(t, l))
                dve.tensor_scalar(lane[l].clip[:, 1:2], lane[l].mx[:, 1:2], 1e-5, None, ALU.max).then_inc(s.hclip, 1)

            def scale_h(t, l):
                dve.wait_ge(s.hclip, nth(t, l))
                dve.reciprocal(lane[l].rcp[:, 1:2], lane[l].clip[:, 1:2]).then_inc(s.hrcp, 1)
                dve.tensor_scalar(lane[l].dq[:, 2:3], wdg[:], lane[l].clip[:, 1:2], 1.0 / 127, ALU.mult, ALU.mult
                                  ).then_inc(s.hdq, 1)
                dve.wait_ge(s.hrcp, nth(t, l))
                dve.tensor_scalar(lane[l].qs[:, 1:2], lane[l].rcp[:, 1:2], 127.0, None, ALU.mult).then_inc(s.hqs, 1)

            def round_h(t, l):
                dve.wait_ge(s.hqs, nth(t, l))
                dve.tensor_scalar(lane[l].sg[:], lane[l].h[:], lane[l].qs[:, 1:2], ROUND, ALU.mult, ALU.add
                                  ).then_inc(s.ha, 1)

            def clip_q(t, l):
                dve.wait_ge(s.ha, nth(t, l))
                dve.tensor_scalar(lane[l].h[:], lane[l].sg[:], ROUND - 128, ROUND + 127, ALU.max, ALU.min
                                  ).then_inc(s.hb, 1)

            def residual(t, l):
                xb = m.x[:, bass.ds((t * LANES + l) * D, D)]
                dve.wait_ge(s.hdq, nth(t, l))
                dve.wait_ge(s.y_ps, nth(t, l))
                dve.scalar_tensor_tensor(xb, ps[l][:, 1, 0:D], lane[l].dq[:, 2:3], xb, ALU.mult, ALU.add).then_inc(s.x, 1)

            staggered(dve, TURNS, LANES, PLACES, {
                -7: stats, -6: normalise, -5: maximum, -4: clip, -3: scale, -2: round_x, -1: clip_x,
                3: hidden, 4: maximum_h, 5: clip_h, 6: scale_h, 7: round_h, 8: clip_q, 12: residual})


@sublayer
def switch_ffn(nc, ctx, m, weights):
    E, F = 8, 512
    FC = F // 128
    CAP = B * S // E
    TILES = CAP // 128
    GROUP = 4
    NORM = 4
    s = semaphores(nc, ctx, "f3", "zero init stats mv var_eps rstd sub0 xn xt_ps xt r_ps r mx sub exp den gate eq key kmax idx "
                   "oh cnt_ps pre excl pos sel place base over tok alt1 alt dest gidx wt wtg iota tri one in0 in1 in2 in3 in4 "
                   "in5 in6 in7 xet_ps xet up_ps h y_ps y out sc0 sc1 sc2 sc3 g0 g1 g2 g3 x")
    expert_in = [s.in0, s.in1, s.in2, s.in3, s.in4, s.in5, s.in6, s.in7]
    scattered = [s.sc0, s.sc1, s.sc2, s.sc3]
    gathered = [s.g0, s.g1, s.g2, s.g3]
    rows_in = nc.dram_tensor("f3_rows_in", (E * CAP + B * S, D), F32, kind="Internal").ap()
    rows_out = nc.dram_tensor("f3_rows_out", (E * CAP, D), F32, kind="Internal").ap()

    with ExitStack() as mem:
        def sb(name, shape, dt=F32):
            return mem.enter_context(nc.sbuf_tensor("f3_" + name, shape, dt))

        wr, w1, w3, b1, b2 = weights.wr, weights.w1, weights.w3, weights.b1, weights.b2
        zeros = sb("zeros", [128, 8 * D])
        tri = sb("tri", [S, S])
        ones = sb("ones", [S, S])
        experts = sb("experts", [S, E])
        token = sb("token", [S, B])
        stats, mv = sb("stats", [S, B, 6]), sb("mv", [S, B, 2])
        var_eps, rstd = sb("var", [S, B]), sb("rstd", [S, B])
        xn = sb("xn", [S, B, D])
        xt = [sb(f"xt{k}", [D, GROUP, S]) for k in range(2)]
        r, sub, eq, key, oh = (sb(n, [S, B, E]) for n in ("r", "sub", "eq", "key", "oh"))
        cum = [sb(f"cum{k}", [S, B, E]) for k in range(2)]
        pos, sel = sb("pos", [S, B, E]), sb("sel", [S, B, E])
        mx, den, gate, kmax, idx, place, base, over, alt1, alt, dest_f, gidx_f, keep, wt, wtg = (
            sb(n, [S, B]) for n in ("mx", "den", "gate", "kmax", "idx", "place", "base", "over", "alt1", "alt", "destf",
                                    "gidxf", "keep", "wt", "wtg"))
        dest, gidx = sb("dest", [S, B], U32), sb("gidx", [S, B], U32)
        rows = sb("rows", [128, E, TILES * D])
        xet = [sb(f"xet{k}", [D, CAP]) for k in range(2)]
        hid = [sb(f"hid{k}", [128, CAP]) for k in range(2 * FC)]
        tp = mem.enter_context(nc.psum_tensor("f3_tp", [128, 2, 512], F32))
        up = mem.enter_context(nc.psum_tensor("f3_up", [128, 4, 512], F32))
        yps = mem.enter_context(nc.psum_tensor("f3_y", [128, 2, 512], F32))
        scores_ps = yps[:, 0, 0:B * E].rearrange("p (b e) -> p b e", e=E)
        before_ps = yps[:, 1, 0:B * E].rearrange("p (b e) -> p b e", e=E)
        count_ps = yps[:, 1, 256:256 + B * E].rearrange("p (b e) -> p b e", e=E)
        block = mem.enter_context(nc.Block())

        @block.sync
        def _(sp):
            if 6 not in PHASES:
                weights.load(sp)
            sp.wait_ge(s.zero, 1)
            empty = rows_in[0:E * CAP, :].rearrange("(p r) d -> p (r d)", p=128)
            for i in range(4):
                sp.dma_start(empty[:, 8 * D * i:8 * D * (i + 1)], zeros[:]).then_inc(s.init, 16)
            for l in range(4):
                sp.wait_ge(scattered[l], 16 * (B // 4))
            for e in range(E):
                sp.dma_start(rows[:, e, :].rearrange("p (k d) -> p k d", d=D),
                             rows_in[CAP * e:CAP * (e + 1), :].rearrange("(k p) d -> p k d", p=128)
                             ).then_inc(expert_in[e], 16)
            for e in range(E):
                sp.wait_ge(s.y, e + 1)
                sp.dma_start(rows_out[CAP * e:CAP * (e + 1), :].rearrange("(k p) d -> p k d", p=128),
                             rows[:, e, :].rearrange("p (k d) -> p k d", d=D)).then_inc(s.out, 16)
            sp.wait_ge(s.out, 16 * E)

        def router(pe, g):
            pe.wait_ge(s.xt, g + 1)
            for l in range(GROUP):
                b = GROUP * g + l
                mm = pe.matmul(scores_ps[:, b, :], xt[g % 2][:, l, :], wr[:], start=True, stop=True)
            mm.then_inc(s.r_ps, 1)

        def inputs(pe, e):
            pe.wait_ge(expert_in[e], 16)
            if e >= 2:
                pe.wait_ge(s.xet, e - 1)
            for k in range(TILES):
                mm = pe.transpose(tp[:, e % 2, 128 * k:128 * k + 128], rows[:, e, D * k:D * k + D], m.ident[:])
            mm.then_inc(s.xet_ps, 1)

        def first(pe, e):
            pe.wait_ge(s.xet, e + 1)
            for c in range(FC):
                if e:
                    pe.wait_ge(s.h, FC * (e - 1) + c + 1)
                pe.matmul(up[:, c, :], w1[:, e, c, :], xet[e % 2][:], start=True, stop=True).then_inc(s.up_ps, 1)

        def second(pe, e):
            pe.wait_ge(s.h, FC * (e + 1))
            if e >= 2:
                pe.wait_ge(s.y, e - 1)
            for k in range(TILES):
                for c in range(FC):
                    mm = pe.matmul(yps[:, e % 2, D * k:D * k + D], hid[e % 2 * FC + c][:, 128 * k:128 * k + 128],
                                   w3[:, e, c, :], start=(c == 0), stop=(c == FC - 1))
            mm.then_inc(s.y_ps, 1)

        @block.tensor
        def _(pe):
            for g in range(B // GROUP):
                pe.wait_ge(s.xn, GROUP * g // NORM + 1)
                if g >= 2:
                    pe.wait_ge(s.xt, g - 1)
                for l in range(GROUP):
                    mm = pe.transpose(tp[:, g % 2, S * l:S * l + S], xn[:, GROUP * g + l, :], m.ident[:])
                mm.then_inc(s.xt_ps, 1)
                if g == 0:
                    pe.wait_ge(weights.first, 16)
                else:
                    router(pe, g - 1)
            router(pe, B // GROUP - 1)
            pe.wait_ge(s.oh, 1)
            pe.wait_ge(s.tri, 1)
            flat_oh = oh[:].rearrange("p b e -> p (b e)")
            pe.matmul(yps[:, 1, 0:B * E], tri[:], flat_oh, start=True, stop=True)
            pe.matmul(yps[:, 1, 256:256 + B * E], ones[:], flat_oh, start=True, stop=True).then_inc(s.cnt_ps, 1)
            pe.wait_ge(weights.rest, 64)
            for e in range(E + 1):
                if e == 0:
                    inputs(pe, 0)
                if e + 1 < E:
                    inputs(pe, e + 1)
                if e < E:
                    first(pe, e)
                if e:
                    second(pe, e - 1)

        @block.scalar
        def _(act):
            for g in range(B // GROUP):
                act.wait_ge(s.xt_ps, g + 1)
                if g >= 2:
                    act.wait_ge(s.r_ps, g - 1)
                act.copy(xt[g % 2][:], tp[:, g % 2, :].rearrange("p (l n) -> p l n", n=S)).then_inc(s.xt, 1)
            act.wait_ge(s.sub, 1)
            act.activation(sub[:], sub[:], ACT.Exp).then_inc(s.exp, 1)
            act.wait_ge(weights.rest, 64)
            for e in range(E + 1):
                for i in ((0, 1) if e == 0 else (e + 1,)):
                    if i < E:
                        act.wait_ge(s.xet_ps, i + 1)
                        if i >= 2:
                            act.wait_ge(s.up_ps, FC * (i - 1))
                        act.copy(xet[i % 2][:], tp[:, i % 2, :]).then_inc(s.xet, 1)
                if e < E:
                    for c in range(FC):
                        act.wait_ge(s.up_ps, FC * e + c + 1)
                        if e >= 2:
                            act.wait_ge(s.y_ps, e - 1)
                        act.activation(hid[e % 2 * FC + c][:], up[:, c, :], ACT.Relu, bias=b1[:, e, c:c + 1]
                                       ).then_inc(s.h, 1)

        @block.gpsimd
        def _(pool):
            pool.memset(zeros[:], 0.0).then_inc(s.zero, 1)
            pool.iota(experts[:], [[1, E]], base=0, channel_multiplier=0, allow_small_or_imprecise_dtypes=True
                      ).then_inc(s.iota, 1)
            pool.iota(token[:], [[S, B]], base=0, channel_multiplier=1, allow_small_or_imprecise_dtypes=True
                      ).then_inc(s.iota, 1)
            pool.memset(ones[:], 1.0).then_inc(s.one, 1)
            pool.wait_ge(s.one, 1)
            pool.affine_select(tri[:], ones[:], [[1, S]], ALU.is_ge, 0.0, 0, -1).then_inc(s.tri, 1)
            for i in range(B // NORM):
                part = slice(NORM * i, NORM * i + NORM)
                pool.wait_ge(s.var_eps, i + 1)
                inverse_root(pool, rstd[:, part], var_eps[:, part], m, s.rstd)
            pool.wait_ge(s.init, 64)
            pool.wait_ge(s.dest, 1)
            for b in range(B):
                if b >= 4:
                    pool.wait_ge(scattered[b % 4], 16 * (b // 4))
                pool.indirect_dma_start(rows_in, bass.IndirectOffsetOnAxis(ap=dest[:, b:b + 1], axis=0), xn[:, b, :], None
                                        ).then_inc(scattered[b % 4], 16)
            pool.wait_ge(s.out, 16 * E)
            for l in range(4):
                pool.wait_ge(scattered[l], 16 * (B // 4))
            for b in range(B):
                if b >= 4:
                    pool.wait_ge(gathered[b % 4], 16 * (b // 4))
                pool.indirect_dma_start(xn[:, b, :], None, rows_out, bass.IndirectOffsetOnAxis(ap=gidx[:, b:b + 1], axis=0)
                                        ).then_inc(gathered[b % 4], 16)

        @block.vector
        def _(dve):
            xb = m.x[:].rearrange("p (b d) -> p b d", d=D)

            def over_deviation(i):
                part = slice(NORM * i, NORM * i + NORM)
                dve.wait_ge(s.sub0, i + 1)
                dve.wait_ge(s.rstd, i + 1)
                dve.tensor_tensor(xn[:, part, :], xn[:, part, :], bcast(rstd[:, part], D), ALU.mult).then_inc(s.xn, 1)

            for i in range(B // NORM):
                part = slice(NORM * i, NORM * i + NORM)
                for b in range(NORM * i, NORM * i + NORM):
                    dve.bn_stats(stats[:, b, :], xb[:, b, :]).then_inc(s.stats, 1)
                dve.wait_ge(s.stats, NORM * (i + 1))
                for b in range(NORM * i, NORM * i + NORM):
                    dve.bn_aggr(mv[:, b, :], stats[:, b, :]).then_inc(s.mv, 1)
                dve.wait_ge(s.mv, NORM * (i + 1))
                dve.tensor_scalar(var_eps[:, part], mv[:, part, 1], LN_EPS, None, ALU.add).then_inc(s.var_eps, 1)
                dve.tensor_tensor(xn[:, part, :], xb[:, part, :], bcast(mv[:, part, 0], D), ALU.subtract).then_inc(s.sub0, 1)
                if i:
                    over_deviation(i - 1)
            over_deviation(B // NORM - 1)
            dve.wait_ge(s.r_ps, B // GROUP)
            dve.tensor_copy(r[:], scores_ps).then_inc(s.r, 1)
            dve.wait_ge(s.r, 1)
            dve.tensor_reduce(mx[:], r[:], AX.X, ALU.max).then_inc(s.mx, 1)
            dve.wait_ge(s.mx, 1)
            dve.tensor_tensor(eq[:], r[:], bcast(mx[:], E), ALU.is_equal).then_inc(s.eq, 1)
            dve.tensor_tensor(sub[:], r[:], bcast(mx[:], E), ALU.subtract).then_inc(s.sub, 1)
            dve.wait_ge(s.iota, 2)
            dve.wait_ge(s.eq, 1)
            each = experts[:].unsqueeze(1).broadcast_to([S, B, E])
            dve.scalar_tensor_tensor(key[:], eq[:], float(E), each, ALU.mult, ALU.subtract).then_inc(s.key, 1)
            dve.wait_ge(s.key, 1)
            dve.tensor_reduce(kmax[:], key[:], AX.X, ALU.max).then_inc(s.kmax, 1)
            dve.wait_ge(s.kmax, 1)
            dve.tensor_scalar(idx[:], kmax[:], -1.0, float(E), ALU.mult, ALU.add).then_inc(s.idx, 1)
            dve.wait_ge(s.idx, 1)
            dve.tensor_tensor(oh[:], each, bcast(idx[:], E), ALU.is_equal).then_inc(s.oh, 1)
            dve.wait_ge(s.exp, 1)
            dve.tensor_reduce(den[:], sub[:], AX.X, ALU.add).then_inc(s.den, 1)
            dve.wait_ge(s.den, 1)
            dve.reciprocal(gate[:], den[:]).then_inc(s.gate, 1)
            dve.wait_ge(s.cnt_ps, 1)
            dve.tensor_copy(cum[0][:], count_ps).then_inc(s.pre, 1)
            step, k = 1, 0
            while step < B:
                dve.wait_ge(s.pre, 2 * k + 1)
                a, c = cum[k % 2], cum[1 - k % 2]
                dve.tensor_copy(c[:, 0:step, :], a[:, 0:step, :]).then_inc(s.pre, 1)
                dve.tensor_tensor(c[:, step:B, :], a[:, step:B, :], a[:, 0:B - step, :], ALU.add).then_inc(s.pre, 1)
                step, k = 2 * step, k + 1
            dve.wait_ge(s.pre, 2 * k + 1)
            total = cum[k % 2]
            dve.tensor_copy(pos[:, 0:1, :], before_ps[:, 0:1, :]).then_inc(s.pos, 1)
            dve.tensor_tensor(pos[:, 1:B, :], before_ps[:, 1:B, :], total[:, 0:B - 1, :], ALU.add).then_inc(s.pos, 1)
            dve.wait_ge(s.pos, 2)
            dve.wait_ge(s.oh, 1)
            dve.tensor_tensor(sel[:], pos[:], oh[:], ALU.mult).then_inc(s.sel, 1)
            dve.wait_ge(s.sel, 1)
            dve.tensor_reduce(place[:], sel[:], AX.X, ALU.add).then_inc(s.place, 1)
            dve.wait_ge(s.place, 1)
            dve.scalar_tensor_tensor(base[:], idx[:], float(CAP), place[:], ALU.mult, ALU.add).then_inc(s.base, 1)
            dve.tensor_scalar(over[:], place[:], float(CAP), None, ALU.is_gt).then_inc(s.over, 1)
            dve.tensor_scalar(keep[:], place[:], float(CAP), None, ALU.is_le).then_inc(s.tok, 1)
            dve.wait_ge(s.base, 1)
            dve.scalar_tensor_tensor(alt1[:], token[:], float(E * CAP + 1), base[:], ALU.add, ALU.subtract
                                     ).then_inc(s.alt1, 1)
            dve.tensor_scalar(gidx_f[:], base[:], -1.0, float(E * CAP - 1), ALU.add, ALU.min).then_inc(s.gidx, 1)
            dve.wait_ge(s.alt1, 1)
            dve.wait_ge(s.over, 1)
            dve.tensor_tensor(alt[:], alt1[:], over[:], ALU.mult).then_inc(s.alt, 1)
            dve.wait_ge(s.alt, 1)
            dve.scalar_tensor_tensor(dest_f[:], base[:], -1.0, alt[:], ALU.add, ALU.add).then_inc(s.alt, 1)
            dve.wait_ge(s.alt, 2)
            dve.wait_ge(s.gidx, 1)
            dve.tensor_copy(gidx[:], gidx_f[:])
            dve.tensor_copy(dest[:], dest_f[:]).then_inc(s.dest, 1)
            dve.wait_ge(s.gate, 1)
            dve.wait_ge(s.tok, 1)
            dve.tensor_tensor(wt[:], gate[:], keep[:], ALU.mult).then_inc(s.wt, 1)
            dve.wait_ge(s.wt, 1)
            dve.tensor_scalar(wtg[:], wt[:], m.tg[:, 7:8], None, ALU.mult).then_inc(s.wtg, 1)
            dve.wait_ge(weights.rest, 64)
            for e in range(E):
                dve.wait_ge(s.y_ps, e + 1)
                dve.tensor_tensor(rows[:, e, :].rearrange("p (k d) -> p k d", d=D),
                                  yps[:, e % 2, :].rearrange("p (k d) -> p k d", d=D),
                                  b2[:, D * e:D * e + D].unsqueeze(1).broadcast_to([128, TILES, D]), ALU.add
                                  ).then_inc(s.y, 1)
            dve.wait_ge(s.wtg, 1)
            for b in range(B):
                dve.wait_ge(gathered[b % 4], 16 * (b // 4 + 1))
                dve.scalar_tensor_tensor(xb[:, b, :], xn[:, b, :], wtg[:, b:b + 1], xb[:, b, :], ALU.mult, ALU.add
                                         ).then_inc(s.x, 1)
            dve.wait_ge(s.x, B)


HOST_LAYOUT = {
    "L0_ffn_Wg": (1, 0, 2), "L0_ffn_Wu": (1, 0, 2),
    "L1_ffn_Wg": (1, 0), "L1_ffn_W1": (2, 0, 1), "L1_ffn_W2": (2, 0, 1), "L1_ffn_W3": (2, 0, 1),
    "L2_ffn_w_gate": (1, 0), "L2_ffn_w_up": (1, 0), "L2_ffn_w_down": (1, 0),
    "L3_ffn_w1": (1, 0, 2), "L0_ffn_bd": (1, 0),
    "L0_ffn_bg": (2, 0, 1), "L0_ffn_bu": (2, 0, 1), "L3_ffn_b1": (2, 0, 1),
}
HOST_SHAPE = {"L0_ffn_bg": (16, 2, 128), "L0_ffn_bu": (16, 2, 128), "L3_ffn_b1": (8, 4, 128)}


def weights_of(nc, mem, name, tensors):
    tiles = {n: mem.enter_context(nc.sbuf_tensor(f"{name}_{n}", shape, F32)) for n, shape, _ in tensors}
    first = mem.enter_context(nc.semaphore(f"{name}_first_in"))
    rest = mem.enter_context(nc.semaphore(f"{name}_rest_in"))

    def load(eng):
        for n, _, src in tensors:
            dst = tiles[n]
            eng.dma_start(dst[:], src).then_inc(first if n == tensors[0][0] else rest, 16)

    return Names(load=load, first=first, rest=rest, **tiles)


def run_phases(nc, ctx, m, io):
    ios = Names(ctx=io["ctx_1024"])
    E, FF = 8, 512
    m.load_next = None
    if 1 in PHASES:
        f = {n: io["L0_ffn_" + n] for n in ("norm_g", "norm_b", "slot_g", "slot_b", "scale", "slot_embeds", "Wg", "Wu")}
        l0_ffn(nc, m, Names(
            Wd=io["L0_ffn_Wd"].rearrange("e (c p) n -> p e c n", p=128),
            bg=io["L0_ffn_bg"], bu=io["L0_ffn_bu"], bd=io["L0_ffn_bd"], **f))
    with ExitStack() as mem:
        if 3 in PHASES:
            f1 = weights_of(nc, mem, "f1w", (
                ("wr", [D, E], io["L1_ffn_Wg"]),
                ("w1", [D, E, 2, 128], io["L1_ffn_W1"].rearrange("d e (c p) -> d e c p", p=128)),
                ("w2", [D, E, 2, 128], io["L1_ffn_W2"].rearrange("d e (c p) -> d e c p", p=128)),
                ("w3", [128, E, 2, D], io["L1_ffn_W3"].rearrange("(c p) e n -> p e c n", p=128))))
            m.load_next = f1.load
        if 2 in PHASES:
            l1_attention(nc, m, ios)
        if 3 in PHASES:
            top2_ffn(nc, m, f1)
        m.load_next = None
    with ExitStack() as mem:
        if 5 in PHASES:
            f2 = weights_of(nc, mem, "f2w", (
                ("gate", [128, FF], io["L2_ffn_w_gate"]), ("up", [128, FF], io["L2_ffn_w_up"]),
                ("down", [128, FF // 128, D], io["L2_ffn_w_down"].rearrange("(c p) n -> p c n", p=128))))
            m.load_next = f2.load
        if 4 in PHASES:
            l2_attention(nc, m, ios)
        if 5 in PHASES:
            l2_ffn(nc, m, f2)
        m.load_next = None
    with ExitStack() as mem:
        if 7 in PHASES:
            f3 = weights_of(nc, mem, "f3w", (
                ("wr", [D, E], io["L3_ffn_router_w"]),
                ("w1", [D, E, 4, 128], io["L3_ffn_w1"].rearrange("d e (c p) -> d e c p", p=128)),
                ("w3", [128, E, 4, D], io["L3_ffn_w2"].rearrange("e (c p) n -> p e c n", p=128)),
                ("b1", [128, E, 4], io["L3_ffn_b1"]),
                ("b2", [128, E * D], io["L3_ffn_b2"].rearrange("e d -> (e d)").partition_broadcast(128))))
            m.load_next = f3.load
        if 6 in PHASES:
            l3_attention(nc, m, ios)
        if 7 in PHASES:
            switch_ffn(nc, m, f3)


def bass_flamingo_gated_stack(nc, io, out):
    with ExitStack() as ctx:
        def sb(name, shape, dt=F32):
            return ctx.enter_context(nc.sbuf_tensor(name, shape, dt))

        m = Shared()
        m.x = sb("x_res", [S, B * D])
        m.ident = sb("ident", [128, 128])
        m.identb = sb("identb", [128, 128], BF16)
        m.causal = sb("causal", [S, SC + S], BF16)
        m.first_row = sb("first_row", [128, 128], BF16)
        m.minus_half = sb("minus_half", [128, 16])
        m.ones_row = sb("ones_row", [1, 128])
        m.wait_pad = sb("wait_pad", [128, 1])
        m.zero = sb("zero", [128, 1])
        m.g_raw = sb("g_raw", [128, 8])
        m.tg = sb("tg", [128, 8])
        m.mask = sb("mask", [128, B * SC], U8)
        m.maskneg = sb("maskneg", [128, B * SC], BF16)
        ROWS = "bo0 bv1 bout2 bv3 bo3".split()
        m.rows = sb("rows", [1, len(ROWS), D])
        m.row_bo0, m.row_bv1, m.row_bout2, m.row_bv3, m.row_bo3 = range(5)
        m.gq = sb("gq", [128, 1])
        m.gk = sb("gk", [128, 1])
        m.gqk = sb("gqk", [128, 1])
        m.bqk1 = sb("bqk1", [128, 2])
        m.bqk3 = sb("bqk3", [128, 2])
        m.headmask = sb("headmask", [128, 4])
        m.wq1, m.wk1, m.wv1 = (sb(n, [D, D]) for n in ("wq1", "wk1", "wv1"))
        m.wq2, m.wkv2, m.wout2 = sb("wq2", [D, D]), sb("wkv2", [D, 2 * D]), sb("wout2", [D, D])
        m.wq3, m.wk3, m.wv3, m.wo3 = (sb(n, [D, D]) for n in ("wq3", "wk3", "wv3", "wo3"))

        m.s_small = ctx.enter_context(nc.semaphore("small_in"))
        m.s_x = ctx.enter_context(nc.semaphore("x_in"))
        m.s_later = ctx.enter_context(nc.semaphore("later_in"))
        m.s_x_rest = ctx.enter_context(nc.semaphore("x_rest_in"))
        m.s_wk0, m.s_wv0, m.s_wq0, m.s_wo0 = (ctx.enter_context(nc.semaphore(n + "_in")) for n in ("wk0", "wv0", "wq0", "wo0"))
        m.s_out = ctx.enter_context(nc.semaphore("out_done"))
        m.s_ready = ctx.enter_context(nc.semaphore("ready"))
        setup = semaphores(nc, [], "setup", "zero ident identb causal misc tanh vec hm")
        small = [(m.g_raw[:, 0:4], io["g_xattn"].partition_broadcast(128)),
                 (m.g_raw[:, 4:8], io["g_ffn"].partition_broadcast(128)),
                 (m.rows[0:1, 0, :], io["L0_xattn_bo"].unsqueeze(0))]
        later = []
        for i, n in enumerate(("L1_xattn_bv", "L2_xattn_bout", "L3_xattn_bv", "L3_xattn_bo")):
            later.append((m.rows[0:1, i + 1, :], io[n].unsqueeze(0)))
        later += [(m.mask[:], io["mask_BxS2_bk0"].rearrange("b s -> (b s)").partition_broadcast(128)),
                  (m.bqk1[:, 0:1], io["L1_xattn_bq"].unsqueeze(1)), (m.bqk1[:, 1:2], io["L1_xattn_bk"].unsqueeze(1)),
                  (m.bqk3[:, 0:1], io["L3_xattn_bq"].unsqueeze(1)), (m.bqk3[:, 1:2], io["L3_xattn_bk"].unsqueeze(1)),
                  (m.wq1[:], io["L1_xattn_Wq"]), (m.wk1[:], io["L1_xattn_Wk"]), (m.wv1[:], io["L1_xattn_Wv"]),
                  (m.wq2[:], io["L2_xattn_Wq"]), (m.wkv2[:], io["L2_xattn_Wkv"]), (m.wout2[:], io["L2_xattn_Wout"]),
                  (m.wq3[:], io["L3_xattn_Wq"]), (m.wk3[:], io["L3_xattn_Wk"]), (m.wv3[:], io["L3_xattn_Wv"]),
                  (m.wo3[:], io["L3_xattn_Wo"])]
        for half in range(2):
            row = slice(64 * half, 64 * half + 64)
            small += [(m.gq[row], io["L0_xattn_gq"].unsqueeze(1)), (m.gk[row], io["L0_xattn_gk"].unsqueeze(1))]

        with ExitStack() as mem0:
            if 0 in PHASES:
                m.wq0, m.wk0, m.wv0 = (mem0.enter_context(nc.sbuf_tensor(n, [D, 1024], F32)) for n in ("wq0", "wk0", "wv0"))
                m.wo0 = mem0.enter_context(nc.sbuf_tensor("wo0", [128, 8, D], F32))
            with nc.Block() as block:
                @block.sync
                def _(sp):
                    xv, xs = io["x"].rearrange("b s d -> s b d"), m.x[:].rearrange("p (b d) -> p b d", d=D)
                    sp.dma_start(xs[:, 0:4, :], xv[:, 0:4, :]).then_inc(m.s_x, 16)
                    if 0 in PHASES:
                        sp.dma_start(m.wk0[:], io["L0_xattn_Wk"].rearrange("d h e -> d (h e)")).then_inc(m.s_wk0, 16)
                        sp.dma_start(m.wv0[:], io["L0_xattn_Wv"].rearrange("d h e -> d (h e)")).then_inc(m.s_wv0, 16)
                        sp.dma_start(m.wq0[:], io["L0_xattn_Wq"].rearrange("d h e -> d (h e)")).then_inc(m.s_wq0, 16)
                    sp.dma_start(xs[:, 4:B, :], xv[:, 4:B, :]).then_inc(m.s_x_rest, 16)
                    if 0 in PHASES:
                        sp.dma_start(m.wo0[:], io["L0_xattn_Wo"].rearrange("(j a) e n -> (a e) j n", a=2)).then_inc(m.s_wo0, 16)
                    for dst, src in later:
                        sp.dma_start(dst, src).then_inc(m.s_later, 16)

                @block.gpsimd
                def _(pool):
                    pool.memset(m.ident[:], 0.0).then_inc(setup.zero, 1)
                    pool.memset(m.causal[:], 0.0).then_inc(setup.zero, 1)
                    pool.memset(m.minus_half[:], -0.5)
                    pool.memset(m.ones_row[:], 1.0)
                    pool.memset(m.first_row[:], 0.0).then_inc(setup.zero, 1)
                    pool.memset(m.headmask[:], 1.0).then_inc(setup.zero, 1)
                    pool.wait_ge(setup.zero, 4)
                    pool.memset(m.first_row[0:1, :], 1.0).then_inc(setup.misc, 1)
                    pool.wait_ge(setup.misc, 1)
                    pool.affine_select(m.ident[:], m.ident[:], [[-1, 128]], ALU.not_equal, 1.0, 0, 1).then_inc(setup.ident, 1)
                    pool.affine_select(m.causal[:, SC:SC + S], m.causal[:, SC:SC + S], [[-1, S]], ALU.is_ge, NEG, 0, 1).then_inc(setup.causal, 1)
                    for quad in range(4):
                        if quad:
                            pool.wait_ge(setup.hm, 2 * quad)
                        part = m.headmask[32 * quad:32 * quad + 32, :]
                        pool.affine_select(part, part, [[-8, 4]], ALU.is_ge, 0.0, 0, 1).then_inc(setup.hm, 1)
                        pool.wait_ge(setup.hm, 2 * quad + 1)
                        pool.affine_select(part, part, [[8, 4]], ALU.is_ge, 0.0, 7, -1).then_inc(setup.hm, 1)
                    pool.wait_ge(setup.hm, 8)
                    pool.wait_ge(setup.ident, 1)
                    pool.tensor_copy(m.identb[:], m.ident[:]).then_inc(setup.identb, 1)

                @block.scalar
                def _(act):
                    for dst, src in small:
                        act.dma_start(dst, src).then_inc(m.s_small, 16)
                    act.wait_ge(m.s_small, 16 * len(small))
                    act.activation(m.tg[:], m.g_raw[:], ACT.Tanh).then_inc(setup.tanh, 1)

                @block.vector
                def _(dve):
                    dve.wait_ge(m.s_small, 16 * len(small))
                    dve.tensor_tensor(m.gqk[:], m.gq[:], m.gk[:], ALU.mult).then_inc(setup.vec, 1)
                    dve.memset(m.zero[:], 0.0).then_inc(m.s_ready, 1)
                    dve.wait_ge(m.s_x, 16)
                    if 0 not in PHASES:
                        dve.wait_ge(m.s_x_rest, 16)
            ios = Names(ctx=io["ctx_1024"])
            if 0 in PHASES:
                l0_attention(nc, m, ios)
        with nc.Block() as block:
            @block.vector
            def _(dve):
                dve.wait_ge(m.s_later, 16 * len(later))
                dve.tensor_scalar(m.maskneg[:], m.mask[:], NEG, None, ALU.mult).then_inc(setup.vec, 1)

        run_phases(nc, ctx, m, io)

        with nc.Block() as block:
            @block.sync
            def _(sp):
                sp.dma_start(out.rearrange("b s d -> s b d"), m.x[:].rearrange("p (b d) -> p b d", d=D)
                             ).then_inc(m.s_out, 16)
                sp.wait_ge(m.s_out, 16)


def kernel(**inputs):
    import numpy as np
    import concourse.bacc as bacc
    from concourse.bass_utils import run_bass_kernel_spmd

    nc = bacc.Bacc("TRN2", target_bir_lowering=False, num_devices=1)
    arrays, io = {}, {}
    for name, value in inputs.items():
        a = np.ascontiguousarray(value)
        if name in HOST_SHAPE:
            a = a.reshape(HOST_SHAPE[name])
        if name in HOST_LAYOUT:
            a = np.ascontiguousarray(np.transpose(a, HOST_LAYOUT[name]))
        arrays[f"in_{name}"] = a
        io[name] = nc.dram_tensor(f"in_{name}", a.shape, mybir.dt.from_np(a.dtype), kind="ExternalInput").ap()
    out = nc.dram_tensor("out_x", (B, S, D), F32, kind="ExternalOutput").ap()
    bass_flamingo_gated_stack(nc, io, out)
    result = run_bass_kernel_spmd(nc, [arrays], core_ids=[0])
    return result.results[0]["out_x"]
```
